# Optimizing a Trainium2 kernel written in Bass

```python
import numpy as np
import jax
import jax.numpy as jnp

def _softmax(x, axis=-1):
    return jax.nn.softmax(x, axis=axis)

def _gelu(x):
    return jax.nn.gelu(x, approximate=True)

def _silu(x):
    return jax.nn.silu(x)

def _sigmoid(x):
    return jax.nn.sigmoid(x)

def _layernorm(x, axis=-1, eps=1e-05):
    m = jnp.mean(x, axis=axis, keepdims=True)
    v = jnp.var(x, axis=axis, keepdims=True)
    return (x - m) / jnp.sqrt(v + eps)

def _scatter_add(tgt, idx, src, axis=0):
    return tgt.at[idx].add(src)

def _segment_sum(src, seg, n):
    return jax.ops.segment_sum(src, seg, n)
kernel_name = 'mk_seq_preln_d2_jaxref_r8_cc8c81'

def setup_inputs(seed: int=0):
    np.random.seed(seed)
    _w = jnp.asarray

    def _L0_attn_setup():
        import jax, jax.numpy as jnp
        import numpy as np
        DIM = 128
        HEADS = 16
        HD = DIM // HEADS
        HID = 4 * DIM
        TPF = 1374
        LR = 0.1
        NS_ITERS = 5
        TTT_STEPS = 2
        B, S = (2, 4)
        SN = S * TPF

        def _newton_schulz(G, iters=NS_ITERS):
            a, b, c = (3.4445, -4.775, 2.0315)
            X = G / (jnp.linalg.norm(G) + 1e-07)
            transposed = G.shape[0] > G.shape[1]
            if transposed:
                X = X.T
            for _ in range(iters):
                A = X @ X.T
                X = a * X + (b * A + c * (A @ A)) @ X
            return X.T if transposed else X

        def _muon_update(p, g):
            return p - LR * _newton_schulz(g)
        key = jax.random.key(seed)
        ks = jax.random.split(key, 8)
        inp = {'x': jax.random.normal(ks[0], (B, SN, DIM), jnp.float32), 'qkv_w': jax.random.normal(ks[1], (DIM, 3 * DIM), jnp.float32) * DIM ** (-0.5), 'qkv_b': jnp.zeros((3 * DIM,), jnp.float32), 'qn_scale': jnp.ones((HD,), jnp.float32), 'qn_bias': jnp.zeros((HD,), jnp.float32), 'kn_scale': jnp.ones((HD,), jnp.float32), 'kn_bias': jnp.zeros((HD,), jnp.float32), 'ttt_gate': jax.random.normal(ks[2], (DIM, HID), jnp.float32) * DIM ** (-0.5), 'ttt_val': jax.random.normal(ks[3], (DIM, HID), jnp.float32) * DIM ** (-0.5), 'ttt_proj': jax.random.normal(ks[4], (HID, DIM), jnp.float32) * HID ** (-0.5), 'proj_w': jax.random.normal(ks[5], (DIM, DIM), jnp.float32) * DIM ** (-0.5), 'proj_b': jnp.zeros((DIM,), jnp.float32)}
        return inp
    _L0_attn_in = _L0_attn_setup()

    def _L0_ffn_setup():
        import jax, jax.numpy as jnp
        import numpy as np
        E, D, F = (8, 128, 512)
        LN_EPS = 1e-05
        key = jax.random.key(seed)
        k = jax.random.split(key, 8)
        x = jax.random.normal(k[0], (4, 256, D), jnp.float32)
        centroids = jax.random.normal(k[1], (E, D), jnp.float32) * 0.1
        ln_g = jnp.ones((E, D), jnp.float32)
        ln_b = jnp.zeros((E, D), jnp.float32)
        w1 = jax.random.normal(k[2], (E, F, D), jnp.float32) * (1.0 / np.sqrt(D))
        b1 = jnp.zeros((E, F), jnp.float32)
        w2 = jax.random.normal(k[3], (E, D, F), jnp.float32) * (1.0 / np.sqrt(F))
        b2 = jnp.zeros((E, D), jnp.float32)
        return {'input_features': x, 'centroids': centroids, 'ln_g': ln_g, 'ln_b': ln_b, 'w1': w1, 'b1': b1, 'w2': w2, 'b2': b2}
    _L0_ffn_in = _L0_ffn_setup()

    def _L1_attn_setup():
        import jax, jax.numpy as jnp
        import numpy as np
        HEADS = 16
        key = jax.random.key(seed)
        k1, k2, k3, k4 = jax.random.split(key, 4)
        C, T, E = (8, 512, 128)
        D = E // HEADS
        x = jax.random.normal(k1, (C, T, E), dtype=jnp.float32)
        Wq = jax.random.normal(k2, (D, D), dtype=jnp.float32) * (1.0 / np.sqrt(D))
        Wk = jax.random.normal(k3, (D, D), dtype=jnp.float32) * (1.0 / np.sqrt(D))
        Wv = jax.random.normal(k4, (D, D), dtype=jnp.float32) * (1.0 / np.sqrt(D))
        return {'x': x, 'Wq': Wq, 'Wk': Wk, 'Wv': Wv}
    _L1_attn_in = _L1_attn_setup()

    def _L1_ffn_setup():
        import jax, jax.numpy as jnp
        import numpy as np
        B, N, D = (4, 512, 128)
        E, K, H, ITERS = (8, 2, 64, 2)
        DT = 0.1
        C = 2 * D

        def _gelu(x):
            return jax.nn.gelu(x, approximate=False)

        def _inl(ctrl, xs, vs, mu):
            a, b, g = jnp.split(ctrl, 3, axis=-1)
            v_next = jax.nn.sigmoid(a) * vs - jax.nn.softplus(b) * (xs - mu)
            x_next = xs + DT * jax.nn.sigmoid(g) * v_next
            return (x_next, v_next)

        def _experts(ctx, idx, w1, b1, w2, b2):
            out = jnp.zeros((ctx.shape[0], w2.shape[2]), ctx.dtype)
            for e in range(E):
                h = _gelu(ctx @ w1[e] + b1[e])
                o = h @ w2[e] + b2[e]
                out = out + jnp.where((idx == e)[:, None], o, jnp.float32(0))
            return out

        def _forward(x, integration_weight, mu, router_w1, router_b1, router_w2, router_b2, halt_w1, halt_b1, halt_w2, halt_b2, expert_w1, expert_b1, expert_w2, expert_b2, shared_w1, shared_b1, shared_w2, shared_b2, shared_weight, refine_w1, refine_b1, refine_w2, refine_b2):
            b, n, d = x.shape
            xf = x.reshape(b * n, d)
            logits = _gelu(xf @ router_w1 + router_b1) @ router_w2 + router_b2
            probs = jax.nn.softmax(logits, axis=-1)
            topk_p, topk_i = jax.lax.top_k(probs, K)
            topk_p = topk_p / jnp.sum(topk_p, axis=-1, keepdims=True)
            flat_idx = topk_i.reshape(-1)
            flat_w = topk_p.reshape(-1, 1)
            v = jnp.zeros_like(xf)
            integrated = xf
            for _ in range(ITERS):
                ctx = jnp.concatenate([integrated, v], axis=-1)
                shared_ctrl = _gelu(ctx @ shared_w1 + shared_b1) @ shared_w2 + shared_b2
                x_sh, v_sh = _inl(shared_ctrl, integrated, v, mu)
                sw = jax.nn.sigmoid(shared_weight)
                ctx_e = jnp.repeat(ctx, K, axis=0)
                x_e = jnp.repeat(integrated, K, axis=0)
                v_e = jnp.repeat(v, K, axis=0)
                ctrl = _experts(ctx_e, flat_idx, expert_w1, expert_b1, expert_w2, expert_b2)
                x_r, v_r = _inl(ctrl, x_e, v_e, mu)
                x_r = (x_r * flat_w).reshape(-1, K, d).sum(axis=1)
                v_r = (v_r * flat_w).reshape(-1, K, d).sum(axis=1)
                x_next = sw * x_sh + (1.0 - sw) * x_r
                v_next = sw * v_sh + (1.0 - sw) * v_r
                halt = jax.nn.sigmoid(_gelu(integrated @ halt_w1 + halt_b1) @ halt_w2 + halt_b2)
                integrated = integrated + halt * (x_next - integrated)
                v = v + halt * (v_next - v)
            refined = _gelu(integrated @ refine_w1 + refine_b1) @ refine_w2 + refine_b2
            out = xf + integration_weight * refined
            return out.reshape(b, n, d)
        key = jax.random.key(seed)
        ks = jax.random.split(key, 12)
        rn = lambda k, s, sc=0.02: jax.random.normal(k, s, dtype=jnp.float32) * sc
        z = lambda s: jnp.zeros(s, jnp.float32)
        return {'x': jax.random.normal(ks[0], (B, N, D), dtype=jnp.float32), 'integration_weight': jnp.full((D,), 0.5, jnp.float32), 'mu': z((D,)), 'router_w1': rn(ks[1], (D, D // 4)), 'router_b1': z((D // 4,)), 'router_w2': rn(ks[2], (D // 4, E)), 'router_b2': z((E,)), 'halt_w1': rn(ks[3], (D, D // 4)), 'halt_b1': z((D // 4,)), 'halt_w2': rn(ks[4], (D // 4, 1)), 'halt_b2': z((1,)), 'expert_w1': rn(ks[5], (E, C, H)), 'expert_b1': z((E, H)), 'expert_w2': rn(ks[6], (E, H, 3 * D)), 'expert_b2': z((E, 3 * D)), 'shared_w1': rn(ks[7], (C, H)), 'shared_b1': z((H,)), 'shared_w2': rn(ks[8], (H, 3 * D)), 'shared_b2': z((3 * D,)), 'shared_weight': jnp.float32(0.5), 'refine_w1': rn(ks[9], (D, 2 * D)), 'refine_b1': z((2 * D,)), 'refine_w2': rn(ks[10], (2 * D, D)), 'refine_b2': z((D,))}
    _L1_ffn_in = _L1_ffn_setup()
    _d = {'L0_attn_x': _L0_attn_in['x'], 'L0_attn_qkv_w': _L0_attn_in['qkv_w'], 'L0_attn_qkv_b': _L0_attn_in['qkv_b'], 'L0_attn_qn_scale': _L0_attn_in['qn_scale'], 'L0_attn_qn_bias': _L0_attn_in['qn_bias'], 'L0_attn_kn_scale': _L0_attn_in['kn_scale'], 'L0_attn_kn_bias': _L0_attn_in['kn_bias'], 'L0_attn_ttt_gate': _L0_attn_in['ttt_gate'], 'L0_attn_ttt_val': _L0_attn_in['ttt_val'], 'L0_attn_ttt_proj': _L0_attn_in['ttt_proj'], 'L0_attn_proj_w': _L0_attn_in['proj_w'], 'L0_attn_proj_b': _L0_attn_in['proj_b'], 'L0_ffn_centroids': _L0_ffn_in['centroids'], 'L0_ffn_ln_g': _L0_ffn_in['ln_g'], 'L0_ffn_ln_b': _L0_ffn_in['ln_b'], 'L0_ffn_w1': _L0_ffn_in['w1'], 'L0_ffn_b1': _L0_ffn_in['b1'], 'L0_ffn_w2': _L0_ffn_in['w2'], 'L0_ffn_b2': _L0_ffn_in['b2'], 'L1_attn_Wq': _L1_attn_in['Wq'], 'L1_attn_Wk': _L1_attn_in['Wk'], 'L1_attn_Wv': _L1_attn_in['Wv'], 'L1_ffn_integration_weight': _L1_ffn_in['integration_weight'], 'L1_ffn_mu': _L1_ffn_in['mu'], 'L1_ffn_router_w1': _L1_ffn_in['router_w1'], 'L1_ffn_router_b1': _L1_ffn_in['router_b1'], 'L1_ffn_router_w2': _L1_ffn_in['router_w2'], 'L1_ffn_router_b2': _L1_ffn_in['router_b2'], 'L1_ffn_halt_w1': _L1_ffn_in['halt_w1'], 'L1_ffn_halt_b1': _L1_ffn_in['halt_b1'], 'L1_ffn_halt_w2': _L1_ffn_in['halt_w2'], 'L1_ffn_halt_b2': _L1_ffn_in['halt_b2'], 'L1_ffn_expert_w1': _L1_ffn_in['expert_w1'], 'L1_ffn_expert_b1': _L1_ffn_in['expert_b1'], 'L1_ffn_expert_w2': _L1_ffn_in['expert_w2'], 'L1_ffn_expert_b2': _L1_ffn_in['expert_b2'], 'L1_ffn_shared_w1': _L1_ffn_in['shared_w1'], 'L1_ffn_shared_b1': _L1_ffn_in['shared_b1'], 'L1_ffn_shared_w2': _L1_ffn_in['shared_w2'], 'L1_ffn_shared_b2': _L1_ffn_in['shared_b2'], 'L1_ffn_shared_weight': _L1_ffn_in['shared_weight'], 'L1_ffn_refine_w1': _L1_ffn_in['refine_w1'], 'L1_ffn_refine_b1': _L1_ffn_in['refine_b1'], 'L1_ffn_refine_w2': _L1_ffn_in['refine_w2'], 'L1_ffn_refine_b2': _L1_ffn_in['refine_b2']}
    _x0 = _d['L0_attn_x']
    _d['L0_attn_x'] = jax.random.normal(jax.random.fold_in(jax.random.key(seed), 1), (8, 512, 128), dtype=_x0.dtype)
    del _x0
    return _d

def reference(L0_attn_x, L0_attn_qkv_w, L0_attn_qkv_b, L0_attn_qn_scale, L0_attn_qn_bias, L0_attn_kn_scale, L0_attn_kn_bias, L0_attn_ttt_gate, L0_attn_ttt_val, L0_attn_ttt_proj, L0_attn_proj_w, L0_attn_proj_b, L0_ffn_centroids, L0_ffn_ln_g, L0_ffn_ln_b, L0_ffn_w1, L0_ffn_b1, L0_ffn_w2, L0_ffn_b2, L1_attn_Wq, L1_attn_Wk, L1_attn_Wv, L1_ffn_integration_weight, L1_ffn_mu, L1_ffn_router_w1, L1_ffn_router_b1, L1_ffn_router_w2, L1_ffn_router_b2, L1_ffn_halt_w1, L1_ffn_halt_b1, L1_ffn_halt_w2, L1_ffn_halt_b2, L1_ffn_expert_w1, L1_ffn_expert_b1, L1_ffn_expert_w2, L1_ffn_expert_b2, L1_ffn_shared_w1, L1_ffn_shared_b1, L1_ffn_shared_w2, L1_ffn_shared_b2, L1_ffn_shared_weight, L1_ffn_refine_w1, L1_ffn_refine_b1, L1_ffn_refine_w2, L1_ffn_refine_b2):

    def _L0_attn_ref(x, qkv_w, qkv_b, qn_scale, qn_bias, kn_scale, kn_bias, ttt_gate, ttt_val, ttt_proj, proj_w, proj_b):
        import jax, jax.numpy as jnp
        import numpy as np
        DIM = 128
        HEADS = 16
        HD = DIM // HEADS
        HID = 4 * DIM
        TPF = 1374
        LR = 0.1
        NS_ITERS = 5
        TTT_STEPS = 2
        B, S = (2, 4)
        SN = S * TPF

        def _newton_schulz(G, iters=NS_ITERS):
            a, b, c = (3.4445, -4.775, 2.0315)
            X = G / (jnp.linalg.norm(G) + 1e-07)
            transposed = G.shape[0] > G.shape[1]
            if transposed:
                X = X.T
            for _ in range(iters):
                A = X @ X.T
                X = a * X + (b * A + c * (A @ A)) @ X
            return X.T if transposed else X

        def _muon_update(p, g):
            return p - LR * _newton_schulz(g)
        Bx, SNx, _ = x.shape
        qkv = x @ qkv_w + qkv_b
        q, k, v = jnp.split(qkv, 3, axis=-1)
        q = q.reshape(Bx, SNx, HEADS, HD)
        k = k.reshape(Bx, SNx, HEADS, HD)
        q = q / (jnp.linalg.norm(q, axis=-1, keepdims=True) + 1e-06) * qn_scale + qn_bias
        k = k / (jnp.linalg.norm(k, axis=-1, keepdims=True) + 1e-06) * kn_scale + kn_bias
        q_ttt = q.reshape(-1, DIM)
        k_ttt = k.reshape(-1, DIM)
        v_ttt = v.reshape(-1, DIM)
        theta = {'gate': ttt_gate, 'val': ttt_val, 'proj': ttt_proj}

        def loss_fn(p):
            h = jax.nn.swish(k_ttt @ p['gate']) * (k_ttt @ p['val'])
            pred = h @ p['proj']
            return jnp.mean((pred - v_ttt) ** 2)
        for _ in range(TTT_STEPS):
            grads = jax.grad(loss_fn)(theta)
            theta = {kk: _muon_update(theta[kk], grads[kk]) for kk in theta}
        h_q = jax.nn.swish(q_ttt @ theta['gate']) * (q_ttt @ theta['val'])
        o = h_q @ theta['proj'] @ proj_w + proj_b
        return o.reshape(Bx, SNx, DIM)

    def _L0_ffn_ref(input_features, centroids, ln_g, ln_b, w1, b1, w2, b2):
        import jax, jax.numpy as jnp
        import numpy as np
        E, D, F = (8, 128, 512)
        LN_EPS = 1e-05
        x = input_features.reshape(-1, D)
        aff = jax.lax.stop_gradient(x) @ centroids.T
        assign = jnp.argmax(aff, axis=1)
        onehot = jax.nn.one_hot(assign, E, dtype=x.dtype)
        mu = jnp.mean(x, axis=-1, keepdims=True)
        var = jnp.mean((x - mu) ** 2, axis=-1, keepdims=True)
        xhat = (x - mu) * jax.lax.rsqrt(var + LN_EPS)
        xn = xhat[None, :, :] * ln_g[:, None, :] + ln_b[:, None, :]
        h = jax.nn.relu(jnp.einsum('etd,efd->etf', xn, w1) + b1[:, None, :])
        y = x[None, :, :] + jnp.einsum('etf,edf->etd', h, w2) + b2[:, None, :]
        alpha = jax.nn.sigmoid(x @ centroids.T)
        a = alpha.T[:, :, None]
        gated = a * y + (1.0 - a) * x[None, :, :]
        out = jnp.einsum('te,etd->td', onehot, gated)
        return out.reshape(input_features.shape)

    def _L1_attn_ref(x, Wq, Wk, Wv):
        import jax, jax.numpy as jnp
        import numpy as np
        HEADS = 16
        C, T, E = x.shape
        H = HEADS
        D = E // H
        xr = x.reshape(C, T, H, D)
        q = jnp.einsum('cthd,ed->cthe', xr, Wq)
        k = jnp.einsum('cthd,ed->cthe', xr, Wk)
        v = jnp.einsum('cthd,ed->cthe', xr, Wv)
        diag_scores = jnp.einsum('cthd,cthd->cth', q, k) / jnp.sqrt(jnp.asarray(E, x.dtype))
        probs = jax.nn.softmax(diag_scores, axis=0)
        vsum = v.sum(axis=1)
        attn = probs[..., None] * vsum[:, None, :, :]
        return attn.reshape(C, T, E)

    def _L1_ffn_ref(x, integration_weight, mu, router_w1, router_b1, router_w2, router_b2, halt_w1, halt_b1, halt_w2, halt_b2, expert_w1, expert_b1, expert_w2, expert_b2, shared_w1, shared_b1, shared_w2, shared_b2, shared_weight, refine_w1, refine_b1, refine_w2, refine_b2):
        import jax, jax.numpy as jnp
        import numpy as np
        B, N, D = (4, 512, 128)
        E, K, H, ITERS = (8, 2, 64, 2)
        DT = 0.1
        C = 2 * D

        def _gelu(x):
            return jax.nn.gelu(x, approximate=False)

        def _inl(ctrl, xs, vs, mu):
            a, b, g = jnp.split(ctrl, 3, axis=-1)
            v_next = jax.nn.sigmoid(a) * vs - jax.nn.softplus(b) * (xs - mu)
            x_next = xs + DT * jax.nn.sigmoid(g) * v_next
            return (x_next, v_next)

        def _experts(ctx, idx, w1, b1, w2, b2):
            out = jnp.zeros((ctx.shape[0], w2.shape[2]), ctx.dtype)
            for e in range(E):
                h = _gelu(ctx @ w1[e] + b1[e])
                o = h @ w2[e] + b2[e]
                out = out + jnp.where((idx == e)[:, None], o, jnp.float32(0))
            return out

        def _forward(x, integration_weight, mu, router_w1, router_b1, router_w2, router_b2, halt_w1, halt_b1, halt_w2, halt_b2, expert_w1, expert_b1, expert_w2, expert_b2, shared_w1, shared_b1, shared_w2, shared_b2, shared_weight, refine_w1, refine_b1, refine_w2, refine_b2):
            b, n, d = x.shape
            xf = x.reshape(b * n, d)
            logits = _gelu(xf @ router_w1 + router_b1) @ router_w2 + router_b2
            probs = jax.nn.softmax(logits, axis=-1)
            topk_p, topk_i = jax.lax.top_k(probs, K)
            topk_p = topk_p / jnp.sum(topk_p, axis=-1, keepdims=True)
            flat_idx = topk_i.reshape(-1)
            flat_w = topk_p.reshape(-1, 1)
            v = jnp.zeros_like(xf)
            integrated = xf
            for _ in range(ITERS):
                ctx = jnp.concatenate([integrated, v], axis=-1)
                shared_ctrl = _gelu(ctx @ shared_w1 + shared_b1) @ shared_w2 + shared_b2
                x_sh, v_sh = _inl(shared_ctrl, integrated, v, mu)
                sw = jax.nn.sigmoid(shared_weight)
                ctx_e = jnp.repeat(ctx, K, axis=0)
                x_e = jnp.repeat(integrated, K, axis=0)
                v_e = jnp.repeat(v, K, axis=0)
                ctrl = _experts(ctx_e, flat_idx, expert_w1, expert_b1, expert_w2, expert_b2)
                x_r, v_r = _inl(ctrl, x_e, v_e, mu)
                x_r = (x_r * flat_w).reshape(-1, K, d).sum(axis=1)
                v_r = (v_r * flat_w).reshape(-1, K, d).sum(axis=1)
                x_next = sw * x_sh + (1.0 - sw) * x_r
                v_next = sw * v_sh + (1.0 - sw) * v_r
                halt = jax.nn.sigmoid(_gelu(integrated @ halt_w1 + halt_b1) @ halt_w2 + halt_b2)
                integrated = integrated + halt * (x_next - integrated)
                v = v + halt * (v_next - v)
            refined = _gelu(integrated @ refine_w1 + refine_b1) @ refine_w2 + refine_b2
            out = xf + integration_weight * refined
            return out.reshape(b, n, d)
        return _forward(x, integration_weight, mu, router_w1, router_b1, router_w2, router_b2, halt_w1, halt_b1, halt_w2, halt_b2, expert_w1, expert_b1, expert_w2, expert_b2, shared_w1, shared_b1, shared_w2, shared_b2, shared_weight, refine_w1, refine_b1, refine_w2, refine_b2)
    x = L0_attn_x
    x = x + _L0_attn_ref(_layernorm(x, axis=-1), L0_attn_qkv_w, L0_attn_qkv_b, L0_attn_qn_scale, L0_attn_qn_bias, L0_attn_kn_scale, L0_attn_kn_bias, L0_attn_ttt_gate, L0_attn_ttt_val, L0_attn_ttt_proj, L0_attn_proj_w, L0_attn_proj_b)
    x = x + _L0_ffn_ref(_layernorm(x, axis=-1), L0_ffn_centroids, L0_ffn_ln_g, L0_ffn_ln_b, L0_ffn_w1, L0_ffn_b1, L0_ffn_w2, L0_ffn_b2)
    x = x + _L1_attn_ref(_layernorm(x, axis=-1), L1_attn_Wq, L1_attn_Wk, L1_attn_Wv)
    x = x + _L1_ffn_ref(_layernorm(x, axis=-1), L1_ffn_integration_weight, L1_ffn_mu, L1_ffn_router_w1, L1_ffn_router_b1, L1_ffn_router_w2, L1_ffn_router_b2, L1_ffn_halt_w1, L1_ffn_halt_b1, L1_ffn_halt_w2, L1_ffn_halt_b2, L1_ffn_expert_w1, L1_ffn_expert_b1, L1_ffn_expert_w2, L1_ffn_expert_b2, L1_ffn_shared_w1, L1_ffn_shared_b1, L1_ffn_shared_w2, L1_ffn_shared_b2, L1_ffn_shared_weight, L1_ffn_refine_w1, L1_ffn_refine_b1, L1_ffn_refine_w2, L1_ffn_refine_b2)
    return x

_drawn_inputs = setup_inputs


def setup_inputs(seed=0):
    import zlib

    import numpy as np

    out = dict(_drawn_inputs(seed))
    spreads = {'L0_attn_qkv_b': (0.0, 0.1),
     'L0_attn_qn_scale': (1.0, 0.6),
     'L0_attn_qn_bias': (0.0, 0.1),
     'L0_attn_kn_scale': (1.0, 0.6),
     'L0_attn_kn_bias': (0.0, 0.315),
     'L0_attn_proj_b': (0.0, 0.1),
     'L0_ffn_ln_g': (1.0, 0.2),
     'L0_ffn_ln_b': (0.0, 0.1),
     'L0_ffn_b1': (0.0, 0.1),
     'L0_ffn_b2': (0.0, 0.1),
     'L1_ffn_integration_weight': (0.5, 0.6),
     'L1_ffn_mu': (0.0, 2.0),
     'L1_ffn_router_b1': (0.0, 2.0),
     'L1_ffn_router_b2': (0.0, 2.0),
     'L1_ffn_halt_b1': (0.0, 2.0),
     'L1_ffn_expert_b1': (0.0, 2.0),
     'L1_ffn_expert_b2': (0.0, 2.0),
     'L1_ffn_shared_b1': (0.0, 2.0),
     'L1_ffn_shared_b2': (0.0, 2.0),
     'L1_ffn_refine_b1': (0.0, 0.8),
     'L1_ffn_refine_b2': (0.0, 0.8)}
    factors = {'L1_ffn_router_w1': 64.0,
     'L1_ffn_router_w2': 64.0,
     'L1_ffn_halt_w1': 64.0,
     'L1_ffn_halt_w2': 64.0,
     'L1_ffn_expert_w1': 64.0,
     'L1_ffn_expert_w2': 64.0,
     'L1_ffn_shared_w1': 52.769,
     'L1_ffn_shared_w2': 54.044,
     'L1_ffn_refine_w1': 8.0,
     'L1_ffn_refine_w2': 8.0}
    for name, (base, spread) in spreads.items():
        noise = np.random.default_rng([zlib.crc32(name.encode()), seed]).standard_normal(out[name].shape)
        drawn = base * np.exp(spread * noise) if base else spread * noise
        out[name] = jnp.asarray(drawn.astype(out[name].dtype))
    for name, factor in factors.items():
        out[name] = (out[name] * factor).astype(out[name].dtype)
    return out
```

```python
from contextlib import ExitStack

import concourse.bass as bass
import numpy as np
from concourse import mybir

FP32 = mybir.dt.float32
BF16 = mybir.dt.bfloat16
I32 = mybir.dt.int32
U32 = mybir.dt.uint32
ALU = mybir.AluOpType
ACT = mybir.ActivationFunctionType
AXX = mybir.AxisListType.X

P = 128
SEQS, SEQ = 8, 512
TOKENS = SEQS * SEQ
TILES = TOKENS // P
CT = SEQ // P
CHUNKS = TOKENS // SEQ
HEADS, HD = 16, 8
LN_EPS = 1e-5
HID = 512
HT = HID // P
E = 8
PADDED = TILES + E - 1
NS_A, NS_B, NS_C = 3.4445, -4.775, 2.0315
NS_ITERS, LR = 5, 0.1
GRAD_SCALE = 2.0 / (TOKENS * P)
EH = 64
PAIRS = E // 2
CTRL = 3 * P
RH = 32
DT = 0.1
ONE = EH + RH


def constant_columns():
    row = np.arange(P)[:, None]
    col = np.arange(P)[None, :]
    sel = np.zeros((P, 2 * PAIRS, P))
    for k in range(2):
        for q in range(PAIRS):
            sel[k * E + 2 * q, k * PAIRS + q, :EH] = 1
            sel[k * E + 2 * q + 1, k * PAIRS + q, EH:] = 1
    starts = np.ones((P, E, TILES))
    starts[:, :, 0] = 0
    parts = {
        "ident": row == col,
        "before": row < col,
        "ones": np.ones((P, P)),
        "headmask": row // HD == col // HD,
        "headtile": (row == col % HD),
        "sel": sel.reshape(P, -1),
        "starts": starts.reshape(P, -1),
        "rank8": np.tile(E - np.arange(E), (P, 1)),
        "tilestart": np.tile(P * np.arange(TILES), (P, 1)),
        "slot": np.tile(np.arange(PADDED), (P, 1)),
    }
    at, cols, out = 0, {}, []
    for name, a in parts.items():
        a = np.asarray(a, np.float32)
        cols[name] = (at, at + a.shape[1])
        at += a.shape[1]
        out.append(a)
    return np.ascontiguousarray(np.concatenate(out, 1)), cols


class Chain:

    def __init__(self, eng, sem, base=0):
        self.eng, self.sem, self.base, self.n = eng, sem, base, 0

    def mark(self, ins):
        ins.then_inc(self.sem, 1)
        self.n += 1
        return self.base + self.n

    def link(self, ins):
        self.eng.wait_ge(self.sem, self.mark(ins))


def wait(eng, sem, n):
    if not (isinstance(n, int) and n <= 0):
        eng.wait_ge(sem, n)


def rounds(eng, n):
    def run(body):
        body(0)
        with eng.Fori(1, n) as i:
            body(i)
    return run


class Core:

    def __init__(self, nc, ctx, dram):
        self.nc, self.dram, self.sems = nc, dram, []
        self.bank = [ctx.enter_context(nc.psum_tensor(f"bank{i}", [P, 512], FP32)) for i in range(8)]

    def sb(self, ctx, name, shape, dt=FP32):
        return ctx.enter_context(self.nc.sbuf_tensor(name, shape, dt))

    def sem(self, name):
        self.sems.append(self.nc.alloc_semaphore(name=name))
        return self.sems[-1]

    def clear_semaphores(self):
        self.nc.clear_and_free_semaphores(self.sems)
        self.nc.all_engine_barrier()
        self.sems = []


def mul(nc, out, a, b):
    return nc.vector.tensor_tensor(out, a, b, ALU.mult)


def row(ap):
    return ap.rearrange("(a n) -> a n", a=1)


def spread(ap, n=P):
    return row(ap).to_broadcast([n, ap.shape[0]])


def load_phase(k, clear):
    nc, d = k.nc, k.dram
    loaded, ready, cleared = k.sem("x_loaded"), k.sem("zeros_ready"), k.sem("sorted_cleared")
    R = 13
    assert PADDED % R == 0
    with ExitStack() as ctx, nc.Block() as block:
        blank = k.sb(ctx, "blank", [P, R * P])

        @block.sync
        def _(sp):
            sp.dma_start(k.const[:, :], d["const"]).then_inc(loaded, 16)
            for c in range(CHUNKS):
                sp.dma_start(k.x[:, c * CT:(c + 1) * CT, :], d["L0_attn_x"][c, :, :].rearrange("(t p) c -> p t c", p=P)
                             ).then_inc(loaded, 16)
            sp.wait_ge(ready, 2)
            for t in range(0, PADDED, R):
                sp.dma_start(clear[t * P:(t + R) * P, :].rearrange("(p a) c -> p (a c)", p=P), blank[:, :]
                             ).then_inc(cleared, 16)
            sp.wait_ge(loaded, 16 * (CHUNKS + 1))
            sp.wait_ge(cleared, 16 * (PADDED // R))

        @block.vector
        def _(dve):
            dve.memset(blank[:, :], 0.0).then_inc(ready, 1)
            dve.memset(k.zeros[:, :], 0.0).then_inc(ready, 1)
            dve.wait_ge(ready, 2)


def statistics_phase(k, name, src):
    nc = k.nc
    counted, order = k.sem(f"{name}_rows_counted"), k.sem(f"{name}_order")
    var_ready, std_ready = k.sem(f"{name}_var_ready"), k.sem(f"{name}_std_ready")
    with ExitStack() as ctx:
        st = k.sb(ctx, f"{name}_st", [P, TILES, 6])
        tmp = k.sb(ctx, f"{name}_tmp", [P, 4, TILES])
        diff, var, std, fix = (tmp[:, n, :] for n in range(4))
        with nc.Block() as block:
            @block.vector
            def _(dve):
                @rounds(dve, CHUNKS)
                def _(i):
                    for j in range(CT):
                        nc.vector.bn_stats(st[:, bass.ds(i * CT + j, 1), :].rearrange("p a s -> p (a s)"),
                                           src[:, bass.ds(i * CT + j, 1), :].rearrange("p a c -> p (a c)")
                                           ).then_inc(counted, 1)
                wait(dve, counted, TILES)
                c = Chain(dve, order)
                c.mark(nc.vector.tensor_tensor(k.mean[:, :], st[:, :, 1], st[:, :, 4], ALU.add))
                c.mark(nc.vector.tensor_tensor(diff, st[:, :, 1], st[:, :, 4], ALU.subtract))
                c.link(nc.vector.tensor_tensor(var, st[:, :, 2], st[:, :, 5], ALU.add))
                c.mark(nc.vector.tensor_scalar(k.mean[:, :], k.mean[:, :], 0.5, None, ALU.mult))
                c.mark(mul(nc, diff, diff, diff))
                c.link(nc.vector.tensor_scalar(var, var, 1.0 / P, LN_EPS, ALU.mult, ALU.add))
                nc.vector.scalar_tensor_tensor(out=var, in0=diff, scalar=0.25, in1=var,
                                               op0=ALU.mult, op1=ALU.add).then_inc(var_ready, 1)
                wait(dve, std_ready, 1)
                c.link(nc.vector.reciprocal(k.rstd[:, :], std))
                c.link(mul(nc, fix, k.rstd[:, :], k.rstd[:, :]))
                c.link(mul(nc, fix, fix, var))
                c.link(nc.vector.tensor_scalar(fix, fix, -0.5, 1.5, ALU.mult, ALU.add))
                c.link(mul(nc, k.rstd[:, :], k.rstd[:, :], fix))

            @block.scalar
            def _(act):
                wait(act, var_ready, 1)
                nc.scalar.activation(std, var, ACT.Sqrt).then_inc(std_ready, 1)
                wait(act, std_ready, 1)


def tiles_of(t, i, n=CT):
    return t[:, bass.ds(i * n, n), :]


def per_token(t, i, width=P):
    return t[:, bass.ds(i * CT, CT)].unsqueeze(2).to_broadcast([P, CT, width])


def qkv_phase(k, s):
    nc, d = k.nc, k.dram
    W_LOADS = 8
    loaded, order_p = k.sem("qkv_w_loaded"), k.sem("qkv_pool_order")
    xn_ready, xn_transposed, xT_copied = k.sem("xn_ready"), k.sem("xn_transposed"), k.sem("xT_copied")
    qk_done, v_done, v_copied = k.sem("qk_done"), k.sem("v_done"), k.sem("v_copied")
    qk_copied, ss_ready, norm_ready = k.sem("qk_copied"), k.sem("ss_ready"), k.sem("norm_ready")
    unit_ready, qkn_ready, qkn_transposed = k.sem("unit_ready"), k.sem("qkn_ready"), k.sem("qkn_transposed")
    qT_copied, kT_copied, ktok_copied, order_v = (k.sem("qT_copied"), k.sem("kT_copied"), k.sem("ktok_copied"),
                                                  k.sem("qkv_dve_order"))
    G = CT * 2 * HEADS
    with ExitStack() as ctx:
        w = k.sb(ctx, "qkv_w_sb", [P, 3 * P])
        bqk = k.sb(ctx, "qk_bias", [P, 2 * P])
        bv = k.sb(ctx, "v_bias", [P, 1])
        hs = k.sb(ctx, "head_scale_bias", [P, 4, HD])
        xc = k.sb(ctx, "xc", [P, CT, P])
        xn = k.sb(ctx, "xn_chunk", [P, CT, P])
        xT = k.sb(ctx, "xT_chunk", [P, SEQ])
        qk = k.sb(ctx, "qk_chunk", [P, CT, 2 * P])
        sq = k.sb(ctx, "qk_squares", [P, CT * 2 * P])
        ss = k.sb(ctx, "qk_ss", [P, G])
        nrm = k.sb(ctx, "qk_norm", [P, G])
        inv = k.sb(ctx, "qk_inv", [P, G])
        qn = k.sb(ctx, "qk_unit", [P, CT, 2 * P])
        qkn = k.sb(ctx, "qkn_chunk", [P, CT, 2 * P])

        def heads(t):
            return t.rearrange("p (g e) -> p g e", e=HD)

        def q_or_k(t, which):
            return t[:, :, which * P:(which + 1) * P]

        with nc.Block() as block:
            @block.sync
            def _(sp):
                sp.dma_start(w[:, :], d["L0_attn_qkv_w"]).then_inc(loaded, 16)
                sp.dma_start(bqk[:, :], spread(d["L0_attn_qkv_b"][0:2 * P])).then_inc(loaded, 16)
                sp.dma_start(bv[:, :], d["L0_attn_qkv_b"][2 * P:3 * P].rearrange("(p a) -> p a", a=1)).then_inc(loaded, 16)
                for n, name in enumerate(("qn_scale", "kn_scale", "qn_bias", "kn_bias")):
                    sp.dma_start(hs[:, n, :], spread(d["L0_attn_" + name])).then_inc(loaded, 16)
                sp.dma_start(k.theta_gate[:, :], d["L0_attn_ttt_gate"]).then_inc(loaded, 16)
                sp.dma_start(k.theta_val[:, :], d["L0_attn_ttt_val"]).then_inc(s.theta_loaded, 16)
                sp.dma_start(k.theta_proj[:, :, :], d["L0_attn_ttt_proj"].rearrange("(j p) c -> p j c", p=P)
                             ).then_inc(s.theta_loaded, 16)
                wait(sp, s.theta_loaded, 32)

            @block.gpsimd
            def _(pool):
                wait(pool, loaded, 16 * W_LOADS)
                @rounds(pool, CHUNKS)
                def _(i):
                    c = Chain(pool, order_p, i * 1)
                    c.link(nc.gpsimd.tensor_tensor(xc[:, :, :], tiles_of(k.x, i), per_token(k.mean, i), ALU.subtract))
                    wait(pool, xn_transposed, i)
                    nc.gpsimd.tensor_tensor(xn[:, :, :], xc[:, :, :], per_token(k.rstd, i), ALU.mult
                                            ).then_inc(xn_ready, 1)
                    wait(pool, unit_ready, i + 1)
                    wait(pool, xn_ready, i + 1)
                    for n in range(2):
                        src = q_or_k(qn, n)
                        for t in range(CT):
                            nc.gpsimd.tensor_tensor(heads(qn[:, t, n * P:(n + 1) * P]), heads(qn[:, t, n * P:(n + 1) * P]),
                                                    hs[:, n:n + 1, :].to_broadcast([P, HEADS, HD]), ALU.mult
                                                    ).then_inc(s.scaled, 1)
                    wait(pool, s.scaled, (i + 1) * 2 * CT)
                    wait(pool, qkn_transposed, i)
                    wait(pool, ktok_copied, i)
                    for n in range(2):
                        for t in range(CT):
                            nc.gpsimd.tensor_tensor(heads(qkn[:, t, n * P:(n + 1) * P]), heads(qn[:, t, n * P:(n + 1) * P]),
                                                    hs[:, n + 2:n + 3, :].to_broadcast([P, HEADS, HD]), ALU.add
                                                    ).then_inc(qkn_ready, 1)

            @block.tensor
            def _(pe):
                wait(pe, loaded, 16 * W_LOADS)
                @rounds(pe, CHUNKS)
                def _(i):
                    wait(pe, xn_ready, i + 1)
                    wait(pe, xT_copied, i)
                    for j in range(CT):
                        last = nc.tensor.transpose(k.bank[0][:, j * P:(j + 1) * P], xn[:, j, :], k.ident)
                    last.then_inc(xn_transposed, 1)
                    wait(pe, xT_copied, i + 1)
                    wait(pe, qk_copied, 2 * i)
                    for j in range(CT):
                        last = nc.tensor.matmul(k.bank[1 + j // 2][:, (j % 2) * 2 * P:(j % 2 + 1) * 2 * P],
                                                xT[:, j * P:(j + 1) * P], w[:, 0:2 * P], start=True, stop=True)
                        if j % 2:
                            last.then_inc(qk_done, 1)
                    wait(pe, v_copied, i)
                    nc.tensor.matmul(k.bank[3][:, :], w[:, 2 * P:3 * P], xT[:, :], start=True, stop=True).then_inc(v_done, 1)
                    wait(pe, qkn_ready, (i + 1) * 2 * CT)
                    for n, copied in ((0, qT_copied), (1, kT_copied)):
                        wait(pe, copied, i)
                        for j in range(CT):
                            last = nc.tensor.transpose(k.bank[4 + n][:, j * P:(j + 1) * P],
                                                       qkn[:, j, n * P:(n + 1) * P], k.ident)
                    last.then_inc(qkn_transposed, 1)

            @block.scalar
            def _(act):
                wait(act, loaded, 16 * W_LOADS)
                @rounds(act, CHUNKS)
                def _(i):
                    wait(act, xn_transposed, i + 1)
                    wait(act, v_done, i)
                    nc.scalar.copy(xT[:, :], k.bank[0][:, :]).then_inc(xT_copied, 1)
                    wait(act, v_done, i + 1)
                    nc.scalar.activation(k.vT[:, bass.ds(i * SEQ, SEQ)], k.bank[3][:, :], ACT.Identity,
                                         bias=bv[:, 0:1]).then_inc(v_copied, 1)
                    wait(act, ss_ready, i + 1)
                    nc.scalar.activation(nrm[:, :], ss[:, :], ACT.Sqrt).then_inc(norm_ready, 1)
                    wait(act, qkn_transposed, i + 1)
                    nc.scalar.copy(k.qT[:, bass.ds(i * SEQ, SEQ)], k.bank[4][:, :]).then_inc(qT_copied, 1)
                    nc.scalar.copy(k.kT[:, bass.ds(i * SEQ, SEQ)], k.bank[5][:, :]).then_inc(kT_copied, 1)
                    nc.scalar.copy(tiles_of(k.ktok, i), q_or_k(qkn, 1)).then_inc(ktok_copied, 1)
                wait(act, ktok_copied, CHUNKS)

            @block.vector
            def _(dve):
                wait(dve, loaded, 16 * W_LOADS)
                LINKS = 7
                @rounds(dve, CHUNKS)
                def _(i):
                    c = Chain(dve, order_v, i * LINKS)
                    for h in range(2):
                        wait(dve, qk_done, 2 * i + h + 1)
                        nc.vector.tensor_tensor(qk[:, 2 * h:2 * h + 2, :],
                                                k.bank[1 + h][:, :].rearrange("p (j c) -> p j c", j=2),
                                                bqk[:, :].unsqueeze(1).to_broadcast([P, 2, 2 * P]), ALU.add
                                                ).then_inc(qk_copied, 1)
                    wait(dve, qk_copied, 2 * i + 2)
                    flat = qk[:, :, :].rearrange("p t c -> p (t c)")
                    c.link(mul(nc, sq[:, :], flat, flat))
                    nc.vector.tensor_reduce(ss[:, :], heads(sq[:, :]), AXX, ALU.add).then_inc(ss_ready, 1)
                    wait(dve, norm_ready, i + 1)
                    c.link(nc.vector.tensor_scalar(inv[:, :], nrm[:, :], 1e-30, None, ALU.max))
                    c.link(nc.vector.reciprocal(inv[:, :], inv[:, :]))
                    c.link(mul(nc, inv[:, :], inv[:, :], ss[:, :]))
                    c.link(nc.vector.tensor_tensor(inv[:, :], inv[:, :], nrm[:, :], ALU.add))
                    c.link(nc.vector.tensor_scalar(inv[:, :], inv[:, :], 0.5, 1e-6, ALU.mult, ALU.add))
                    c.link(nc.vector.reciprocal(inv[:, :], inv[:, :]))
                    assert c.n == LINKS
                    wait(dve, qkn_ready, i * 2 * CT)
                    mul(nc, heads(qn[:, :, :].rearrange("p t c -> p (t c)")), heads(flat),
                        inv[:, :].unsqueeze(2).to_broadcast([P, G, HD])).then_inc(unit_ready, 1)


def transpose_proj_phase(k):
    nc = k.nc
    done, copied = k.sem("projT_transposed"), k.sem("projT_copied")
    with nc.Block() as block:
        @block.tensor
        def _(pe):
            for j in range(HT):
                last = nc.tensor.transpose(k.bank[0][:, j * P:(j + 1) * P], k.theta_proj[:, j, :], k.ident)
            last.then_inc(done, 1)

        @block.scalar
        def _(act):
            wait(act, done, 1)
            nc.scalar.copy(k.theta_projT[:, :], k.bank[0][:, :]).then_inc(copied, 1)
            wait(act, copied, 1)


def gradient_phase(k, name):
    nc = k.nc
    m = {n: k.sem(f"{name}_{n}") for n in (
        "kT_loaded0", "kT_loaded1", "k_loaded0", "k_loaded1", "G_done", "V_done", "sig_ready", "V_copied",
        "s_ready", "h_ready", "dact_ready", "hT_done", "hT_copied", "pred_done", "rT_ready", "r_done",
        "r_copied", "dh_done", "dproj_added", "dval_in_ready", "dgate_in_ready", "dgate_added", "order",
        "closed")}
    G_BANK, V_BANK, HT_BANK, R_BANK, DH_BANK, PROJ_BANK, VAL_BANK, GATE_BANK = k.bank
    PAIR_LOOPS = TILES // 2 - 1
    with ExitStack() as ctx:
        def two(n, shape):
            return [k.sb(ctx, f"{name}_{n}{a}", shape) for a in range(2)]
        kT, kt = two("kT", [P, P]), two("k", [P, P])
        sig, s, h, hv, dact = (two(n, [P, HID]) for n in ("sig", "s", "h", "hv", "dact"))
        hT = k.sb(ctx, f"{name}_hT", [P, HID])
        rT = k.sb(ctx, f"{name}_rT", [P, P])
        r = k.sb(ctx, f"{name}_r", [P, P])
        dval_in = k.sb(ctx, f"{name}_dval_in", [P, HID])
        dgate_in = k.sb(ctx, f"{name}_dgate_in", [P, HID])
        u = k.sb(ctx, f"{name}_u", [P, HID])

        with nc.Block() as block:
            @block.sync
            def _(sp):
                for a in range(2):
                    sp.dma_start(kT[a][:, :], k.kT[:, a * P:(a + 1) * P]).then_inc(m[f"kT_loaded{a}"], 16)
                sp.dma_start(kt[0][:, :], k.ktok[:, 0, :]).then_inc(m["k_loaded0"], 16)

            @block.tensor
            def _(pe):
                def open_or_close(start):
                    for b in (PROJ_BANK, VAL_BANK, GATE_BANK):
                        last = nc.tensor.matmul(b[:, :], k.zeros[:, 0:P], k.zeros[:, :], start=start, stop=not start)
                    return last

                def gate(t, i, a):
                    wait(pe, m[f"kT_loaded{a}"], (i + 1) * 16)
                    wait(pe, m["s_ready"], t)
                    nc.tensor.matmul(G_BANK[:, :], kT[a][:, :], k.theta_gate[:, :], start=True, stop=True
                                     ).then_inc(m["G_done"], 1)

                def val(t, a):
                    wait(pe, m["V_copied"], t)
                    nc.tensor.matmul(V_BANK[:, :], kT[a][:, :], k.theta_val[:, :], start=True, stop=True
                                     ).then_inc(m["V_done"], 1)

                def step(i, a, last_tile=False):
                    t = i * 2 + a
                    ni, na = (i, 1) if a == 0 else (i + 1, 0)
                    wait(pe, m["h_ready"], t + 1)
                    wait(pe, m["hT_copied"], t)
                    for j in range(HT):
                        x = nc.tensor.transpose(HT_BANK[:, j * P:(j + 1) * P], h[a][:, j * P:(j + 1) * P], k.ident)
                    x.then_inc(m["hT_done"], 1)
                    if not last_tile:
                        gate(t + 1, ni, na)
                    wait(pe, m["hT_copied"], t + 1)
                    wait(pe, m["r_copied"], t)
                    for j in range(HT):
                        x = nc.tensor.matmul(R_BANK[:, 0:P], k.theta_proj[:, j, :], hT[:, j * P:(j + 1) * P],
                                             start=j == 0, stop=j == HT - 1)
                    x.then_inc(m["pred_done"], 1)
                    if not last_tile:
                        val(t + 1, na)
                    wait(pe, m["rT_ready"], t + 1)
                    nc.tensor.transpose(R_BANK[:, P:2 * P], rT[:, :], k.ident).then_inc(m["r_done"], 1)
                    wait(pe, m["dgate_in_ready"], t)
                    nc.tensor.matmul(DH_BANK[:, :], rT[:, :], k.theta_projT[:, :], start=True, stop=True
                                     ).then_inc(m["dh_done"], 1)
                    wait(pe, m["r_copied"], t + 1)
                    nc.tensor.matmul(PROJ_BANK[:, :], r[:, :], h[a][:, :], start=False, stop=False
                                     ).then_inc(m["dproj_added"], 1)
                    wait(pe, m[f"k_loaded{a}"], (i + 1) * 16)
                    wait(pe, m["dval_in_ready"], t + 1)
                    nc.tensor.matmul(VAL_BANK[:, :], kt[a][:, :], dval_in[:, :], start=False, stop=False)
                    wait(pe, m["dgate_in_ready"], t + 1)
                    nc.tensor.matmul(GATE_BANK[:, :], kt[a][:, :], dgate_in[:, :], start=False, stop=False
                                     ).then_inc(m["dgate_added"], 1)

                open_or_close(True)
                gate(0, 0, 0)
                val(0, 0)
                @rounds(pe, PAIR_LOOPS)
                def _(i):
                    step(i, 0)
                    step(i, 1)
                step(PAIR_LOOPS, 0)
                step(PAIR_LOOPS, 1, last_tile=True)
                open_or_close(False).then_inc(m["closed"], 1)
                wait(pe, m["closed"], 1)

            @block.scalar
            def _(act):
                def forward(t, a):
                    wait(act, m["G_done"], t + 1)
                    if not (isinstance(t, int) and t < 2):
                        wait(act, m["dact_ready"], t - 1)
                    nc.scalar.activation(sig[a][:, :], G_BANK[:, :], ACT.Sigmoid).then_inc(m["sig_ready"], 1)
                    wait(act, m["V_done"], t + 1)
                    nc.scalar.copy(hv[a][:, :], V_BANK[:, :]).then_inc(m["V_copied"], 1)

                def step(i, a, last_tile=False):
                    t = i * 2 + a
                    wait(act, m["hT_done"], t + 1)
                    wait(act, m["pred_done"], t)
                    nc.scalar.copy(hT[:, :], HT_BANK[:, :]).then_inc(m["hT_copied"], 1)
                    if not (isinstance(i, int) and i == PAIR_LOOPS):
                        wait(act, m["V_done"], t + 1)
                        act.dma_start(kT[a][:, :], k.kT[:, bass.ds((t + 2) * P, P)]).then_inc(m[f"kT_loaded{a}"], 16)
                    if not last_tile:
                        wait(act, m["dgate_added"], t)
                        act.dma_start(kt[1 - a][:, :],
                                      k.ktok[:, :, :].rearrange("p t c -> p (t c)")[:, bass.ds((t + 1) * P, P)]
                                      ).then_inc(m[f"k_loaded{1 - a}"], 16)
                    if not last_tile:
                        forward(t + 1, 1 - a)
                    wait(act, m["r_done"], t + 1)
                    wait(act, m["dproj_added"], t)
                    nc.scalar.copy(r[:, :], R_BANK[:, P:2 * P]).then_inc(m["r_copied"], 1)

                forward(0, 0)
                step(0, 0)
                step(0, 1)
                with act.Fori(1, PAIR_LOOPS) as i:
                    step(i, 0)
                    step(i, 1)
                step(PAIR_LOOPS, 0)
                step(PAIR_LOOPS, 1, last_tile=True)

            @block.vector
            def _(dve):
                def activate(t, a):
                    wait(dve, m["sig_ready"], t + 1)
                    mul(nc, s[a][:, :], G_BANK[:, :], sig[a][:, :]).then_inc(m["s_ready"], 1)

                def hidden(t, a):
                    wait(dve, m["V_copied"], t + 1)
                    wait(dve, m["s_ready"], t + 1)
                    if not (isinstance(t, int) and t < 2):
                        wait(dve, m["dproj_added"], t - 1)
                    mul(nc, h[a][:, :], s[a][:, :], hv[a][:, :]).then_inc(m["h_ready"], 1)

                def derivative(t, a):
                    nc.vector.scalar_tensor_tensor(out=u[:, :], in0=sig[a][:, :], scalar=1.0, in1=s[a][:, :],
                                                   op0=ALU.subtract, op1=ALU.mult).then_inc(m["order"], 1)
                    wait(dve, m["order"], t * 2 + 1)
                    nc.vector.tensor_tensor(u[:, :], sig[a][:, :], u[:, :], ALU.subtract).then_inc(m["order"], 1)
                    wait(dve, m["order"], t * 2 + 2)
                    mul(nc, dact[a][:, :], u[:, :], hv[a][:, :]).then_inc(m["dact_ready"], 1)

                def step(i, a, last_tile=False):
                    t = i * 2 + a
                    if not last_tile:
                        activate(t + 1, 1 - a)
                    wait(dve, m["pred_done"], t + 1)
                    wait(dve, m["dh_done"], t)
                    nc.vector.tensor_tensor(rT[:, :], R_BANK[:, 0:P], k.vT[:, bass.ds(t * P, P)], ALU.subtract
                                            ).then_inc(m["rT_ready"], 1)
                    if not last_tile:
                        hidden(t + 1, 1 - a)
                    wait(dve, m["dh_done"], t + 1)
                    wait(dve, m["dgate_added"], t)
                    mul(nc, dval_in[:, :], DH_BANK[:, :], s[a][:, :]).then_inc(m["dval_in_ready"], 1)
                    wait(dve, m["dact_ready"], t + 1)
                    mul(nc, dgate_in[:, :], DH_BANK[:, :], dact[a][:, :]).then_inc(m["dgate_in_ready"], 1)
                    if not last_tile:
                        derivative(t + 1, 1 - a)

                activate(0, 0)
                hidden(0, 0)
                derivative(0, 0)
                step(0, 0)
                step(0, 1)
                with dve.Fori(1, PAIR_LOOPS) as i:
                    step(i, 0)
                    step(i, 1)
                step(PAIR_LOOPS, 0)
                step(PAIR_LOOPS, 1, last_tile=True)


def muon_phase(k, name):
    nc = k.nc
    grads = [k.bank[7], k.bank[6], k.bank[5]]
    xbank = [k.bank[0], k.bank[1], k.bank[2]]
    tbank = [k.bank[3], k.bank[4], k.bank[5]]
    M = 3
    m = {n: k.sem(f"{name}_{n}") for n in (
        "grad_copied", "squares_summed", "total_done", "norm_ready", "scaled", "xT_first", "xT_copied",
        "A_done", "A_copied", "AA_done", "poly_ready", "X_done", "X_copied", "XT_done", "order", "scaled_A",
        "updated")}
    with ExitStack() as ctx:
        X = [k.sb(ctx, f"{name}_X{n}", [P, HID]) for n in range(M)]
        XT = [k.sb(ctx, f"{name}_XT{n}", [P, HID]) for n in range(M)]
        A = [k.sb(ctx, f"{name}_A{n}", [P, P]) for n in range(M)]
        poly = [k.sb(ctx, f"{name}_poly{n}", [P, P]) for n in range(M)]
        aI = k.sb(ctx, f"{name}_aI", [P, P])
        squares = k.sb(ctx, f"{name}_squares", [P, HID])
        ssq = k.sb(ctx, f"{name}_ssq", [P, M])
        tot = k.sb(ctx, f"{name}_tot", [P, M])
        nrm = k.sb(ctx, f"{name}_nrm", [P, M])
        inv = k.sb(ctx, f"{name}_inv", [P, M])
        with nc.Block() as block:
            @block.tensor
            def _(pe):
                wait(pe, m["squares_summed"], M)
                nc.tensor.matmul(xbank[0][:, 0:M], k.c("ones"), ssq[:, :], start=True, stop=True
                                 ).then_inc(m["total_done"], 1)
                for n in range(M):
                    wait(pe, m["scaled"], n + 1)
                    for j in range(HT):
                        last = nc.tensor.transpose(tbank[n][:, j * P:(j + 1) * P], X[n][:, j * P:(j + 1) * P], k.ident)
                    last.then_inc(m["XT_done"], 1)
                @rounds(pe, NS_ITERS)
                def _(i):
                    for n in range(M):
                        wait(pe, m["xT_copied"], i * M + n + 1)
                        wait(pe, m["X_copied"], i * M)
                        for j in range(HT):
                            xt = XT[n][:, j * P:(j + 1) * P]
                            last = nc.tensor.matmul(xbank[n][:, 0:P], xt, xt, start=j == 0, stop=j == HT - 1)
                        last.then_inc(m["A_done"], 1)
                    for n in range(M):
                        wait(pe, m["A_copied"], i * M + n + 1)
                        nc.tensor.matmul(xbank[n][:, P:2 * P], A[n][:, :], A[n][:, :], start=True, stop=True
                                         ).then_inc(m["AA_done"], 1)
                    for n in range(M):
                        wait(pe, m["poly_ready"], i * M + n + 1)
                        for j in range(HT):
                            last = nc.tensor.matmul(tbank[n][:, j * P:(j + 1) * P], X[n][:, j * P:(j + 1) * P],
                                                    poly[n][:, :], start=True, stop=True)
                        last.then_inc(m["XT_done"], 1)
                        nc.tensor.matmul(xbank[n][:, :], poly[n][:, :], X[n][:, :], start=True, stop=True
                                         ).then_inc(m["X_done"], 1)

            @block.scalar
            def _(act):
                for n in range(M):
                    nc.scalar.copy(X[n][:, :], grads[n][:, :]).then_inc(m["grad_copied"], 1)
                for n in range(M):
                    wait(act, m["grad_copied"], n + 1)
                    if n:
                        wait(act, m["squares_summed"], n)
                    nc.scalar.activation(squares[:, :], X[n][:, :], ACT.Square, accum_out=ssq[:, n:n + 1]
                                         ).then_inc(m["squares_summed"], 1)
                wait(act, m["total_done"], 1)
                nc.scalar.copy(tot[:, :], xbank[0][:, 0:M]).then_inc(m["order"], 1)
                wait(act, m["order"], 1)
                nc.scalar.activation(nrm[:, :], tot[:, :], ACT.Sqrt).then_inc(m["norm_ready"], 1)
                for n in range(M):
                    wait(act, m["XT_done"], n + 1)
                    nc.scalar.copy(XT[n][:, :], tbank[n][:, :]).then_inc(m["xT_copied"], 1)
                @rounds(act, NS_ITERS)
                def _(i):
                    for n in range(M):
                        wait(act, m["XT_done"], (i + 1) * M + n + 1)
                        nc.scalar.copy(XT[n][:, :], tbank[n][:, :]).then_inc(m["xT_copied"], 1)
                wait(act, m["xT_copied"], (NS_ITERS + 1) * M)

            @block.vector
            def _(dve):
                nc.vector.tensor_scalar(aI[:, :], k.ident, NS_A, None, ALU.mult).then_inc(m["scaled_A"], 1)
                wait(dve, m["norm_ready"], 1)
                c = Chain(dve, m["updated"])
                c.link(nc.vector.tensor_scalar(inv[:, :], nrm[:, :], 1e-30, None, ALU.max))
                c.link(nc.vector.reciprocal(inv[:, :], inv[:, :]))
                c.link(mul(nc, inv[:, :], inv[:, :], tot[:, :]))
                c.link(nc.vector.tensor_tensor(inv[:, :], inv[:, :], nrm[:, :], ALU.add))
                c.link(nc.vector.tensor_scalar(inv[:, :], inv[:, :], 0.5, 1e-7 / GRAD_SCALE, ALU.mult, ALU.add))
                c.link(nc.vector.reciprocal(inv[:, :], inv[:, :]))
                for n in range(M):
                    nc.vector.tensor_scalar(X[n][:, :], X[n][:, :], inv[:, n:n + 1], None, ALU.mult
                                            ).then_inc(m["scaled"], 1)
                wait(dve, m["scaled"], M)
                @rounds(dve, NS_ITERS)
                def _(i):
                    for n in range(M):
                        wait(dve, m["A_done"], i * M + n + 1)
                        nc.vector.tensor_copy(A[n][:, :], xbank[n][:, 0:P]).then_inc(m["A_copied"], 1)
                    for n in range(M):
                        wait(dve, m["A_copied"], i * M + n + 1)
                        nc.vector.scalar_tensor_tensor(out=poly[n][:, :], in0=A[n][:, :], scalar=NS_B, in1=aI[:, :],
                                                       op0=ALU.mult, op1=ALU.add).then_inc(m["scaled_A"], 1)
                        wait(dve, m["scaled_A"], i * M + n + 2)
                        wait(dve, m["AA_done"], i * M + n + 1)
                        nc.vector.scalar_tensor_tensor(out=poly[n][:, :], in0=xbank[n][:, P:2 * P], scalar=NS_C,
                                                       in1=poly[n][:, :], op0=ALU.mult, op1=ALU.add
                                                       ).then_inc(m["poly_ready"], 1)
                    for n in range(M):
                        wait(dve, m["X_done"], i * M + n + 1)
                        nc.vector.tensor_copy(X[n][:, :], xbank[n][:, :]).then_inc(m["X_copied"], 1)
                wait(dve, m["X_copied"], NS_ITERS * M)
                wait(dve, m["xT_copied"], (NS_ITERS + 1) * M)
                for theta, step in ((k.theta_gate[:, :], X[0][:, :]), (k.theta_val[:, :], X[1][:, :]),
                                    (k.theta_projT[:, :], X[2][:, :]),
                                    (k.theta_proj[:, :, :].rearrange("p j c -> p (j c)"), XT[2][:, :])):
                    c.mark(nc.vector.scalar_tensor_tensor(out=theta, in0=step, scalar=-LR, in1=theta,
                                                          op0=ALU.mult, op1=ALU.add))
                wait(dve, m["updated"], c.n)


def query_phase(k):
    nc, d = k.nc, k.dram
    loaded, pp_done, pp_copied = k.sem("proj_w_loaded"), k.sem("pp_done"), k.sem("pp_copied")
    G_done, V_done, s_ready, hq_ready = k.sem("qG_done"), k.sem("qV_done"), k.sem("qs_ready"), k.sem("hq_ready")
    o_done, xb_ready, x_ready = k.sem("o_done"), k.sem("xb_ready"), k.sem("x1_ready")
    with ExitStack() as ctx:
        pw = k.sb(ctx, "proj_w_sb", [P, P])
        pb = k.sb(ctx, "proj_b_sb", [P, P])
        pp = k.sb(ctx, "proj_proj_w", [P, HT, P])
        s = k.sb(ctx, "q_s", [P, 2, SEQ])
        hq = [k.sb(ctx, f"hq{j}", [P, SEQ]) for j in range(HT)]
        xb = k.sb(ctx, "x_plus_b", [P, CT, P])
        with nc.Block() as block:
            @block.sync
            def _(sp):
                sp.dma_start(pw[:, :], d["L0_attn_proj_w"]).then_inc(loaded, 16)
                sp.dma_start(pb[:, :], spread(d["L0_attn_proj_b"])).then_inc(loaded, 16)

            @block.tensor
            def _(pe):
                wait(pe, loaded, 32)
                for j in range(HT):
                    last = nc.tensor.matmul(k.bank[0][:, j * P:(j + 1) * P], k.theta_projT[:, j * P:(j + 1) * P],
                                            pw[:, :], start=True, stop=True)
                last.then_inc(pp_done, 1)
                wait(pe, pp_copied, 1)
                @rounds(pe, CHUNKS)
                def _(i):
                    q = k.qT[:, bass.ds(i * SEQ, SEQ)]
                    for j in range(HT):
                        if j >= 2:
                            wait(pe, s_ready, i * HT + j - 1)
                        else:
                            wait(pe, hq_ready, i * HT)
                        nc.tensor.matmul(k.bank[j % 2][:, :], k.theta_gate[:, j * P:(j + 1) * P], q,
                                         start=True, stop=True).then_inc(G_done, 1)
                        if j >= 2:
                            wait(pe, hq_ready, i * HT + j - 1)
                        nc.tensor.matmul(k.bank[2 + j % 2][:, :], k.theta_val[:, j * P:(j + 1) * P], q,
                                         start=True, stop=True).then_inc(V_done, 1)
                    wait(pe, hq_ready, (i + 1) * HT)
                    wait(pe, x_ready, i)
                    for t in range(CT):
                        for j in range(HT):
                            last = nc.tensor.matmul(k.bank[4][:, t * P:(t + 1) * P], hq[j][:, t * P:(t + 1) * P],
                                                    pp[:, j, :], start=j == 0, stop=j == HT - 1)
                    last.then_inc(o_done, 1)

            @block.scalar
            def _(act):
                wait(act, pp_done, 1)
                nc.scalar.copy(pp[:, :, :].rearrange("p j c -> p (j c)"), k.bank[0][:, :]).then_inc(pp_copied, 1)
                @rounds(act, CHUNKS)
                def _(i):
                    for j in range(HT):
                        wait(act, G_done, i * HT + j + 1)
                        if j >= 2:
                            wait(act, hq_ready, i * HT + j - 1)
                        else:
                            wait(act, hq_ready, i * HT)
                        nc.scalar.activation(s[:, j % 2, :], k.bank[j % 2][:, :], ACT.Silu).then_inc(s_ready, 1)

            @block.gpsimd
            def _(pool):
                wait(pool, loaded, 32)
                @rounds(pool, CHUNKS)
                def _(i):
                    wait(pool, x_ready, i)
                    nc.gpsimd.tensor_tensor(xb[:, :, :], tiles_of(k.x, i),
                                            pb[:, :].unsqueeze(1).to_broadcast([P, CT, P]), ALU.add
                                            ).then_inc(xb_ready, 1)

            @block.vector
            def _(dve):
                @rounds(dve, CHUNKS)
                def _(i):
                    for j in range(HT):
                        wait(dve, s_ready, i * HT + j + 1)
                        wait(dve, V_done, i * HT + j + 1)
                        wait(dve, o_done, i)
                        mul(nc, hq[j][:, :], k.bank[2 + j % 2][:, :], s[:, j % 2, :]).then_inc(hq_ready, 1)
                    wait(dve, xb_ready, i + 1)
                    wait(dve, o_done, i + 1)
                    nc.vector.tensor_tensor(tiles_of(k.x, i), k.bank[4][:, :].rearrange("p (t c) -> p t c", t=CT),
                                            xb[:, :, :], ALU.add).then_inc(x_ready, 1)
                wait(dve, x_ready, CHUNKS)


def expert_weights_phase(k, f):
    nc, d = k.nc, k.dram
    vec_loaded, w_loaded, bias_loaded = k.sem("ln_vectors_loaded"), k.sem("experts_loaded"), k.sem("b_loaded")
    vecT_done, vecT_copied, lnb_ready = k.sem("vecT_done"), k.sem("vecT_copied"), k.sem("lnb_spread")
    w1T_done, w1T_copied, b1_done, b1_ready = (k.sem("w1T_done"), k.sem("w1T_copied"), k.sem("b1_done"),
                                               k.sem("b1_ready"))
    w2T_done, w2T_copied, scaled = k.sem("w2T_done"), k.sem("w2T_copied"), k.sem("w1_scaled")
    with ExitStack() as ctx:
        vec = k.sb(ctx, "centroids_g_b", [3 * E, P])
        w1n = k.sb(ctx, "w1_natural", [P, E * HT, P])
        w2n = k.sb(ctx, "w2_natural", [P, E, HID])
        lnb = [k.sb(ctx, f"ln_b_spread{a}", [P, P]) for a in range(2)]
        with nc.Block() as block:
            @block.sync
            def _(sp):
                for n, name in enumerate(("centroids", "ln_g", "ln_b")):
                    sp.dma_start(vec[n * E:(n + 1) * E, :], d["L0_ffn_" + name]).then_inc(vec_loaded, 16)
                for e in range(E):
                    sp.dma_start(w1n[:, e * HT:(e + 1) * HT, :], d["L0_ffn_w1"][e, :, :].rearrange("(j p) c -> p j c", p=P)
                                 ).then_inc(w_loaded, 16)
                    sp.dma_start(w2n[:, e, :], d["L0_ffn_w2"][e, :, :]).then_inc(w_loaded, 16)
                    sp.dma_start(f.b1[:, e, :], spread(d["L0_ffn_b1"][e, :])).then_inc(bias_loaded, 16)
                    sp.dma_start(f.b2[:, e, :], spread(d["L0_ffn_b2"][e, :])).then_inc(bias_loaded, 16)
                sp.wait_ge(bias_loaded, 32 * E)

            @block.tensor
            def _(pe):
                pe.wait_ge(vec_loaded, 48)
                nc.tensor.transpose(k.bank[4][:, 0:3 * E], vec[:, :], k.ident[0:3 * E, 0:3 * E]).then_inc(vecT_done, 1)
                pe.wait_ge(w_loaded, 32 * E)
                for e in range(E):
                    wait(pe, w1T_copied, e)
                    for j in range(HT):
                        last = nc.tensor.transpose(k.bank[0][:, j * P:(j + 1) * P], w1n[:, e * HT + j, :], k.ident)
                    last.then_inc(w1T_done, 1)
                    wait(pe, w2T_copied, e)
                    for j in range(HT):
                        last = nc.tensor.transpose(k.bank[1][:, j * P:(j + 1) * P], w2n[:, e, j * P:(j + 1) * P], k.ident)
                    last.then_inc(w2T_done, 1)
                    pe.wait_ge(w1T_copied, e + 1)
                    pe.wait_ge(lnb_ready, e + 1)
                    wait(pe, b1_ready, e)
                    nc.tensor.matmul(k.bank[2][:, :], lnb[e % 2][:, :], f.w1[:, e, :], start=True, stop=True
                                     ).then_inc(b1_done, 1)

            @block.scalar
            def _(act):
                act.wait_ge(vecT_done, 1)
                nc.scalar.copy(f.vecT[:, :], k.bank[4][:, 0:3 * E]).then_inc(vecT_copied, 1)
                for e in range(E):
                    act.wait_ge(w1T_done, e + 1)
                    nc.scalar.copy(f.w1[:, e, :], k.bank[0][:, :]).then_inc(w1T_copied, 1)
                    act.wait_ge(w2T_done, e + 1)
                    nc.scalar.copy(f.w2[:, e, :], k.bank[1][:, :]).then_inc(w2T_copied, 1)
                act.wait_ge(w2T_copied, E)

            @block.vector
            def _(dve):
                dve.wait_ge(vecT_copied, 1)
                dve.wait_ge(bias_loaded, 32 * E)

                def spread_ln_b(e):
                    wait(dve, b1_done, e - 1)
                    nc.vector.tensor_scalar(lnb[e % 2][:, :], k.c("ones"), f.vecT[:, 2 * E + e:2 * E + e + 1], None,
                                            ALU.mult).then_inc(lnb_ready, 1)

                spread_ln_b(0)
                for e in range(E):
                    if e + 1 < E:
                        spread_ln_b(e + 1)
                    dve.wait_ge(b1_done, e + 1)
                    nc.vector.tensor_tensor(f.b1[:, e, :], k.bank[2][:, :], f.b1[:, e, :], ALU.add).then_inc(b1_ready, 1)
                    nc.vector.tensor_scalar(f.w1[:, e, :], f.w1[:, e, :], f.vecT[:, E + e:E + e + 1], None,
                                            ALU.mult).then_inc(scaled, 1)
                dve.wait_ge(b1_ready, E)
                dve.wait_ge(scaled, E)


def affinity_phase(k, f):
    nc = k.nc
    order_p, xl_ready, xlT_done, xlT_copied = k.sem("aff_order"), k.sem("xl_ready"), k.sem("xlT_done"), k.sem("xlT_copied")
    xl_kept, aff_done, aff_copied = k.sem("xl_kept"), k.sem("aff_done"), k.sem("aff_copied")
    max_ready, alpha_ready, order_v, count_done = (k.sem("aff_max_ready"), k.sem("alpha_ready"), k.sem("route_order"),
                                                   k.sem("count_done"))
    oh_ready = k.sem("onehot_ready")
    with ExitStack() as ctx:
        xc = k.sb(ctx, "aff_xc", [P, CT, P])
        xl = k.sb(ctx, "aff_xl", [P, CT, P])
        xT = k.sb(ctx, "aff_xT", [P, SEQ])
        aff = k.sb(ctx, "aff", [P, TILES, E])
        oh = k.sb(ctx, "onehot", [P, TILES, E])
        key = k.sb(ctx, "route_key", [P, TILES, E])
        top = k.sb(ctx, "route_max", [P, TILES])
        rank = k.sb(ctx, "route_rank", [P, TILES])
        total = k.sb(ctx, "totals", [P, E, TILES])
        incl = k.sb(ctx, "inclusive", [P, E, TILES])
        cmp = k.sb(ctx, "tile_starts_used", [P, E, TILES])
        ntile = k.sb(ctx, "tiles_of_expert", [P, E])
        ends = k.sb(ctx, "expert_ends", [P, E])
        firsts = k.sb(ctx, "expert_firsts", [P, E])
        pos = k.sb(ctx, "positions", [P, TILES])
        scmp = k.sb(ctx, "slot_compare", [P, PADDED, E - 1])
        sexp = k.sb(ctx, "slot_expert_f", [P, PADDED])
        with nc.Block() as block:
            @block.gpsimd
            def _(pool):
                @rounds(pool, CHUNKS)
                def _(i):
                    c = Chain(pool, order_p, i)
                    wait(pool, xl_ready, i)
                    c.link(nc.gpsimd.tensor_tensor(xc[:, :, :], tiles_of(k.x, i), per_token(k.mean, i), ALU.subtract))
                    wait(pool, xlT_done, i)
                    wait(pool, xl_kept, i)
                    nc.gpsimd.tensor_tensor(xl[:, :, :], xc[:, :, :], per_token(k.rstd, i), ALU.mult).then_inc(xl_ready, 1)

            @block.scalar
            def _(act):
                @rounds(act, CHUNKS)
                def _(i):
                    act.wait_ge(xl_ready, i + 1)
                    nc.scalar.copy(tiles_of(f.xl, i), xl[:, :, :]).then_inc(xl_kept, 1)
                    act.wait_ge(xlT_done, i + 1)
                    wait(act, aff_done, i)
                    nc.scalar.copy(xT[:, :], k.bank[2][:, :]).then_inc(xlT_copied, 1)
                act.wait_ge(max_ready, 1)
                nc.scalar.activation(f.alpha[:, :], top[:, :], ACT.Sigmoid).then_inc(alpha_ready, 1)
                act.wait_ge(alpha_ready, 1)
                act.wait_ge(xl_kept, CHUNKS)

            @block.tensor
            def _(pe):
                @rounds(pe, CHUNKS)
                def _(i):
                    pe.wait_ge(xl_ready, i + 1)
                    wait(pe, xlT_copied, i)
                    for j in range(CT):
                        last = nc.tensor.transpose(k.bank[2][:, j * P:(j + 1) * P], xl[:, j, :], k.ident)
                    last.then_inc(xlT_done, 1)
                    pe.wait_ge(xlT_copied, i + 1)
                    wait(pe, aff_copied, i)
                    for j in range(CT):
                        last = nc.tensor.matmul(k.bank[3][:, j * E:(j + 1) * E], xT[:, j * P:(j + 1) * P],
                                                f.vecT[:, 0:E], start=True, stop=True)
                    last.then_inc(aff_done, 1)
                flat = oh[:, :, :].rearrange("p t e -> p (t e)")
                pe.wait_ge(oh_ready, 1)
                nc.tensor.matmul(k.bank[4][:, 0:TILES * E], k.c("before"), flat, start=True, stop=True)
                nc.tensor.matmul(k.bank[5][:, 0:TILES * E], k.c("ones"), flat, start=True, stop=True
                                 ).then_inc(count_done, 1)

            @block.vector
            def _(dve):
                @rounds(dve, CHUNKS)
                def _(i):
                    dve.wait_ge(aff_done, i + 1)
                    nc.vector.tensor_copy(tiles_of(aff, i), k.bank[3][:, 0:CT * E].rearrange("p (t e) -> p t e", e=E)
                                          ).then_inc(aff_copied, 1)
                dve.wait_ge(aff_copied, CHUNKS)

                def over_e(t):
                    return t.unsqueeze(2).to_broadcast([P, TILES, E])
                nc.vector.tensor_reduce(top[:, :], aff[:, :, :], AXX, ALU.max).then_inc(max_ready, 1)
                dve.wait_ge(max_ready, 1)
                c = Chain(dve, order_v)
                rank8 = k.c("rank8").unsqueeze(1).to_broadcast([P, TILES, E])
                c.link(nc.vector.tensor_tensor(key[:, :, :], aff[:, :, :], over_e(top[:, :]), ALU.is_equal))
                c.link(mul(nc, key[:, :, :], key[:, :, :], rank8))
                c.link(nc.vector.tensor_reduce(rank[:, :], key[:, :, :], AXX, ALU.max))
                nc.vector.tensor_tensor(oh[:, :, :], key[:, :, :], over_e(rank[:, :]), ALU.is_equal).then_inc(oh_ready, 1)
                dve.wait_ge(count_done, 1)
                tot_ps = k.bank[5][:, 0:TILES * E].rearrange("p (t e) -> p e t", e=E)
                pre_ps = k.bank[4][:, 0:TILES * E].rearrange("p (t e) -> p t e", e=E)
                c.link(nc.vector.tensor_copy(total[:, :, :], tot_ps))

                def flat(t):
                    return t[:, :, :].rearrange("p e t -> p (e t)")
                c.link(nc.vector.tensor_tensor_scan(flat(incl), k.c("starts"), flat(total), 0.0, ALU.mult, ALU.add))
                c.mark(nc.vector.tensor_tensor(total[:, :, :], incl[:, :, :], total[:, :, :], ALU.subtract))
                c.link(nc.vector.tensor_tensor(cmp[:, :, :], incl[:, :, TILES - 1:TILES].to_broadcast([P, E, TILES]),
                                               k.c("tilestart").unsqueeze(1).to_broadcast([P, E, TILES]), ALU.is_gt))
                c.link(nc.vector.tensor_reduce(ntile[:, :], cmp[:, :, :], AXX, ALU.add))
                c.link(nc.vector.tensor_tensor_scan(ends[:, :], k.c("ones")[:, 0:E], ntile[:, :], 0.0, ALU.mult, ALU.add))
                c.mark(nc.vector.tensor_tensor(scmp[:, :, :], k.c("slot").unsqueeze(2).to_broadcast([P, PADDED, E - 1]),
                                               ends[:, 0:E - 1].unsqueeze(1).to_broadcast([P, PADDED, E - 1]), ALU.is_ge))
                c.link(nc.vector.tensor_tensor(firsts[:, :], ends[:, :], ntile[:, :], ALU.subtract))
                c.link(nc.vector.tensor_reduce(sexp[:, :], scmp[:, :, :], AXX, ALU.add))
                c.mark(nc.vector.tensor_copy(f.slot_expert[:, :], sexp[:, :]))
                c.link(nc.vector.tensor_scalar(firsts[:, :], firsts[:, :], float(P), None, ALU.mult))
                c.link(nc.vector.tensor_tensor(total[:, :, :], total[:, :, :],
                                               firsts[:, :].unsqueeze(2).to_broadcast([P, E, TILES]), ALU.add))
                c.link(nc.vector.tensor_tensor(key[:, :, :], pre_ps, total[:, :, :].rearrange("p e t -> p t e"), ALU.add))
                c.link(mul(nc, key[:, :, :], key[:, :, :], oh[:, :, :]))
                c.link(nc.vector.tensor_reduce(pos[:, :], key[:, :, :], AXX, ALU.add))
                c.link(nc.vector.tensor_copy(f.pos[:, :], pos[:, :]))


def sort_phase(k, f):
    nc = k.nc
    order, halves, scattered = k.sem("xhat_order"), k.sem("xhat_ready"), k.sem("xhat_scattered")
    H = TILES // 2
    with nc.Block() as block:
        def normalise(eng, ns, at, c):
            t = slice(at, at + H)
            c.link(ns.tensor_tensor(f.xhat[:, t, :], f.xl[:, t, :], k.mean[:, t].unsqueeze(2).to_broadcast([P, H, P]),
                                    ALU.subtract))
            ns.tensor_tensor(f.xhat[:, t, :], f.xhat[:, t, :], k.rstd[:, t].unsqueeze(2).to_broadcast([P, H, P]),
                             ALU.mult).then_inc(halves, 1)

        @block.vector
        def _(dve):
            normalise(dve, nc.vector, 0, Chain(dve, order))

        @block.gpsimd
        def _(pool):
            normalise(pool, nc.gpsimd, H, Chain(pool, k.sem("xhat_order_pool")))
            pool.wait_ge(halves, 2)
            for t in range(TILES):
                pool.indirect_dma_start(out=f.sorted_in, out_offset=bass.IndirectOffsetOnAxis(ap=f.pos[:, t:t + 1], axis=0),
                                        in_=f.xhat[:, t, :], in_offset=None).then_inc(scattered, 16)
            pool.wait_ge(scattered, 16 * TILES)


def experts_phase(k, f):
    nc = k.nc
    R = 3
    assert PADDED % R == 0
    x_loaded = [k.sem(f"xs_loaded{a}") for a in range(R)]
    y_stored = [k.sem(f"ys_stored{a}") for a in range(R)]
    m = {n: k.sem(f"moe_{n}") for n in ("xT_done", "xT_copied", "h_done", "h_ready", "hT_done", "hT_ready",
                                        "y_done", "y_ready")}
    with ExitStack() as ctx:
        xs = [k.sb(ctx, f"xs{a}", [P, P]) for a in range(R)]
        ys = [k.sb(ctx, f"ys{a}", [P, P]) for a in range(R)]
        xT = [k.sb(ctx, f"xsT{a}", [P, P]) for a in range(2)]
        h = k.sb(ctx, "moe_h", [P, HID])
        hT = k.sb(ctx, "moe_hT", [P, HID])
        w1 = f.w1[:, :, :].rearrange("p e c -> p (e c)")
        w2 = f.w2[:, :, :].rearrange("p e c -> p (e c)")
        b1 = f.b1[:, :, :].rearrange("p e c -> p (e c)")
        b2 = f.b2[:, :, :].rearrange("p e c -> p (e c)")
        XT_BANK, H_BANK, HT_BANK, Y_BANK = k.bank[0:4]

        def expert(eng, t):
            return eng.value_load(f.slot_expert[0:1, bass.ds(t, 1)], min_val=0, max_val=E - 1)

        with nc.Block() as block:
            @block.gpsimd
            def _(pool):
                def load(i, a, prefetch=True):
                    t = i * R + a
                    wait(pool, m["xT_done"], t - R + 1)
                    pool.dma_start(xs[a][:, :], f.sorted_in[bass.ds(t * P, P), :]).then_inc(x_loaded[a], 16)

                def store(i, a):
                    t = i * R + a
                    pool.wait_ge(m["y_ready"], t + 1)
                    pool.dma_start(f.sorted_out[bass.ds(t * P, P), :], ys[a][:, :]).then_inc(y_stored[a], 16)

                for a in range(R):
                    load(0, a)
                for a in range(R):
                    load(1, a)
                    store(0, a)
                with pool.Fori(1, PADDED // R - 1) as i:
                    for a in range(R):
                        load(i + 1, a)
                        store(i, a)
                for a in range(R):
                    store(PADDED // R - 1, a)
                for a in range(R):
                    pool.wait_ge(y_stored[a], 16 * (PADDED // R))

            @block.tensor
            def _(pe):
                def transpose_x(i, a, odd):
                    t = i * R + a
                    pe.wait_ge(x_loaded[a], (i + 1) * 16)
                    wait(pe, m["xT_copied"], t)
                    nc.tensor.transpose(XT_BANK[:, 0:P], xs[a][:, :], k.ident).then_inc(m["xT_done"], 1)

                def hidden(t):
                    e = expert(pe, t)
                    pe.wait_ge(m["xT_copied"], t + 1)
                    wait(pe, m["h_ready"], t)
                    nc.tensor.matmul(H_BANK[:, :], xT[0][:, :], w1[:, bass.ds(e * HID, HID)], start=True, stop=True
                                     ).then_inc(m["h_done"], 1)

                def finish(t, i, a, ahead=True):
                    e = expert(pe, t)
                    pe.wait_ge(m["h_ready"], t + 1)
                    wait(pe, m["hT_ready"], t)
                    for j in range(HT):
                        last = nc.tensor.transpose(HT_BANK[:, j * P:(j + 1) * P], h[:, j * P:(j + 1) * P], k.ident)
                    last.then_inc(m["hT_done"], 1)
                    if ahead:
                        ni, na = (i, a + 1) if a + 1 < R else (i + 1, 0)
                        transpose_x(ni, na, 0)
                        hidden(t + 1)
                    pe.wait_ge(m["hT_ready"], t + 1)
                    wait(pe, m["y_ready"], t)
                    for j in range(HT):
                        last = nc.tensor.matmul(Y_BANK[:, 0:P], hT[:, j * P:(j + 1) * P],
                                                w2[:, bass.ds(e * HID + j * P, P)], start=j == 0, stop=j == HT - 1)
                    last.then_inc(m["y_done"], 1)

                transpose_x(0, 0, 0)
                hidden(0)
                for a in range(R):
                    finish(a, 0, a)
                with pe.Fori(1, PADDED // R - 1) as i:
                    for a in range(R):
                        finish(i * R + a, i, a)
                for a in range(R):
                    finish(PADDED - R + a, PADDED // R - 1, a, ahead=a < R - 1)

            @block.scalar
            def _(act):
                def copy_x(t):
                    act.wait_ge(m["xT_done"], t + 1)
                    wait(act, m["h_done"], t)
                    nc.scalar.copy(xT[0][:, :], XT_BANK[:, 0:P]).then_inc(m["xT_copied"], 1)

                def step(t, ahead=True):
                    if ahead:
                        copy_x(t + 1)
                    act.wait_ge(m["hT_done"], t + 1)
                    wait(act, m["y_done"], t)
                    nc.scalar.activation(hT[:, :], HT_BANK[:, :], ACT.Relu).then_inc(m["hT_ready"], 1)

                copy_x(0)
                step(0)
                with act.Fori(1, PADDED - 1) as t:
                    step(t)
                step(PADDED - 1, ahead=False)

            @block.vector
            def _(dve):
                def bias_h(t):
                    e = expert(dve, t)
                    dve.wait_ge(m["h_done"], t + 1)
                    wait(dve, m["hT_done"], t)
                    nc.vector.tensor_tensor(h[:, :], H_BANK[:, :], b1[:, bass.ds(e * HID, HID)], ALU.add
                                            ).then_inc(m["h_ready"], 1)

                def step(i, a, ahead=True):
                    t = i * R + a
                    if ahead:
                        bias_h(t + 1)
                    e = expert(dve, t)
                    dve.wait_ge(m["y_done"], t + 1)
                    wait(dve, y_stored[a], i * 16)
                    nc.vector.tensor_tensor(ys[a][:, :], Y_BANK[:, 0:P], b2[:, bass.ds(e * P, P)], ALU.add
                                            ).then_inc(m["y_ready"], 1)

                bias_h(0)
                for a in range(R):
                    step(0, a)
                with dve.Fori(1, PADDED // R - 1) as i:
                    for a in range(R):
                        step(i, a)
                for a in range(R):
                    step(PADDED // R - 1, a, ahead=a < R - 1)


def combine_phase(k, f):
    nc = k.nc
    fetched, order, order_p = k.sem("expert_out_fetched"), k.sem("combine_order"), k.sem("x_plus_xl")
    y = f.xhat
    with nc.Block() as block:
        @block.gpsimd
        def _(pool):
            for t in range(TILES):
                pool.indirect_dma_start(out=y[:, t, :], out_offset=None, in_=f.sorted_out,
                                        in_offset=bass.IndirectOffsetOnAxis(ap=f.pos[:, t:t + 1], axis=0)
                                        ).then_inc(fetched, 16)
            pool.wait_ge(fetched, 16 * TILES)

        @block.vector
        def _(dve):
            c = Chain(dve, order)
            c.link(nc.vector.tensor_tensor(k.x[:, :, :], k.x[:, :, :], f.xl[:, :, :], ALU.add))
            dve.wait_ge(fetched, 16 * TILES)
            c.link(mul(nc, y[:, :, :], y[:, :, :], f.alpha[:, :].unsqueeze(2).to_broadcast([P, TILES, P])))
            c.link(nc.vector.tensor_tensor(k.x[:, :, :], k.x[:, :, :], y[:, :, :], ALU.add))


def diagonal_attention_phase(k):
    nc, d = k.nc, k.dram
    G = CT * HEADS
    loaded, order_p = k.sem("wqkv_loaded"), k.sem("da_order_p")
    prep_done, prep_ready = k.sem("blockdiag_done"), k.sem("blockdiag_ready")
    xn_ready, xT_done, xT_copied = k.sem("da_xn_ready"), k.sem("da_xT_done"), k.sem("da_xT_copied")
    form_done, form_used, score_ready = k.sem("form_done"), k.sem("form_used"), k.sem("score_ready")
    sum_spread, vsum_done, vsum_copied = k.sem("sum_spread"), k.sem("vsum_done"), k.sem("vsum_copied")
    order, shifted, exp_ready = k.sem("da_order"), k.sem("scores_shifted"), k.sem("da_exp_ready")
    probs_ready, term_ready, x_ready = k.sem("da_probs_ready"), k.sem("da_term_ready"), k.sem("x3_ready")
    with ExitStack() as ctx:
        wq = k.sb(ctx, "wq", [HD, HD])
        wkr = k.sb(ctx, "wk_repeated", [HD, HEADS, HD])
        wvr = k.sb(ctx, "wv_repeated", [HD, HEADS, HD])
        a1 = k.sb(ctx, "wq_wk", [HD, P])
        form = k.sb(ctx, "qk_form", [P, P])
        bdv = k.sb(ctx, "wv_blocks", [P, P])
        xc = k.sb(ctx, "da_xc", [P, CT, P])
        xn = [k.sb(ctx, f"da_xn{a}", [P, CT, P]) for a in range(2)]
        xT = k.sb(ctx, "da_xT", [P, SEQ])
        xsum = k.sb(ctx, "da_xsum", [P, 1])
        xsb = k.sb(ctx, "da_xsum_spread", [P, P])
        prod = k.sb(ctx, "da_prod", [P, SEQ])
        sc = k.sb(ctx, "da_scores", [P, CHUNKS, G])
        top = k.sb(ctx, "da_max", [P, G])
        den = k.sb(ctx, "da_den", [P, G])
        vs = k.sb(ctx, "da_vsum", [P, CHUNKS, P])
        term = [k.sb(ctx, f"da_term{a}", [P, CT, P]) for a in range(2)]
        CH2 = CHUNKS // 2

        def pairs(eng):
            def run(body):
                body(0, 0)
                body(0, 1)
                with eng.Fori(1, CH2) as i:
                    body(i, 0)
                    body(i, 1)
            return run

        with nc.Block() as block:
            @block.sync
            def _(sp):
                sp.dma_start(wq[:, :], d["L1_attn_Wq"]).then_inc(loaded, 16)
                for h in range(HEADS):
                    sp.dma_start(wkr[:, h, :], d["L1_attn_Wk"]).then_inc(loaded, 16)
                    sp.dma_start(wvr[:, h, :], d["L1_attn_Wv"]).then_inc(loaded, 16)

            @block.gpsimd
            def _(pool):
                @pairs(pool)
                def _(i, a):
                    t = i * 2 + a
                    c = Chain(pool, order_p, t)
                    wait(pool, xn_ready, t)
                    c.link(nc.gpsimd.tensor_tensor(xc[:, :, :], tiles_of(k.x, t), per_token(k.mean, t), ALU.subtract))
                    wait(pool, score_ready, t - 1)
                    nc.gpsimd.tensor_tensor(xn[a][:, :, :], xc[:, :, :], per_token(k.rstd, t), ALU.mult
                                            ).then_inc(xn_ready, 1)
                for c in range(CHUNKS):
                    pool.wait_ge(term_ready, c + 1)
                    at = slice(c * CT, (c + 1) * CT)
                    nc.gpsimd.tensor_tensor(k.x[:, at, :], k.x[:, at, :], term[c % 2][:, :, :], ALU.add).then_inc(x_ready, 1)
                pool.wait_ge(x_ready, CHUNKS)

            @block.tensor
            def _(pe):
                pe.wait_ge(loaded, 16 * (1 + 2 * HEADS))
                nc.tensor.matmul(k.bank[0][0:HD, 0:P], wq[:, :], wkr[:, :, :].rearrange("e h d -> e (h d)"),
                                 start=True, stop=True).then_inc(prep_done, 1)
                nc.tensor.matmul(k.bank[1][:, 0:P], wvr[:, :, :].rearrange("e h d -> e (h d)"), k.c("headtile")[0:HD, :],
                                 start=True, stop=True).then_inc(prep_done, 1)
                pe.wait_ge(prep_ready, 1)
                nc.tensor.matmul(k.bank[2][:, 0:P], k.c("headtile")[0:HD, :], a1[:, :], start=True, stop=True
                                 ).then_inc(prep_done, 1)
                pe.wait_ge(prep_ready, 3)

                @pairs(pe)
                def _(i, a):
                    t = i * 2 + a
                    pe.wait_ge(xn_ready, t + 1)
                    wait(pe, xT_copied, t)
                    for j in range(CT):
                        last = nc.tensor.transpose(k.bank[0][:, j * P:(j + 1) * P], xn[a][:, j, :], k.ident)
                    last.then_inc(xT_done, 1)
                    pe.wait_ge(xT_copied, t + 1)
                    wait(pe, form_used, t)
                    for j in range(CT):
                        last = nc.tensor.matmul(k.bank[1][:, j * P:(j + 1) * P], xT[:, j * P:(j + 1) * P], form[:, :],
                                                start=True, stop=True)
                    last.then_inc(form_done, 1)
                    pe.wait_ge(sum_spread, t + 1)
                    wait(pe, vsum_copied, t)
                    nc.tensor.matmul(k.bank[2][:, 0:P], xsb[:, :], bdv[:, :], start=True, stop=True).then_inc(vsum_done, 1)

            @block.scalar
            def _(act):
                @pairs(act)
                def _(i, a):
                    t = i * 2 + a
                    act.wait_ge(xT_done, t + 1)
                    wait(act, form_done, t)
                    wait(act, sum_spread, t)
                    nc.scalar.activation(xT[:, :], k.bank[0][:, :], ACT.Identity, accum_out=xsum[:, :]).then_inc(xT_copied, 1)
                    act.wait_ge(vsum_done, t + 1)
                    nc.scalar.copy(vs[:, bass.ds(t, 1), :].rearrange("p a c -> p (a c)"), k.bank[2][:, 0:P]
                                   ).then_inc(vsum_copied, 1)
                act.wait_ge(shifted, 1)
                nc.scalar.activation(sc[:, :, :], sc[:, :, :], ACT.Exp, scale=float(P) ** -0.5).then_inc(exp_ready, 1)

            @block.vector
            def _(dve):
                dve.wait_ge(prep_done, 2)
                nc.vector.tensor_copy(a1[:, :], k.bank[0][0:HD, 0:P]).then_inc(prep_ready, 1)
                mul(nc, bdv[:, :], k.bank[1][:, 0:P], k.c("headmask")).then_inc(prep_ready, 1)
                dve.wait_ge(prep_done, 3)
                mul(nc, form[:, :], k.bank[2][:, 0:P], k.c("headmask")).then_inc(prep_ready, 1)

                @pairs(dve)
                def _(i, a):
                    t = i * 2 + a
                    dve.wait_ge(xT_copied, t + 1)
                    wait(dve, vsum_done, t)
                    nc.vector.tensor_scalar(xsb[:, :], k.c("ones"), xsum[:, 0:1], None, ALU.mult).then_inc(sum_spread, 1)
                    dve.wait_ge(form_done, t + 1)
                    wait(dve, score_ready, t)
                    mul(nc, prod[:, :], k.bank[1][:, :], xn[a][:, :, :].rearrange("p t c -> p (t c)")).then_inc(form_used, 1)
                    dve.wait_ge(form_used, t + 1)
                    nc.vector.tensor_reduce(sc[:, bass.ds(t, 1), :].rearrange("p a g -> p (a g)"),
                                            prod[:, :].rearrange("p (g e) -> p g e", e=HD), AXX, ALU.add
                                            ).then_inc(score_ready, 1)
                dve.wait_ge(score_ready, CHUNKS)
                dve.wait_ge(vsum_copied, CHUNKS)
                c = Chain(dve, order)
                by_group = sc[:, :, :].rearrange("p c g -> p g c")

                def over_c(t):
                    return t.unsqueeze(1).to_broadcast([P, CHUNKS, G])
                c.link(nc.vector.tensor_reduce(top[:, :], by_group, AXX, ALU.max))
                nc.vector.tensor_tensor(sc[:, :, :], sc[:, :, :], over_c(top[:, :]), ALU.subtract).then_inc(shifted, 1)
                dve.wait_ge(exp_ready, 1)
                c.link(nc.vector.tensor_reduce(den[:, :], by_group, AXX, ALU.add))
                c.link(nc.vector.reciprocal(den[:, :], den[:, :]))
                c.link(mul(nc, sc[:, :, :], sc[:, :, :], over_c(den[:, :])))
                for s in range(CHUNKS):
                    wait(dve, x_ready, s - 1)
                    mul(nc, term[s % 2][:, :, :].rearrange("p t (h e) -> p t h e", e=HD),
                        sc[:, s, :].rearrange("p (t h) -> p t h", h=HEADS).unsqueeze(3).to_broadcast([P, CT, HEADS, HD]),
                        vs[:, s, :].rearrange("p (h e) -> p h e", e=HD).unsqueeze(1).to_broadcast([P, CT, HEADS, HD])
                        ).then_inc(term_ready, 1)


def router_phase(k, g):
    nc, d = k.nc, k.dram
    loaded, order_p, xf_ready = k.sem("router_loaded"), k.sem("r_order_p"), k.sem("xf_ready")
    xf_kept, xT_done, xT_copied = k.sem("xf_kept"), k.sem("r_xT_done"), k.sem("r_xT_copied")
    hid_done, hid_ready, log_done, log_copied = k.sem("r_hid_done"), k.sem("r_hid_ready"), k.sem("log_done"), k.sem("log_copied")
    sw_ready, shifted, exp_ready, order = k.sem("sw_ready"), k.sem("r_shifted"), k.sem("r_exp_ready"), k.sem("r_order")
    with ExitStack() as ctx:
        w1 = k.sb(ctx, "router_w1", [P, RH])
        b1 = k.sb(ctx, "router_b1", [RH, 1])
        w2 = k.sb(ctx, "router_w2", [RH, E])
        b2 = k.sb(ctx, "router_b2", [P, E])
        sw = k.sb(ctx, "shared_weight", [P, 2])
        xc = k.sb(ctx, "r_xc", [P, CT, P])
        xf = k.sb(ctx, "r_xf", [P, CT, P])
        hid = k.sb(ctx, "r_hid", [RH, SEQ])
        lg = k.sb(ctx, "logits", [P, TILES, E])
        key = k.sb(ctx, "r_key", [P, TILES, E])
        one = k.sb(ctx, "r_one", [P, TILES])
        best = k.sb(ctx, "r_best", [P, 2, TILES])
        with nc.Block() as block:
            @block.sync
            def _(sp):
                sp.dma_start(w1[:, :], d["L1_ffn_router_w1"]).then_inc(loaded, 16)
                sp.dma_start(b1[:, :], d["L1_ffn_router_b1"].rearrange("(p a) -> p a", a=1)).then_inc(loaded, 16)
                sp.dma_start(w2[:, :], d["L1_ffn_router_w2"]).then_inc(loaded, 16)
                sp.dma_start(b2[:, :], spread(d["L1_ffn_router_b2"])).then_inc(loaded, 16)
                sp.dma_start(sw[:, 0:1], spread(d["L1_ffn_shared_weight"])).then_inc(loaded, 16)

            @block.gpsimd
            def _(pool):
                @rounds(pool, CHUNKS)
                def _(i):
                    c = Chain(pool, order_p, i)
                    wait(pool, xf_ready, i)
                    c.link(nc.gpsimd.tensor_tensor(xc[:, :, :], tiles_of(k.x, i), per_token(k.mean, i), ALU.subtract))
                    wait(pool, xT_done, i)
                    wait(pool, xf_kept, i)
                    nc.gpsimd.tensor_tensor(xf[:, :, :], xc[:, :, :], per_token(k.rstd, i), ALU.mult).then_inc(xf_ready, 1)

            @block.tensor
            def _(pe):
                pe.wait_ge(loaded, 80)

                @rounds(pe, CHUNKS)
                def _(i):
                    pe.wait_ge(xf_ready, i + 1)
                    wait(pe, xT_copied, i)
                    for j in range(CT):
                        last = nc.tensor.transpose(k.bank[0][:, j * P:(j + 1) * P], xf[:, j, :], k.ident)
                    last.then_inc(xT_done, 1)
                    pe.wait_ge(xT_copied, i + 1)
                    wait(pe, hid_ready, i)
                    nc.tensor.matmul(k.bank[1][0:RH, :], w1[:, :], g.xfT[:, bass.ds(i * SEQ, SEQ)], start=True, stop=True
                                     ).then_inc(hid_done, 1)
                    pe.wait_ge(hid_ready, i + 1)
                    wait(pe, log_copied, i)
                    for j in range(CT):
                        last = nc.tensor.matmul(k.bank[2][:, j * E:(j + 1) * E], hid[:, j * P:(j + 1) * P], w2[:, :],
                                                start=True, stop=True)
                    last.then_inc(log_done, 1)

            @block.scalar
            def _(act):
                act.wait_ge(loaded, 80)
                nc.scalar.activation(sw[:, 0:1], sw[:, 0:1], ACT.Sigmoid).then_inc(sw_ready, 1)

                @rounds(act, CHUNKS)
                def _(i):
                    act.wait_ge(xf_ready, i + 1)
                    nc.scalar.copy(tiles_of(g.xf, i), xf[:, :, :]).then_inc(xf_kept, 1)
                    act.wait_ge(xT_done, i + 1)
                    nc.scalar.copy(g.xfT[:, bass.ds(i * SEQ, SEQ)], k.bank[0][:, :]).then_inc(xT_copied, 1)
                    act.wait_ge(hid_done, i + 1)
                    wait(act, log_done, i)
                    nc.scalar.activation(hid[:, :], k.bank[1][0:RH, :], ACT.Gelu, bias=b1[:, 0:1]).then_inc(hid_ready, 1)
                act.wait_ge(shifted, 1)
                nc.scalar.activation(lg[:, :, :], lg[:, :, :], ACT.Exp).then_inc(exp_ready, 1)
                act.wait_ge(exp_ready, 1)

            @block.vector
            def _(dve):
                dve.wait_ge(loaded, 80)

                @rounds(dve, CHUNKS)
                def _(i):
                    dve.wait_ge(log_done, i + 1)
                    nc.vector.tensor_tensor(tiles_of(lg, i), k.bank[2][:, 0:CT * E].rearrange("p (t e) -> p t e", e=E),
                                            b2[:, :].unsqueeze(1).to_broadcast([P, CT, E]), ALU.add).then_inc(log_copied, 1)
                dve.wait_ge(log_copied, CHUNKS)
                c = Chain(dve, order)

                def over_e(t):
                    return t.unsqueeze(2).to_broadcast([P, TILES, E])
                rank8 = k.c("rank8").unsqueeze(1).to_broadcast([P, TILES, E])
                c.link(nc.vector.tensor_reduce(one[:, :], lg[:, :, :], AXX, ALU.max))
                nc.vector.tensor_tensor(lg[:, :, :], lg[:, :, :], over_e(one[:, :]), ALU.subtract).then_inc(shifted, 1)
                dve.wait_ge(exp_ready, 1)
                c.link(nc.vector.tensor_reduce(one[:, :], lg[:, :, :], AXX, ALU.add))
                c.link(nc.vector.reciprocal(one[:, :], one[:, :]))
                c.link(mul(nc, lg[:, :, :], lg[:, :, :], over_e(one[:, :])))
                for s in range(2):
                    oh = g.onehot[:, :, s * E:(s + 1) * E]
                    c.link(nc.vector.tensor_reduce(best[:, s, :], lg[:, :, :], AXX, ALU.max))
                    c.link(nc.vector.tensor_tensor(key[:, :, :], lg[:, :, :], over_e(best[:, s, :]), ALU.is_equal))
                    c.link(mul(nc, key[:, :, :], key[:, :, :], rank8))
                    c.link(nc.vector.tensor_reduce(one[:, :], key[:, :, :], AXX, ALU.max))
                    c.link(nc.vector.tensor_tensor(oh, key[:, :, :], over_e(one[:, :]), ALU.is_equal))
                    if s == 0:
                        c.link(nc.vector.scalar_tensor_tensor(out=lg[:, :, :], in0=oh, scalar=-2.0, in1=lg[:, :, :],
                                                              op0=ALU.mult, op1=ALU.add))
                c.link(nc.vector.tensor_tensor(one[:, :], best[:, 0, :], best[:, 1, :], ALU.add))
                c.link(nc.vector.reciprocal(one[:, :], one[:, :]))
                dve.wait_ge(sw_ready, 1)
                c.link(nc.vector.tensor_scalar(sw[:, 1:2], sw[:, 0:1], -1.0, 1.0, ALU.mult, ALU.add))
                c.link(nc.vector.tensor_scalar(one[:, :], one[:, :], sw[:, 1:2], None, ALU.mult))
                c.link(nc.vector.tensor_scalar(g.weight[:, 0, :], k.c("ones")[:, 0:TILES], sw[:, 0:1], None, ALU.mult))
                for s in range(2):
                    c.link(mul(nc, g.weight[:, 1 + s, :], best[:, s, :], one[:, :]))


def dynamics_weights_phase(k, g):
    nc, d = k.nc, k.dram
    loaded, cut, order, placed = k.sem("dyn_loaded"), k.sem("b2_cut"), k.sem("dyn_order"), k.sem("b2_placed")
    H2 = 2 * EH
    loads = []

    def load(sp, to, of):
        loads.append(sp.dma_start(to, of))
        loads[-1].then_inc(loaded, 16)

    with ExitStack() as ctx:
        b2 = k.sb(ctx, "expert_b2_sb", [E, CTRL])
        rest = k.sb(ctx, "b2_rest", [E, CTRL])
        back = k.sb(ctx, "b2_back", [E, CTRL])
        part = k.sb(ctx, "b2_parts", [E, 3, CTRL], BF16)
        with nc.Block() as block:
            @block.sync
            def _(sp):
                sp.wait_ge(order, 3)
                load(sp, b2[:, :], d["L1_ffn_expert_b2"])
                for kt in range(2):
                    rows = slice(kt * P, (kt + 1) * P)
                    load(sp, g.w1[:, kt, 0:E * EH].rearrange("p (e h) -> p e h", h=EH),
                         d["L1_ffn_expert_w1"][:, rows, :].rearrange("e p h -> p e h"))
                    load(sp, g.w1s[:, kt, 0:EH], d["L1_ffn_shared_w1"][rows, :])
                load(sp, g.w2[:, :, :], d["L1_ffn_expert_w2"].rearrange("(q t) h c -> (t h) q c", t=2))
                load(sp, g.w2s[0:EH, 0:CTRL], d["L1_ffn_shared_w2"])
                load(sp, g.w2s[ONE:ONE + 1, 0:CTRL], row(d["L1_ffn_shared_b2"]))
                for q in range(PAIRS):
                    load(sp, g.b1[:, q:q + 1], d["L1_ffn_expert_b1"][2 * q:2 * q + 2, :].rearrange("t (h a) -> (t h) a", a=1))
                load(sp, g.b1s[0:EH, :], d["L1_ffn_shared_b1"].rearrange("(p a) -> p a", a=1))
                load(sp, g.w1s[:, 0, EH:ONE], d["L1_ffn_halt_w1"])
                load(sp, g.b1s[EH:ONE, :], d["L1_ffn_halt_b1"].rearrange("(p a) -> p a", a=1))
                load(sp, g.w2s[EH:ONE, CTRL:CTRL + 1], d["L1_ffn_halt_w2"])
                load(sp, g.w2s[ONE:ONE + 1, CTRL:CTRL + 1], row(d["L1_ffn_halt_b2"]))
                load(sp, g.rw1[:, :], d["L1_ffn_refine_w1"])
                load(sp, g.rw2[:, :, :], d["L1_ffn_refine_w2"].rearrange("(j p) c -> p j c", p=P))
                for j in range(2):
                    load(sp, g.rb1[:, j:j + 1], d["L1_ffn_refine_b1"][j * P:(j + 1) * P].rearrange("(p a) -> p a", a=1))
                load(sp, g.rb2[:, :], spread(d["L1_ffn_refine_b2"]))
                load(sp, g.iw[:, :], spread(d["L1_ffn_integration_weight"]))
                load(sp, g.mu[:, :], spread(d["L1_ffn_mu"]))
                sp.wait_ge(cut, 3)
                for n in range(3):
                    for s in range(2):
                        at = n * 2 * E + s * E
                        sp.dma_start(g.b2[at:at + E, s, :], part[:, n, :]).then_inc(placed, 16)
                sp.wait_ge(placed, 96)
                sp.wait_ge(loaded, 16 * len(loads))

            @block.vector
            def _(dve):
                nc.vector.memset(g.b2[:, :, :], 0.0).then_inc(order, 1)
                nc.vector.memset(g.w1s[:, :, :], 0.0).then_inc(order, 1)
                nc.vector.memset(g.w2s[:, :], 0.0).then_inc(order, 1)
                for u in range(2):
                    nc.vector.memset(g.hs[u][:, :], 1.0)
                nc.vector.tensor_copy(g.sel[:, :], k.c("sel")[0:2 * E, :])
                dve.wait_ge(loaded, 16 * len(loads))
                nc.vector.tensor_copy(part[:, 0, :], b2[:, :]).then_inc(cut, 1)
                dve.wait_ge(cut, 1)
                c = Chain(dve, order, 3)
                c.link(nc.vector.tensor_copy(back[:, :], part[:, 0, :]))
                c.link(nc.vector.tensor_tensor(rest[:, :], b2[:, :], back[:, :], ALU.subtract))
                nc.vector.tensor_copy(part[:, 1, :], rest[:, :]).then_inc(cut, 1)
                dve.wait_ge(cut, 2)
                c.link(nc.vector.tensor_copy(back[:, :], part[:, 1, :]))
                c.link(nc.vector.tensor_tensor(rest[:, :], rest[:, :], back[:, :], ALU.subtract))
                nc.vector.tensor_copy(part[:, 2, :], rest[:, :]).then_inc(cut, 1)
                dve.wait_ge(cut, 3)


def dynamics_phase(k, g, out):
    nc = k.nc
    ROUNDS = CHUNKS // 2
    Z = k.bank[0]
    HB = k.bank[1:3]
    MB = k.bank[3:5]
    CB = k.bank[5:8]
    Z_PER, H_PER, STEP_H = 10, 24, 5
    m = {n: k.sem(n) for n in (
        "oh_staged", "z_done", "z_read", "hid_done", "hid_ready", "mask_done", "masked", "ctrl_done",
        "ctrl_read", "absb_ready", "exp_ready", "ln_ready", "xm_ready", "state_ready", "order", "order_act",
        "halt_ready", "xx_ready", "out_ready", "ref_order")}
    stored = [k.sem(f"out_stored{u}") for u in range(2)]

    def z_index(i, what, u, n=0):
        return i * Z_PER + {"onehot": u, "it1": 2 + 2 * u + n, "refine": 6 + 2 * u + n}[what]

    def h_index(i, what, n):
        return i * H_PER + (n if what == "step" else 4 * STEP_H + n)

    with ExitStack() as ctx:
        def two(n, shape, dt=FP32):
            return [k.sb(ctx, f"{n}{u}", shape, dt) for u in range(2)]
        ohs = two("onehot_copies", [P, CT, P // (2 * E), 2 * E])
        ohT = two("ohT", [6 * E, SEQ], BF16)
        state, vel, xT, vT = two("state", [P, SEQ]), two("vel", [P, SEQ]), two("stateT", [P, SEQ]), two("velT", [P, SEQ])
        hp = two("pair_hidden", [P, SEQ])
        hm = two("masked_hidden", [P, 2, PAIRS, SEQ])
        tt = two("tanh_a_g", [P, 2, 3, SEQ])
        bb = two("ctrl_b", [P, 3, SEQ])
        xm = two("x_minus_mu", [P, SEQ])
        th = two("halt", [P, CT])
        xx = two("x_plus_xf", [P, SEQ])
        L = k.sb(ctx, "softplus", [P, 3, SEQ])
        s1 = k.sb(ctx, "sum_v", [P, SEQ])
        s2 = k.sb(ctx, "sum_g", [P, SEQ])

        def tiles(t):
            return t.rearrange("p (t c) -> p t c", c=P)

        def state_in(i, u, it):
            return tiles_of(g.xf, i * 2 + u) if it == 0 else tiles(state[u][:, :])

        STEPS = [(it, u) for it in range(2) for u in range(2)]

        def each_round(eng):
            return rounds(eng, ROUNDS)

        with nc.Block() as block:
            @block.sync
            def _(sp):
                @each_round(sp)
                def _(i):
                    for u in range(2):
                        to = out[bass.ds(i * 2 + u, 1), :, :].rearrange("s (t p) c -> p (s t) c", p=P)
                        sp.wait_ge(m["out_ready"], i * 2 + u + 1)
                        sp.dma_start(to, tiles(xx[u][:, :])).then_inc(stored[u], 16)
                for u in range(2):
                    sp.wait_ge(stored[u], 16 * ROUNDS)

            @block.gpsimd
            def _(pool):
                @each_round(pool)
                def _(i):
                    for u in range(2):
                        wait(pool, m["z_done"], z_index(i, "onehot", u) + 1 - Z_PER)
                        nc.gpsimd.tensor_copy(ohs[u][:, :, :, :], tiles_of(g.onehot, i * 2 + u).unsqueeze(2).to_broadcast(
                            [P, CT, P // (2 * E), 2 * E])).then_inc(m["oh_staged"], 1)
                    for it, u in STEPS:
                        o = i * 4 + it * 2 + u
                        wait(pool, m["state_ready"], o - 1)
                        nc.gpsimd.tensor_tensor(tiles(xm[u][:, :]), state_in(i, u, it),
                                                g.mu[:, :].unsqueeze(1).to_broadcast([P, CT, P]), ALU.subtract
                                                ).then_inc(m["xm_ready"], 1)
                    for u in range(2):
                        wait(pool, stored[u], i * 16)
                        nc.gpsimd.tensor_tensor(tiles(xx[u][:, :]), tiles_of(k.x, i * 2 + u), tiles_of(g.xf, i * 2 + u),
                                                ALU.add).then_inc(m["xx_ready"], 1)

            def masks_of(pe, o, q, u):
                for s in range(2):
                    wait(pe, m["masked"], o * 8 + q * 2 + s - 1)
                    nc.tensor.matmul(MB[s][:, :], g.sel[:, (s * PAIRS + q) * P:(s * PAIRS + q + 1) * P],
                                     ohT[u][0:2 * E, :], start=True, stop=True).then_inc(m["mask_done"], 1)

            @block.tensor
            def _(pe):
                def use_z(z):
                    wait(pe, m["z_read"], z)

                def transposed(z, src, ident=None):
                    use_z(z)
                    for j in range(CT):
                        last = nc.tensor.transpose(Z[:, j * P:(j + 1) * P], src[:, j * P:(j + 1) * P], k.ident)
                    last.then_inc(m["z_done"], 1)

                @each_round(pe)
                def _(i):
                    for u in range(2):
                        pe.wait_ge(m["oh_staged"], i * 2 + u + 1)
                        use_z(z_index(i, "onehot", u))
                        for j in range(CT):
                            last = nc.tensor.transpose(Z[:, j * P:(j + 1) * P],
                                                       ohs[u][:, j, :, :].rearrange("p n c -> p (n c)"), k.ident)
                        last.then_inc(m["z_done"], 1)
                    for it, u in STEPS:
                        o = i * 4 + it * 2 + u
                        if it == 0:
                            moving = [g.xfT[:, bass.ds((i * 2 + u) * SEQ, SEQ)]]
                        else:
                            pe.wait_ge(m["state_ready"], o - 1)
                            z = z_index(i, "it1", u)
                            transposed(z, state[u])
                            transposed(z + 1, vel[u])
                            pe.wait_ge(m["z_read"], z + 2)
                            moving = [xT[u][:, :], vT[u][:, :]]

                        def hidden(n, weights):
                            h = h_index(i, "step", (it * 2 + u) * STEP_H + n)
                            wait(pe, m["hid_ready"], h - 1)
                            for kt, x in enumerate(moving):
                                last = nc.tensor.matmul(HB[((it * 2 + u) * STEP_H + n) % 2][:, :], weights[:, kt, :], x,
                                                        start=kt == 0, stop=kt == len(moving) - 1)
                            last.then_inc(m["hid_done"], 1)

                        for q in range(PAIRS):
                            hidden(q, g.w1[:, :, q * P:(q + 1) * P])
                            if q >= 1:
                                masks_of(pe, o, q - 1, u)
                        hidden(4, g.w1s)
                        masks_of(pe, o, PAIRS - 1, u)
                        pe.wait_ge(m["hid_ready"], h_index(i, "step", (it * 2 + u) * STEP_H + STEP_H))
                        for t in range(CT):
                            cols = slice(t * P, (t + 1) * P)
                            for s in range(3):
                                n = o * 12 + t * 3 + s
                                wait(pe, m["ctrl_read"], n - 2)
                                if s == 0:
                                    last = nc.tensor.matmul(CB[s][:, 0:CTRL + 1], g.hs[u][:, cols], g.w2s[:, :],
                                                            start=True, stop=True)
                                else:
                                    nc.tensor.matmul(CB[s][:, 0:CTRL], ohT[u][:, cols], g.b2[:, s - 1, :],
                                                     start=True, stop=False)
                                    if t == 0 and s == 1:
                                        pe.wait_ge(m["masked"], o * 8 + 8)
                                    for q in range(PAIRS):
                                        last = nc.tensor.matmul(CB[s][:, 0:CTRL], hm[u][:, s - 1, q, cols],
                                                                g.w2[:, q, :], start=False, stop=q == PAIRS - 1)
                                last.then_inc(m["ctrl_done"], 1)
                    for u in range(2):
                        o = i * 4 + 2 + u
                        z = z_index(i, "refine", u)
                        pe.wait_ge(m["state_ready"], o + 1)
                        transposed(z, state[u])
                        pe.wait_ge(m["z_read"], z + 1)
                        for j in range(2):
                            h = h_index(i, "refine", 2 * u + j)
                            wait(pe, m["hid_ready"], h - 1)
                            nc.tensor.matmul(HB[j][:, :], g.rw1[:, j * P:(j + 1) * P], xT[u][:, :], start=True, stop=True
                                             ).then_inc(m["hid_done"], 1)
                        pe.wait_ge(m["hid_ready"], h_index(i, "refine", 2 * u + 2))
                        for t in range(CT):
                            for j in range(2):
                                last = nc.tensor.matmul(Z[:, t * P:(t + 1) * P], hm[u][:, 0, j, t * P:(t + 1) * P],
                                                        g.rw2[:, j, :], start=j == 0, stop=j == 1)
                        last.then_inc(m["z_done"], 1)

            @block.scalar
            def _(act):
                def read_z(z, to, of=Z[:, :]):
                    act.wait_ge(m["z_done"], z + 1)
                    nc.scalar.copy(to, of).then_inc(m["z_read"], 1)

                def softplus(o, u):
                    act.wait_ge(m["absb_ready"], o + 1)
                    nc.scalar.activation(L[:, :, :], L[:, :, :], ACT.Exp).then_inc(m["exp_ready"], 1)
                    act.wait_ge(m["exp_ready"], o + 1)
                    nc.scalar.activation(L[:, :, :], L[:, :, :], ACT.Ln, bias=1.0).then_inc(m["ln_ready"], 1)

                @each_round(act)
                def _(i):
                    for u in range(2):
                        z = z_index(i, "onehot", u)
                        act.wait_ge(m["z_done"], z + 1)
                        nc.scalar.copy(ohT[u][:, :], Z[0:6 * E, :]).then_inc(m["z_read"], 1)
                    for it, u in STEPS:
                        o = i * 4 + it * 2 + u
                        if it == 1:
                            z = z_index(i, "it1", u)
                            read_z(z, xT[u][:, :])
                            read_z(z + 1, vT[u][:, :])

                        def gelu(n, to, rows, bias):
                            act.wait_ge(m["hid_done"], h_index(i, "step", (it * 2 + u) * STEP_H + n) + 1)
                            nc.scalar.activation(to, HB[((it * 2 + u) * STEP_H + n) % 2][0:rows, :], ACT.Gelu, bias=bias).then_inc(m["hid_ready"], 1)

                        for q in range(PAIRS):
                            wait(act, m["masked"], o * 8 + 2 * (q - 1))
                            gelu(q, hp[q % 2][:, :], P, g.b1[:, q:q + 1])
                        gelu(4, g.hs[u][0:ONE, :], ONE, g.b1s[:, 0:1])
                        if (it, u) != STEPS[0]:
                            softplus(o - 1, 1 - u)
                        for t in range(CT):
                            cols = slice(t * P, (t + 1) * P)
                            for s in range(3):
                                n = o * 12 + t * 3 + s
                                act.wait_ge(m["ctrl_done"], n + 1)
                                if t == 0 and s == 0:
                                    wait(act, m["state_ready"], o - 1)
                                if s == 0:
                                    nc.scalar.activation(th[u][:, t:t + 1], CB[s][:, CTRL:CTRL + 1], ACT.Tanh, scale=0.5)
                                nc.scalar.activation(tt[u][:, :, s, cols], CB[s][:, 0:CTRL].rearrange("p (n c) -> p n c", c=P)[:, 0:3:2, :],
                                                     ACT.Tanh, scale=0.5)
                                nc.scalar.copy(bb[u][:, s, cols], CB[s][:, P:2 * P]).then_inc(m["ctrl_read"], 1)
                    softplus(i * 4 + 3, 1)
                    for u in range(2):
                        z = z_index(i, "refine", u)
                        read_z(z, xT[u][:, :])
                        for j in range(2):
                            act.wait_ge(m["hid_done"], h_index(i, "refine", 2 * u + j) + 1)
                            nc.scalar.activation(hm[u][:, 0, j, :], HB[j][:, :], ACT.Gelu, bias=g.rb1[:, j:j + 1]
                                                 ).then_inc(m["hid_ready"], 1)

            @block.vector
            def _(dve):
                LINKS = {0: 6, 1: 8}
                PER = 2 * (LINKS[0] + LINKS[1])

                def abs_b(o, u):
                    dve.wait_ge(m["ctrl_read"], o * 12 + 12)
                    wait(dve, m["state_ready"], o)
                    nc.vector.scalar_tensor_tensor(out=L[:, :, :], in0=bb[u][:, :, :], scalar=-1.0, in1=bb[u][:, :, :],
                                                   op0=ALU.mult, op1=ALU.min).then_inc(m["absb_ready"], 1)

                def mask(o, u, hid_base):
                    for q in range(PAIRS):
                        for s in range(2):
                            dve.wait_ge(m["mask_done"], o * 8 + q * 2 + s + 1)
                            if s == 0:
                                dve.wait_ge(m["hid_ready"], hid_base + q + 1)
                            mul(nc, hm[u][:, s, q, :], hp[q % 2][:, :], MB[s][:, :]).then_inc(m["masked"], 1)

                def integrate(i, it, u):
                    o = i * 4 + it * 2 + u
                    c = Chain(dve, m["order"], i * PER + it * 2 * LINKS[0] + u * LINKS[it])
                    a, gg = tt[u][:, 0, :, :], tt[u][:, 1, :, :]
                    weight = g.weight[:, :, bass.ds((i * 2 + u) * CT, CT)].unsqueeze(3).to_broadcast([P, 3, CT, P])

                    def sets(t):
                        return t.rearrange("p s (t c) -> p s t c", c=P)

                    def over_sets(t):
                        return t.unsqueeze(1).to_broadcast([P, 3, SEQ])
                    dve.wait_ge(m["ln_ready"], o + 1)
                    c.link(nc.vector.scalar_tensor_tensor(out=L[:, :, :], in0=bb[u][:, :, :], scalar=0.0, in1=L[:, :, :],
                                                          op0=ALU.max, op1=ALU.add))
                    dve.wait_ge(m["xm_ready"], o + 1)
                    if it == 1:
                        c.mark(nc.vector.scalar_tensor_tensor(out=a, in0=a, scalar=1.0, in1=over_sets(vel[u][:, :]),
                                                              op0=ALU.add, op1=ALU.mult))
                    c.link(mul(nc, L[:, :, :], L[:, :, :], over_sets(xm[u][:, :])))
                    if it == 1:
                        c.link(nc.vector.scalar_tensor_tensor(out=L[:, :, :], in0=L[:, :, :], scalar=-2.0, in1=a,
                                                              op0=ALU.mult, op1=ALU.add))
                    c.link(mul(nc, sets(L[:, :, :]), sets(L[:, :, :]), weight))
                    c.link(nc.vector.scalar_tensor_tensor(out=gg, in0=gg, scalar=1.0, in1=L[:, :, :],
                                                          op0=ALU.add, op1=ALU.mult))
                    factor = -1.0 if it == 0 else 0.5
                    c.link(nc.vector.tensor_tensor(s2[:, :], gg[:, 0, :], gg[:, 1, :], ALU.add))
                    if it == 0:
                        nc.vector.tensor_tensor(s1[:, :], L[:, 0, :], L[:, 1, :], ALU.add)
                    c.link(nc.vector.tensor_scalar(th[u][:, :], th[u][:, :], 0.5, 0.5, ALU.mult, ALU.add))
                    nc.vector.tensor_tensor(s2[:, :], s2[:, :], gg[:, 2, :], ALU.add).then_inc(m["ref_order"], 1)
                    halt = th[u][:, :].unsqueeze(2).to_broadcast([P, CT, P])
                    if it == 0:
                        nc.vector.tensor_tensor(s1[:, :], s1[:, :], L[:, 2, :], ALU.add).then_inc(m["ref_order"], 1)
                    n_ref = (i * 12 + u * 4) if it == 0 else (i * 12 + 8 + u * 2)
                    dve.wait_ge(m["ref_order"], n_ref + (2 if it == 0 else 1))
                    mul(nc, tiles(s2[:, :]), tiles(s2[:, :]), halt).then_inc(m["ref_order"], 1)
                    if it == 0:
                        nc.vector.scalar_tensor_tensor(out=tiles(vel[u][:, :]), in0=tiles(s1[:, :]), scalar=factor,
                                                       in1=halt, op0=ALU.mult, op1=ALU.mult).then_inc(m["ref_order"], 1)
                    dve.wait_ge(m["ref_order"], n_ref + (4 if it == 0 else 2))
                    nc.vector.scalar_tensor_tensor(out=tiles(state[u][:, :]), in0=tiles(s2[:, :]), scalar=factor * DT / 2,
                                                   in1=state_in(i, u, it), op0=ALU.mult, op1=ALU.add
                                                   ).then_inc(m["state_ready"], 1)
                    assert c.n == LINKS[it], (it, c.n)

                @each_round(dve)
                def _(i):
                    for n, (it, u) in enumerate(STEPS):
                        o = i * 4 + n
                        if n:
                            abs_b(o - 1, 1 - u)
                        mask(o, u, h_index(i, "step", n * STEP_H))
                        if n:
                            integrate(i, *STEPS[n - 1])
                    abs_b(i * 4 + 3, 1)
                    integrate(i, *STEPS[3])
                    for u in range(2):
                        t = i * 2 + u
                        dve.wait_ge(m["z_done"], z_index(i, "refine", u, 1) + 1)
                        dve.wait_ge(m["xx_ready"], t + 1)
                        wait(dve, m["out_ready"], t)
                        nc.vector.tensor_tensor(tiles(s1[:, :]), tiles(Z[:, :]), g.rb2[:, :].unsqueeze(1).to_broadcast([P, CT, P]),
                                                ALU.add).then_inc(m["z_read"], 1)
                        dve.wait_ge(m["z_read"], z_index(i, "refine", u, 1) + 1)
                        mul(nc, tiles(s1[:, :]), tiles(s1[:, :]), g.iw[:, :].unsqueeze(1).to_broadcast([P, CT, P])
                            ).then_inc(m["order_act"], 1)
                        dve.wait_ge(m["order_act"], t + 1)
                        nc.vector.tensor_tensor(xx[u][:, :], xx[u][:, :], s1[:, :], ALU.add).then_inc(m["out_ready"], 1)


def emit(nc, dram, cols, out):
    with ExitStack() as ctx:
        k = Core(nc, ctx, dram)
        k.x = k.sb(ctx, "x_res", [P, TILES, P])
        k.const = k.sb(ctx, "const_sb", list(dram["const"].shape))
        k.zeros = k.sb(ctx, "zeros", [P, 512], BF16)
        k.mean = k.sb(ctx, "mean", [P, TILES])
        k.rstd = k.sb(ctx, "rstd", [P, TILES])

        def const(name):
            a, b = cols[name]
            return k.const[:, a:b]

        k.c = const
        k.ident = const("ident")
        s = lambda: None
        f = lambda: None
        f.sorted_in = nc.dram_tensor("sorted_in", (PADDED * P, P), FP32, kind="Internal").ap()
        load_phase(k, f.sorted_in)
        statistics_phase(k, "ln1", k.x)
        with ExitStack() as ttt:
            k.kT = k.sb(ttt, "kT", [P, TOKENS])
            k.qT = k.sb(ttt, "qT", [P, TOKENS])
            k.vT = k.sb(ttt, "vT", [P, TOKENS])
            k.ktok = k.sb(ttt, "ktok", [P, TILES, P])
            k.theta_gate = k.sb(ttt, "theta_gate", [P, HID])
            k.theta_val = k.sb(ttt, "theta_val", [P, HID])
            k.theta_proj = k.sb(ttt, "theta_proj", [P, HT, P])
            k.theta_projT = k.sb(ttt, "theta_projT", [P, HID])
            s.theta_loaded, s.scaled = k.sem("theta_loaded"), k.sem("qk_scaled")
            qkv_phase(k, s)
            transpose_proj_phase(k)
            gradient_phase(k, "grad1")
            muon_phase(k, "muon1")
            gradient_phase(k, "grad2")
            muon_phase(k, "muon2")
            query_phase(k)
        k.clear_semaphores()
        f.sorted_out = nc.dram_tensor("sorted_out", (PADDED * P, P), FP32, kind="Internal").ap()
        with ExitStack() as moe:
            f.xl = k.sb(moe, "xl", [P, TILES, P])
            f.xhat = k.sb(moe, "xhat", [P, TILES, P])
            f.w1 = k.sb(moe, "w1T", [P, E, HID])
            f.w2 = k.sb(moe, "w2T", [P, E, HID])
            f.b1 = k.sb(moe, "b1_spread", [P, E, HID])
            f.b2 = k.sb(moe, "b2_spread", [P, E, P])
            f.vecT = k.sb(moe, "centroids_g_b_T", [P, 3 * E])
            f.alpha = k.sb(moe, "alpha", [P, TILES])
            f.slot_expert = k.sb(moe, "slot_expert", [P, PADDED], I32)
            f.pos = k.sb(moe, "pos", [P, TILES], U32)
            expert_weights_phase(k, f)
            statistics_phase(k, "ln2", k.x)
            affinity_phase(k, f)
            statistics_phase(k, "ln2b", f.xl)
            sort_phase(k, f)
            experts_phase(k, f)
            combine_phase(k, f)
        statistics_phase(k, "ln3", k.x)
        diagonal_attention_phase(k)
        statistics_phase(k, "ln4", k.x)
        k.clear_semaphores()
        g = lambda: None
        with ExitStack() as dyn:
            g.xf = k.sb(dyn, "xf", [P, TILES, P])
            g.xfT = k.sb(dyn, "xfT", [P, TOKENS])
            g.onehot = k.sb(dyn, "slot_onehot", [P, TILES, 2 * E])
            g.weight = k.sb(dyn, "control_weight", [P, 3, TILES])
            router_phase(k, g)
            g.w1 = k.sb(dyn, "dyn_w1", [P, 2, E * EH])
            g.w1s = k.sb(dyn, "dyn_w1_shared_halt", [P, 2, P])
            g.w2 = k.sb(dyn, "dyn_w2", [P, PAIRS, CTRL])
            g.w2s = k.sb(dyn, "dyn_w2_shared_halt", [ONE + 1, CTRL + 1])
            g.b1 = k.sb(dyn, "dyn_b1", [P, PAIRS])
            g.b1s = k.sb(dyn, "dyn_b1_shared_halt", [ONE, 1])
            g.b2 = k.sb(dyn, "dyn_b2", [6 * E, 2, CTRL], BF16)
            g.sel = k.sb(dyn, "pair_rows", [2 * E, 2 * PAIRS * P], BF16)
            g.hs = [k.sb(dyn, f"shared_halt_hidden{u}", [ONE + 1, SEQ]) for u in range(2)]
            g.rw1 = k.sb(dyn, "refine_w1", [P, 2 * P])
            g.rw2 = k.sb(dyn, "refine_w2", [P, 2, P])
            g.rb1 = k.sb(dyn, "refine_b1", [P, 2])
            g.rb2 = k.sb(dyn, "refine_b2", [P, P])
            g.iw = k.sb(dyn, "integration_weight", [P, P])
            g.mu = k.sb(dyn, "mu", [P, P])
            dynamics_weights_phase(k, g)
            dynamics_phase(k, g, out)


def kernel(**inputs):
    import concourse.bacc as _bacc
    from concourse.bass_utils import run_bass_kernel_spmd as _run

    nc = _bacc.Bacc("TRN2", target_bir_lowering=False, num_devices=1)
    const, cols = constant_columns()
    arrays = {name: np.ascontiguousarray(a) for name, a in inputs.items()}
    arrays["const"] = const
    dram = {n: nc.dram_tensor(n, a.shape if a.ndim else (1,), mybir.dt.from_np(a.dtype), kind="ExternalInput").ap()
            for n, a in arrays.items()}
    arrays = {n: a.reshape(a.shape or (1,)) for n, a in arrays.items()}
    out = nc.dram_tensor("out", (SEQS, SEQ, P), FP32, kind="ExternalOutput").ap()
    emit(nc, dram, cols, out)
    r = _run(nc, [arrays], core_ids=[0])
    return r.results[0]["out"]
```

```python
from contextlib import ExitStack

import concourse.bass as bass
import numpy as np
from concourse import mybir

FP32 = mybir.dt.float32
BF16 = mybir.dt.bfloat16
I32 = mybir.dt.int32
U32 = mybir.dt.uint32
ALU = mybir.AluOpType
ACT = mybir.ActivationFunctionType
AXX = mybir.AxisListType.X

P = 128
SEQS, SEQ = 8, 512
TOKENS = SEQS * SEQ
TILES = TOKENS // P
CT = SEQ // P
CHUNKS = TOKENS // SEQ
HEADS, HD = 16, 8
LN_EPS = 1e-5
HID = 512
HT = HID // P
E = 8
PADDED = TILES + E - 1
NS_A, NS_B, NS_C = 3.4445, -4.775, 2.0315
NS_ITERS, LR = 5, 0.1
GRAD_SCALE = 2.0 / (TOKENS * P)
EH = 64
PAIRS = E // 2
CTRL = 3 * P
RH = 32
DT = 0.1
ONE = EH + RH


def constant_columns():
    row = np.arange(P)[:, None]
    col = np.arange(P)[None, :]
    sel = np.zeros((P, 2 * PAIRS, P))
    for k in range(2):
        for q in range(PAIRS):
            sel[k * E + 2 * q, k * PAIRS + q, :EH] = 1
            sel[k * E + 2 * q + 1, k * PAIRS + q, EH:] = 1
    starts = np.ones((P, E, TILES))
    starts[:, :, 0] = 0
    parts = {
        "ident": row == col,
        "before": row < col,
        "ones": np.ones((P, P)),
        "headmask": row // HD == col // HD,
        "headtile": (row == col % HD),
        "sel": sel.reshape(P, -1),
        "starts": starts.reshape(P, -1),
        "rank8": np.tile(E - np.arange(E), (P, 1)),
        "tilestart": np.tile(P * np.arange(TILES), (P, 1)),
        "slot": np.tile(np.arange(PADDED), (P, 1)),
    }
    at, cols, out = 0, {}, []
    for name, a in parts.items():
        a = np.asarray(a, np.float32)
        cols[name] = (at, at + a.shape[1])
        at += a.shape[1]
        out.append(a)
    return np.ascontiguousarray(np.concatenate(out, 1)), cols


class Chain:

    def __init__(self, eng, sem, base=0):
        self.eng, self.sem, self.base, self.n = eng, sem, base, 0

    def mark(self, ins):
        ins.then_inc(self.sem, 1)
        self.n += 1
        return self.base + self.n

    def link(self, ins):
        self.eng.wait_ge(self.sem, self.mark(ins))


def wait(eng, sem, n):
    if not (isinstance(n, int) and n <= 0):
        eng.wait_ge(sem, n)


def rounds(eng, n):
    def run(body):
        body(0)
        with eng.Fori(1, n) as i:
            body(i)
    return run


class Core:

    def __init__(self, nc, ctx, dram):
        self.nc, self.dram, self.sems = nc, dram, []
        self.bank = [ctx.enter_context(nc.psum_tensor(f"bank{i}", [P, 512], FP32)) for i in range(8)]

    def sb(self, ctx, name, shape, dt=FP32):
        return ctx.enter_context(self.nc.sbuf_tensor(name, shape, dt))

    def sem(self, name):
        self.sems.append(self.nc.alloc_semaphore(name=name))
        return self.sems[-1]

    def clear_semaphores(self):
        self.nc.clear_and_free_semaphores(self.sems)
        self.nc.all_engine_barrier()
        self.sems = []


def mul(nc, out, a, b):
    return nc.vector.tensor_tensor(out, a, b, ALU.mult)


def row(ap):
    return ap.rearrange("(a n) -> a n", a=1)


def spread(ap, n=P):
    return row(ap).to_broadcast([n, ap.shape[0]])


def load_phase(k, clear):
    nc, d = k.nc, k.dram
    loaded, ready, cleared = k.sem("x_loaded"), k.sem("zeros_ready"), k.sem("sorted_cleared")
    R = 13
    assert PADDED % R == 0
    with ExitStack() as ctx, nc.Block() as block:
        blank = k.sb(ctx, "blank", [P, R * P])

        @block.sync
        def _(sp):
            sp.dma_start(k.const[:, :], d["const"]).then_inc(loaded, 16)
            for c in range(CHUNKS):
                sp.dma_start(k.x[:, c * CT:(c + 1) * CT, :], d["L0_attn_x"][c, :, :].rearrange("(t p) c -> p t c", p=P)
                             ).then_inc(loaded, 16)
            sp.wait_ge(ready, 2)
            for t in range(0, PADDED, R):
                sp.dma_start(clear[t * P:(t + R) * P, :].rearrange("(p a) c -> p (a c)", p=P), blank[:, :]
                             ).then_inc(cleared, 16)
            sp.wait_ge(loaded, 16 * (CHUNKS + 1))
            sp.wait_ge(cleared, 16 * (PADDED // R))

        @block.vector
        def _(dve):
            dve.memset(blank[:, :], 0.0).then_inc(ready, 1)
            dve.memset(k.zeros[:, :], 0.0).then_inc(ready, 1)
            dve.wait_ge(ready, 2)


def count_tile(nc, st, src, t):
    return nc.vector.bn_stats(st[:, bass.ds(t, 1), :].rearrange("p a s -> p (a s)"),
                              src[:, bass.ds(t, 1), :].rearrange("p a c -> p (a c)"))


def statistics_phase(k, name, mean, rstd, st, src=None):
    nc = k.nc
    counted, order = k.sem(f"{name}_rows_counted"), k.sem(f"{name}_order")
    var_ready, std_ready = k.sem(f"{name}_var_ready"), k.sem(f"{name}_std_ready")
    n = mean.shape[1]
    group = n // CHUNKS if n % CHUNKS == 0 else 13
    assert n % group == 0
    with ExitStack() as ctx:
        tmp = k.sb(ctx, f"{name}_tmp", [P, 4, n])
        diff, var, std, fix = (tmp[:, m, :] for m in range(4))
        with nc.Block() as block:
            @block.vector
            def _(dve):
                if src is not None:
                    @rounds(dve, n // group)
                    def _(i):
                        for j in range(group):
                            count_tile(nc, st, src, i * group + j).then_inc(counted, 1)
                    wait(dve, counted, n)
                c = Chain(dve, order)
                c.mark(nc.vector.tensor_tensor(mean, st[:, :, 1], st[:, :, 4], ALU.add))
                c.mark(nc.vector.tensor_tensor(diff, st[:, :, 1], st[:, :, 4], ALU.subtract))
                c.link(nc.vector.tensor_tensor(var, st[:, :, 2], st[:, :, 5], ALU.add))
                c.mark(nc.vector.tensor_scalar(mean, mean, 0.5, None, ALU.mult))
                c.mark(mul(nc, diff, diff, diff))
                c.link(nc.vector.tensor_scalar(var, var, 1.0 / P, LN_EPS, ALU.mult, ALU.add))
                nc.vector.scalar_tensor_tensor(out=var, in0=diff, scalar=0.25, in1=var,
                                               op0=ALU.mult, op1=ALU.add).then_inc(var_ready, 1)
                wait(dve, std_ready, 1)
                c.link(nc.vector.reciprocal(rstd, std))
                c.link(mul(nc, fix, rstd, rstd))
                c.link(mul(nc, fix, fix, var))
                c.link(nc.vector.tensor_scalar(fix, fix, -0.5, 1.5, ALU.mult, ALU.add))
                c.link(mul(nc, rstd, rstd, fix))

            @block.scalar
            def _(act):
                wait(act, var_ready, 1)
                nc.scalar.activation(std, var, ACT.Sqrt).then_inc(std_ready, 1)
                wait(act, std_ready, 1)


def tiles_of(t, i, n=CT):
    return t[:, bass.ds(i * n, n), :]


def per_token(t, i, width=P):
    return t[:, bass.ds(i * CT, CT)].unsqueeze(2).to_broadcast([P, CT, width])


def qkv_phase(k):
    nc, d = k.nc, k.dram
    W_LOADS = 8
    loaded, order_p, theta_loaded = k.sem("qkv_w_loaded"), k.sem("qkv_pool_order"), k.sem("theta_loaded")
    xn_ready, xn_transposed, xT_copied = k.sem("xn_ready"), k.sem("xn_transposed"), k.sem("xT_copied")
    qk_done, v_done, v_copied = k.sem("qk_done"), k.sem("v_done"), k.sem("v_copied")
    qk_copied, squared, ss_ready, norm_ready = k.sem("qk_copied"), k.sem("qk_squared"), k.sem("ss_ready"), k.sem("norm_ready")
    unit_ready, unit_transposed, ktok_ready = k.sem("unit_ready"), k.sem("unit_transposed"), k.sem("ktok_ready")
    qT_copied, kT_copied, order_v = k.sem("qT_copied"), k.sem("kT_copied"), k.sem("qkv_dve_order")
    head_done, head_copied = k.sem("head_vectors_done"), k.sem("head_vectors_copied")
    G = CT * 2 * HEADS
    with ExitStack() as ctx:
        w = k.sb(ctx, "qkv_w_sb", [P, 3 * P])
        bqk = k.sb(ctx, "qk_bias", [P, 2 * P])
        bv = k.sb(ctx, "v_bias", [P, 1])
        kh = k.sb(ctx, "k_scale_bias", [P, 2, HD])
        hv = k.sb(ctx, "head_vectors", [HD, 4])
        hc = k.sb(ctx, "head_vectors_by_channel", [P, 4])
        xc = k.sb(ctx, "xc", [P, CT, P])
        xn = k.sb(ctx, "xn_chunk", [P, CT, P])
        xT = k.sb(ctx, "xT_chunk", [P, SEQ])
        qk = k.sb(ctx, "qk_chunk", [P, CT, 2 * P])
        sq = k.sb(ctx, "qk_squares", [P, CT * 2 * P])
        ss = k.sb(ctx, "qk_ss", [P, G])
        nrm = k.sb(ctx, "qk_norm", [P, G])
        inv = k.sb(ctx, "qk_inv", [P, G])
        unit = k.sb(ctx, "qk_unit", [P, CT, 2 * P])
        ks = k.sb(ctx, "k_scaled", [P, CT, P])

        def flat(t):
            return t.rearrange("p t c -> p (t c)")

        def heads(t):
            return t.rearrange("p (g e) -> p g e", e=HD)

        def by_head(t):
            return t.rearrange("p t (h e) -> p t h e", e=HD)

        def k_vector(n):
            return kh[:, n:n + 1, :].unsqueeze(1).to_broadcast([P, CT, HEADS, HD])

        def pipelined(eng, front, back):
            front(0)
            front(1)
            back(0)
            with eng.Fori(2, CHUNKS) as i:
                front(i)
                back(i - 1)
            back(CHUNKS - 1)

        with nc.Block() as block:
            @block.sync
            def _(sp):
                sp.dma_start(w[:, :], d["L0_attn_qkv_w"]).then_inc(loaded, 16)
                sp.dma_start(bqk[:, :], spread(d["L0_attn_qkv_b"][0:2 * P])).then_inc(loaded, 16)
                sp.dma_start(bv[:, :], d["L0_attn_qkv_b"][2 * P:3 * P].rearrange("(p a) -> p a", a=1)).then_inc(loaded, 16)
                for n, name in enumerate(("qn_scale", "kn_scale", "qn_bias", "kn_bias")):
                    sp.dma_start(hv[:, n:n + 1], d["L0_attn_" + name].rearrange("(p a) -> p a", a=1)).then_inc(loaded, 16)
                sp.dma_start(kh[:, 0, :], spread(d["L0_attn_kn_scale"])).then_inc(loaded, 16)
                sp.dma_start(kh[:, 1, :], spread(d["L0_attn_kn_bias"])).then_inc(loaded, 16)
                sp.dma_start(k.theta_gate[:, :], d["L0_attn_ttt_gate"]).then_inc(theta_loaded, 16)
                sp.dma_start(k.theta_val[:, :], d["L0_attn_ttt_val"]).then_inc(theta_loaded, 16)
                sp.dma_start(k.theta_proj[:, :, :], d["L0_attn_ttt_proj"].rearrange("(j p) c -> p j c", p=P)
                             ).then_inc(theta_loaded, 16)
                wait(sp, theta_loaded, 48)

            @block.gpsimd
            def _(pool):
                def front(i):
                    wait(pool, xn_ready, i)
                    nc.gpsimd.tensor_tensor(xc[:, :, :], tiles_of(k.x, i), per_token(k.mean, i), ALU.subtract
                                            ).then_inc(order_p, 1)
                    wait(pool, order_p, i + 1 if isinstance(i, int) else 2 * i)
                    wait(pool, xn_transposed, i)
                    nc.gpsimd.tensor_tensor(xn[:, :, :], xc[:, :, :], per_token(k.rstd, i), ALU.mult
                                            ).then_inc(xn_ready, 1)

                def back(i):
                    wait(pool, unit_ready, i + 1)
                    wait(pool, ktok_ready, i)
                    nc.gpsimd.tensor_tensor(by_head(ks[:, :, :]), by_head(unit[:, :, P:2 * P]), k_vector(0), ALU.mult
                                            ).then_inc(order_p, 1)
                    wait(pool, order_p, 2 * CHUNKS if isinstance(i, int) and i == CHUNKS - 1 else 2 * i + 3)
                    nc.gpsimd.tensor_tensor(by_head(tiles_of(k.ktok, i)), by_head(ks[:, :, :]), k_vector(1), ALU.add
                                            ).then_inc(ktok_ready, 1)

                wait(pool, loaded, 16 * (W_LOADS + 1))
                pipelined(pool, front, back)

            @block.tensor
            def _(pe):
                def front(i):
                    wait(pe, xn_ready, i + 1)
                    wait(pe, xT_copied, i)
                    for j in range(CT):
                        last = nc.tensor.transpose(k.bank[0][:, j * P:(j + 1) * P], xn[:, j, :], k.ident)
                    last.then_inc(xn_transposed, 1)
                    wait(pe, xT_copied, i + 1)
                    wait(pe, qk_copied, 2 * i)
                    for j in range(CT):
                        last = nc.tensor.matmul(k.bank[1 + j // 2][:, (j % 2) * 2 * P:(j % 2 + 1) * 2 * P],
                                                xT[:, j * P:(j + 1) * P], w[:, 0:2 * P], start=True, stop=True)
                        if j % 2:
                            last.then_inc(qk_done, 1)
                    wait(pe, v_copied, i)
                    nc.tensor.matmul(k.bank[3][:, :], w[:, 2 * P:3 * P], xT[:, :], start=True, stop=True).then_inc(v_done, 1)

                def back(i):
                    wait(pe, unit_ready, i + 1)
                    for n, copied in ((0, qT_copied), (1, kT_copied)):
                        wait(pe, copied, i)
                        for j in range(CT):
                            last = nc.tensor.transpose(k.bank[4 + n][:, j * P:(j + 1) * P],
                                                       unit[:, j, n * P:(n + 1) * P], k.ident)
                        last.then_inc(unit_transposed, 1)

                wait(pe, loaded, 16 * (W_LOADS + 1))
                nc.tensor.matmul(k.bank[6][:, 0:4], k.c("headtile")[0:HD, :], hv[:, :], start=True, stop=True
                                 ).then_inc(head_done, 1)
                pipelined(pe, front, back)
                wait(pe, theta_loaded, 48)
                for j in range(HT):
                    last = nc.tensor.transpose(k.bank[7][:, j * P:(j + 1) * P], k.theta_proj[:, j, :], k.ident)
                last.then_inc(head_done, 1)

            @block.scalar
            def _(act):
                def front(i):
                    wait(act, xn_transposed, i + 1)
                    wait(act, v_done, i)
                    nc.scalar.copy(xT[:, :], k.bank[0][:, :]).then_inc(xT_copied, 1)
                    wait(act, v_done, i + 1)
                    nc.scalar.activation(k.vT[:, bass.ds(i * SEQ, SEQ)], k.bank[3][:, :], ACT.Identity,
                                         bias=bv[:, 0:1]).then_inc(v_copied, 1)
                    wait(act, qk_copied, 2 * i + 2)
                    wait(act, ss_ready, i)
                    nc.scalar.activation(sq[:, :], flat(qk[:, :, :]), ACT.Square).then_inc(squared, 1)
                    wait(act, ss_ready, i + 1)
                    nc.scalar.activation(nrm[:, :], ss[:, :], ACT.Sqrt).then_inc(norm_ready, 1)

                def back(i):
                    for n, to, copied in ((0, k.qT, qT_copied), (1, k.kT, kT_copied)):
                        wait(act, unit_transposed, 2 * i + n + 1)
                        nc.scalar.activation(to[:, bass.ds(i * SEQ, SEQ)], k.bank[4 + n][:, :], ACT.Identity,
                                             scale=hc[:, n:n + 1], bias=hc[:, n + 2:n + 3]).then_inc(copied, 1)

                wait(act, loaded, 16 * (W_LOADS + 1))
                wait(act, head_done, 1)
                nc.scalar.copy(hc[:, :], k.bank[6][:, 0:4]).then_inc(head_copied, 1)
                wait(act, head_copied, 1)
                pipelined(act, front, back)
                wait(act, head_done, 2)
                nc.scalar.copy(k.theta_projT[:, :], k.bank[7][:, :]).then_inc(head_copied, 1)
                wait(act, head_copied, 2)

            @block.vector
            def _(dve):
                wait(dve, loaded, 16 * (W_LOADS + 1))
                LINKS = 6

                @rounds(dve, CHUNKS)
                def _(i):
                    c = Chain(dve, order_v, i * LINKS)
                    wait(dve, unit_ready, i)
                    for h in range(2):
                        wait(dve, qk_done, 2 * i + h + 1)
                        nc.vector.tensor_tensor(qk[:, 2 * h:2 * h + 2, :],
                                                k.bank[1 + h][:, :].rearrange("p (j c) -> p j c", j=2),
                                                bqk[:, :].unsqueeze(1).to_broadcast([P, 2, 2 * P]), ALU.add
                                                ).then_inc(qk_copied, 1)
                    wait(dve, squared, i + 1)
                    nc.vector.tensor_reduce(ss[:, :], heads(sq[:, :]), AXX, ALU.add).then_inc(ss_ready, 1)
                    wait(dve, norm_ready, i + 1)
                    c.link(nc.vector.tensor_scalar(inv[:, :], nrm[:, :], 1e-30, None, ALU.max))
                    c.link(nc.vector.reciprocal(inv[:, :], inv[:, :]))
                    c.link(mul(nc, inv[:, :], inv[:, :], ss[:, :]))
                    c.link(nc.vector.tensor_tensor(inv[:, :], inv[:, :], nrm[:, :], ALU.add))
                    c.link(nc.vector.tensor_scalar(inv[:, :], inv[:, :], 0.5, 1e-6, ALU.mult, ALU.add))
                    c.link(nc.vector.reciprocal(inv[:, :], inv[:, :]))
                    assert c.n == LINKS
                    wait(dve, unit_transposed, 2 * i)
                    wait(dve, ktok_ready, i)
                    mul(nc, heads(flat(unit[:, :, :])), heads(flat(qk[:, :, :])),
                        inv[:, :].unsqueeze(2).to_broadcast([P, G, HD])).then_inc(unit_ready, 1)


def gradient_phase(k, name):
    nc = k.nc
    m = {n: k.sem(f"{name}_{n}") for n in (
        "kT_loaded0", "kT_loaded1", "k_loaded0", "k_loaded1", "G_done", "V_done", "sig_ready", "V_copied",
        "s_ready", "h_ready", "dact_ready", "hT_done", "hT_copied", "pred_done", "rT_ready", "r_done",
        "r_copied", "dh_done", "dproj_added", "dval_in_ready", "dgate_in_ready", "dgate_added", "order",
        "closed")}
    G_BANK, V_BANK, HT_BANK, R_BANK, DH_BANK, PROJ_BANK, VAL_BANK, GATE_BANK = k.bank
    PAIR_LOOPS = TILES // 2 - 1
    with ExitStack() as ctx:
        def two(n, shape):
            return [k.sb(ctx, f"{name}_{n}{a}", shape) for a in range(2)]
        kT, kt = two("kT", [P, P]), two("k", [P, P])
        sig, s, h, hv, dact = (two(n, [P, HID]) for n in ("sig", "s", "h", "hv", "dact"))
        hT = k.sb(ctx, f"{name}_hT", [P, HID])
        rT = k.sb(ctx, f"{name}_rT", [P, P])
        r = k.sb(ctx, f"{name}_r", [P, P])
        dval_in = k.sb(ctx, f"{name}_dval_in", [P, HID])
        dgate_in = k.sb(ctx, f"{name}_dgate_in", [P, HID])
        u = k.sb(ctx, f"{name}_u", [P, HID])

        with nc.Block() as block:
            @block.sync
            def _(sp):
                for a in range(2):
                    sp.dma_start(kT[a][:, :], k.kT[:, a * P:(a + 1) * P]).then_inc(m[f"kT_loaded{a}"], 16)
                sp.dma_start(kt[0][:, :], k.ktok[:, 0, :]).then_inc(m["k_loaded0"], 16)

            @block.tensor
            def _(pe):
                def open_or_close(start):
                    for b in (PROJ_BANK, VAL_BANK, GATE_BANK):
                        last = nc.tensor.matmul(b[:, :], k.zeros[:, 0:P], k.zeros[:, :], start=start, stop=not start)
                    return last

                def gate(t, i, a):
                    wait(pe, m[f"kT_loaded{a}"], (i + 1) * 16)
                    wait(pe, m["s_ready"], t)
                    nc.tensor.matmul(G_BANK[:, :], kT[a][:, :], k.theta_gate[:, :], start=True, stop=True
                                     ).then_inc(m["G_done"], 1)

                def val(t, a):
                    wait(pe, m["V_copied"], t)
                    nc.tensor.matmul(V_BANK[:, :], kT[a][:, :], k.theta_val[:, :], start=True, stop=True
                                     ).then_inc(m["V_done"], 1)

                def step(i, a, last_tile=False):
                    t = i * 2 + a
                    ni, na = (i, 1) if a == 0 else (i + 1, 0)
                    wait(pe, m["h_ready"], t + 1)
                    wait(pe, m["hT_copied"], t)
                    for j in range(HT):
                        x = nc.tensor.transpose(HT_BANK[:, j * P:(j + 1) * P], h[a][:, j * P:(j + 1) * P], k.ident)
                    x.then_inc(m["hT_done"], 1)
                    if not last_tile:
                        gate(t + 1, ni, na)
                    wait(pe, m["hT_copied"], t + 1)
                    wait(pe, m["r_copied"], t)
                    for j in range(HT):
                        x = nc.tensor.matmul(R_BANK[:, 0:P], k.theta_proj[:, j, :], hT[:, j * P:(j + 1) * P],
                                             start=j == 0, stop=j == HT - 1)
                    x.then_inc(m["pred_done"], 1)
                    if not last_tile:
                        val(t + 1, na)
                    wait(pe, m["rT_ready"], t + 1)
                    nc.tensor.transpose(R_BANK[:, P:2 * P], rT[:, :], k.ident).then_inc(m["r_done"], 1)
                    wait(pe, m["dgate_in_ready"], t)
                    nc.tensor.matmul(DH_BANK[:, :], rT[:, :], k.theta_projT[:, :], start=True, stop=True
                                     ).then_inc(m["dh_done"], 1)
                    wait(pe, m["r_copied"], t + 1)
                    nc.tensor.matmul(PROJ_BANK[:, :], r[:, :], h[a][:, :], start=False, stop=False
                                     ).then_inc(m["dproj_added"], 1)
                    wait(pe, m[f"k_loaded{a}"], (i + 1) * 16)
                    wait(pe, m["dval_in_ready"], t + 1)
                    nc.tensor.matmul(VAL_BANK[:, :], kt[a][:, :], dval_in[:, :], start=False, stop=False)
                    wait(pe, m["dgate_in_ready"], t + 1)
                    nc.tensor.matmul(GATE_BANK[:, :], kt[a][:, :], dgate_in[:, :], start=False, stop=False
                                     ).then_inc(m["dgate_added"], 1)

                open_or_close(True)
                gate(0, 0, 0)
                val(0, 0)
                @rounds(pe, PAIR_LOOPS)
                def _(i):
                    step(i, 0)
                    step(i, 1)
                step(PAIR_LOOPS, 0)
                step(PAIR_LOOPS, 1, last_tile=True)
                open_or_close(False).then_inc(m["closed"], 1)
                wait(pe, m["closed"], 1)

            @block.scalar
            def _(act):
                def forward(t, a):
                    wait(act, m["G_done"], t + 1)
                    if not (isinstance(t, int) and t < 2):
                        wait(act, m["dact_ready"], t - 1)
                    nc.scalar.activation(sig[a][:, :], G_BANK[:, :], ACT.Sigmoid).then_inc(m["sig_ready"], 1)
                    wait(act, m["V_done"], t + 1)
                    nc.scalar.copy(hv[a][:, :], V_BANK[:, :]).then_inc(m["V_copied"], 1)

                def step(i, a, last_tile=False):
                    t = i * 2 + a
                    wait(act, m["hT_done"], t + 1)
                    wait(act, m["pred_done"], t)
                    nc.scalar.copy(hT[:, :], HT_BANK[:, :]).then_inc(m["hT_copied"], 1)
                    if not (isinstance(i, int) and i == PAIR_LOOPS):
                        wait(act, m["V_done"], t + 1)
                        act.dma_start(kT[a][:, :], k.kT[:, bass.ds((t + 2) * P, P)]).then_inc(m[f"kT_loaded{a}"], 16)
                    if not last_tile:
                        wait(act, m["dgate_added"], t)
                        act.dma_start(kt[1 - a][:, :],
                                      k.ktok[:, :, :].rearrange("p t c -> p (t c)")[:, bass.ds((t + 1) * P, P)]
                                      ).then_inc(m[f"k_loaded{1 - a}"], 16)
                    if not last_tile:
                        forward(t + 1, 1 - a)
                    wait(act, m["r_done"], t + 1)
                    wait(act, m["dproj_added"], t)
                    nc.scalar.copy(r[:, :], R_BANK[:, P:2 * P]).then_inc(m["r_copied"], 1)

                forward(0, 0)
                step(0, 0)
                step(0, 1)
                with act.Fori(1, PAIR_LOOPS) as i:
                    step(i, 0)
                    step(i, 1)
                step(PAIR_LOOPS, 0)
                step(PAIR_LOOPS, 1, last_tile=True)

            @block.vector
            def _(dve):
                def activate(t, a):
                    wait(dve, m["sig_ready"], t + 1)
                    mul(nc, s[a][:, :], G_BANK[:, :], sig[a][:, :]).then_inc(m["s_ready"], 1)

                def hidden(t, a):
                    wait(dve, m["V_copied"], t + 1)
                    wait(dve, m["s_ready"], t + 1)
                    if not (isinstance(t, int) and t < 2):
                        wait(dve, m["dproj_added"], t - 1)
                    mul(nc, h[a][:, :], s[a][:, :], hv[a][:, :]).then_inc(m["h_ready"], 1)

                def derivative(t, a):
                    nc.vector.scalar_tensor_tensor(out=u[:, :], in0=sig[a][:, :], scalar=1.0, in1=s[a][:, :],
                                                   op0=ALU.subtract, op1=ALU.mult).then_inc(m["order"], 1)
                    wait(dve, m["order"], t * 2 + 1)
                    nc.vector.tensor_tensor(u[:, :], sig[a][:, :], u[:, :], ALU.subtract).then_inc(m["order"], 1)
                    wait(dve, m["order"], t * 2 + 2)
                    mul(nc, dact[a][:, :], u[:, :], hv[a][:, :]).then_inc(m["dact_ready"], 1)

                def step(i, a, last_tile=False):
                    t = i * 2 + a
                    if not last_tile:
                        activate(t + 1, 1 - a)
                    wait(dve, m["pred_done"], t + 1)
                    wait(dve, m["dh_done"], t)
                    nc.vector.tensor_tensor(rT[:, :], R_BANK[:, 0:P], k.vT[:, bass.ds(t * P, P)], ALU.subtract
                                            ).then_inc(m["rT_ready"], 1)
                    if not last_tile:
                        hidden(t + 1, 1 - a)
                    wait(dve, m["dh_done"], t + 1)
                    wait(dve, m["dgate_added"], t)
                    mul(nc, dval_in[:, :], DH_BANK[:, :], s[a][:, :]).then_inc(m["dval_in_ready"], 1)
                    wait(dve, m["dact_ready"], t + 1)
                    mul(nc, dgate_in[:, :], DH_BANK[:, :], dact[a][:, :]).then_inc(m["dgate_in_ready"], 1)
                    if not last_tile:
                        derivative(t + 1, 1 - a)

                activate(0, 0)
                hidden(0, 0)
                derivative(0, 0)
                step(0, 0)
                step(0, 1)
                with dve.Fori(1, PAIR_LOOPS) as i:
                    step(i, 0)
                    step(i, 1)
                step(PAIR_LOOPS, 0)
                step(PAIR_LOOPS, 1, last_tile=True)


def muon_phase(k, name):
    nc = k.nc
    grads = [k.bank[7], k.bank[6], k.bank[5]]
    xbank = [k.bank[0], k.bank[1], k.bank[2]]
    tbank = [k.bank[3], k.bank[4], k.bank[5]]
    M = 3
    m = {n: k.sem(f"{name}_{n}") for n in (
        "grad_copied", "squares_summed", "total_done", "norm_ready", "scaled", "xT_first", "xT_copied",
        "A_done", "A_copied", "AA_done", "poly_ready", "X_done", "X_copied", "XT_done", "order", "scaled_A",
        "updated")}
    with ExitStack() as ctx:
        X = [k.sb(ctx, f"{name}_X{n}", [P, HID]) for n in range(M)]
        XT = [k.sb(ctx, f"{name}_XT{n}", [P, HID]) for n in range(M)]
        A = [k.sb(ctx, f"{name}_A{n}", [P, P]) for n in range(M)]
        poly = [k.sb(ctx, f"{name}_poly{n}", [P, P]) for n in range(M)]
        aI = k.sb(ctx, f"{name}_aI", [P, P])
        squares = k.sb(ctx, f"{name}_squares", [P, HID])
        ssq = k.sb(ctx, f"{name}_ssq", [P, M])
        tot = k.sb(ctx, f"{name}_tot", [P, M])
        nrm = k.sb(ctx, f"{name}_nrm", [P, M])
        inv = k.sb(ctx, f"{name}_inv", [P, M])
        with nc.Block() as block:
            @block.tensor
            def _(pe):
                wait(pe, m["squares_summed"], M)
                nc.tensor.matmul(xbank[0][:, 0:M], k.c("ones"), ssq[:, :], start=True, stop=True
                                 ).then_inc(m["total_done"], 1)
                for n in range(M):
                    wait(pe, m["scaled"], n + 1)
                    for j in range(HT):
                        last = nc.tensor.transpose(tbank[n][:, j * P:(j + 1) * P], X[n][:, j * P:(j + 1) * P], k.ident)
                    last.then_inc(m["XT_done"], 1)
                @rounds(pe, NS_ITERS)
                def _(i):
                    for n in range(M):
                        wait(pe, m["xT_copied"], i * M + n + 1)
                        wait(pe, m["X_copied"], i * M)
                        for j in range(HT):
                            xt = XT[n][:, j * P:(j + 1) * P]
                            last = nc.tensor.matmul(xbank[n][:, 0:P], xt, xt, start=j == 0, stop=j == HT - 1)
                        last.then_inc(m["A_done"], 1)
                    for n in range(M):
                        wait(pe, m["A_copied"], i * M + n + 1)
                        nc.tensor.matmul(xbank[n][:, P:2 * P], A[n][:, :], A[n][:, :], start=True, stop=True
                                         ).then_inc(m["AA_done"], 1)
                    for n in range(M):
                        wait(pe, m["poly_ready"], i * M + n + 1)
                        for j in range(HT):
                            last = nc.tensor.matmul(tbank[n][:, j * P:(j + 1) * P], X[n][:, j * P:(j + 1) * P],
                                                    poly[n][:, :], start=True, stop=True)
                        last.then_inc(m["XT_done"], 1)
                        nc.tensor.matmul(xbank[n][:, :], poly[n][:, :], X[n][:, :], start=True, stop=True
                                         ).then_inc(m["X_done"], 1)

            @block.scalar
            def _(act):
                for n in range(M):
                    nc.scalar.copy(X[n][:, :], grads[n][:, :]).then_inc(m["grad_copied"], 1)
                for n in range(M):
                    wait(act, m["grad_copied"], n + 1)
                    if n:
                        wait(act, m["squares_summed"], n)
                    nc.scalar.activation(squares[:, :], X[n][:, :], ACT.Square, accum_out=ssq[:, n:n + 1]
                                         ).then_inc(m["squares_summed"], 1)
                wait(act, m["total_done"], 1)
                nc.scalar.copy(tot[:, :], xbank[0][:, 0:M]).then_inc(m["order"], 1)
                wait(act, m["order"], 1)
                nc.scalar.activation(nrm[:, :], tot[:, :], ACT.Sqrt).then_inc(m["norm_ready"], 1)
                for n in range(M):
                    wait(act, m["XT_done"], n + 1)
                    nc.scalar.copy(XT[n][:, :], tbank[n][:, :]).then_inc(m["xT_copied"], 1)
                @rounds(act, NS_ITERS)
                def _(i):
                    for n in range(M):
                        wait(act, m["XT_done"], (i + 1) * M + n + 1)
                        nc.scalar.copy(XT[n][:, :], tbank[n][:, :]).then_inc(m["xT_copied"], 1)
                wait(act, m["xT_copied"], (NS_ITERS + 1) * M)

            @block.vector
            def _(dve):
                nc.vector.tensor_scalar(aI[:, :], k.ident, NS_A, None, ALU.mult).then_inc(m["scaled_A"], 1)
                wait(dve, m["norm_ready"], 1)
                c = Chain(dve, m["updated"])
                c.link(nc.vector.tensor_scalar(inv[:, :], nrm[:, :], 1e-30, None, ALU.max))
                c.link(nc.vector.reciprocal(inv[:, :], inv[:, :]))
                c.link(mul(nc, inv[:, :], inv[:, :], tot[:, :]))
                c.link(nc.vector.tensor_tensor(inv[:, :], inv[:, :], nrm[:, :], ALU.add))
                c.link(nc.vector.tensor_scalar(inv[:, :], inv[:, :], 0.5, 1e-7 / GRAD_SCALE, ALU.mult, ALU.add))
                c.link(nc.vector.reciprocal(inv[:, :], inv[:, :]))
                for n in range(M):
                    nc.vector.tensor_scalar(X[n][:, :], X[n][:, :], inv[:, n:n + 1], None, ALU.mult
                                            ).then_inc(m["scaled"], 1)
                wait(dve, m["scaled"], M)
                @rounds(dve, NS_ITERS)
                def _(i):
                    for n in range(M):
                        wait(dve, m["A_done"], i * M + n + 1)
                        nc.vector.tensor_copy(A[n][:, :], xbank[n][:, 0:P]).then_inc(m["A_copied"], 1)
                    for n in range(M):
                        wait(dve, m["A_copied"], i * M + n + 1)
                        nc.vector.scalar_tensor_tensor(out=poly[n][:, :], in0=A[n][:, :], scalar=NS_B, in1=aI[:, :],
                                                       op0=ALU.mult, op1=ALU.add).then_inc(m["scaled_A"], 1)
                        wait(dve, m["scaled_A"], i * M + n + 2)
                        wait(dve, m["AA_done"], i * M + n + 1)
                        nc.vector.scalar_tensor_tensor(out=poly[n][:, :], in0=xbank[n][:, P:2 * P], scalar=NS_C,
                                                       in1=poly[n][:, :], op0=ALU.mult, op1=ALU.add
                                                       ).then_inc(m["poly_ready"], 1)
                    for n in range(M):
                        wait(dve, m["X_done"], i * M + n + 1)
                        nc.vector.tensor_copy(X[n][:, :], xbank[n][:, :]).then_inc(m["X_copied"], 1)
                wait(dve, m["X_copied"], NS_ITERS * M)
                wait(dve, m["xT_copied"], (NS_ITERS + 1) * M)
                for theta, step in ((k.theta_gate[:, :], X[0][:, :]), (k.theta_val[:, :], X[1][:, :]),
                                    (k.theta_projT[:, :], X[2][:, :]),
                                    (k.theta_proj[:, :, :].rearrange("p j c -> p (j c)"), XT[2][:, :])):
                    c.mark(nc.vector.scalar_tensor_tensor(out=theta, in0=step, scalar=-LR, in1=theta,
                                                          op0=ALU.mult, op1=ALU.add))
                wait(dve, m["updated"], c.n)


def query_phase(k):
    nc, d = k.nc, k.dram
    loaded, pp_done, pp_copied = k.sem("proj_w_loaded"), k.sem("pp_done"), k.sem("pp_copied")
    G_done, V_done, s_ready, hq_ready = k.sem("qG_done"), k.sem("qV_done"), k.sem("qs_ready"), k.sem("hq_ready")
    o_done, xb_ready, x_ready = k.sem("o_done"), k.sem("xb_ready"), k.sem("x1_ready")
    with ExitStack() as ctx:
        pw = k.sb(ctx, "proj_w_sb", [P, P])
        pb = k.sb(ctx, "proj_b_sb", [P, P])
        pp = k.sb(ctx, "proj_proj_w", [P, HT, P])
        s = k.sb(ctx, "q_s", [P, 2, SEQ])
        hq = [k.sb(ctx, f"hq{j}", [P, SEQ]) for j in range(HT)]
        xb = k.sb(ctx, "x_plus_b", [P, CT, P])
        with nc.Block() as block:
            @block.sync
            def _(sp):
                sp.dma_start(pw[:, :], d["L0_attn_proj_w"]).then_inc(loaded, 16)
                sp.dma_start(pb[:, :], spread(d["L0_attn_proj_b"])).then_inc(loaded, 16)

            @block.tensor
            def _(pe):
                wait(pe, loaded, 32)
                for j in range(HT):
                    last = nc.tensor.matmul(k.bank[0][:, j * P:(j + 1) * P], k.theta_projT[:, j * P:(j + 1) * P],
                                            pw[:, :], start=True, stop=True)
                last.then_inc(pp_done, 1)
                wait(pe, pp_copied, 1)
                @rounds(pe, CHUNKS)
                def _(i):
                    q = k.qT[:, bass.ds(i * SEQ, SEQ)]
                    for j in range(HT):
                        if j >= 2:
                            wait(pe, s_ready, i * HT + j - 1)
                        else:
                            wait(pe, hq_ready, i * HT)
                        nc.tensor.matmul(k.bank[j % 2][:, :], k.theta_gate[:, j * P:(j + 1) * P], q,
                                         start=True, stop=True).then_inc(G_done, 1)
                        if j >= 2:
                            wait(pe, hq_ready, i * HT + j - 1)
                        nc.tensor.matmul(k.bank[2 + j % 2][:, :], k.theta_val[:, j * P:(j + 1) * P], q,
                                         start=True, stop=True).then_inc(V_done, 1)
                    wait(pe, hq_ready, (i + 1) * HT)
                    wait(pe, x_ready, i)
                    for t in range(CT):
                        for j in range(HT):
                            last = nc.tensor.matmul(k.bank[4][:, t * P:(t + 1) * P], hq[j][:, t * P:(t + 1) * P],
                                                    pp[:, j, :], start=j == 0, stop=j == HT - 1)
                    last.then_inc(o_done, 1)

            @block.scalar
            def _(act):
                wait(act, pp_done, 1)
                nc.scalar.copy(pp[:, :, :].rearrange("p j c -> p (j c)"), k.bank[0][:, :]).then_inc(pp_copied, 1)
                @rounds(act, CHUNKS)
                def _(i):
                    for j in range(HT):
                        wait(act, G_done, i * HT + j + 1)
                        if j >= 2:
                            wait(act, hq_ready, i * HT + j - 1)
                        else:
                            wait(act, hq_ready, i * HT)
                        nc.scalar.activation(s[:, j % 2, :], k.bank[j % 2][:, :], ACT.Silu).then_inc(s_ready, 1)

            @block.gpsimd
            def _(pool):
                wait(pool, loaded, 32)
                @rounds(pool, CHUNKS)
                def _(i):
                    wait(pool, x_ready, i)
                    nc.gpsimd.tensor_tensor(xb[:, :, :], tiles_of(k.x, i),
                                            pb[:, :].unsqueeze(1).to_broadcast([P, CT, P]), ALU.add
                                            ).then_inc(xb_ready, 1)

            @block.vector
            def _(dve):
                @rounds(dve, CHUNKS)
                def _(i):
                    for j in range(HT):
                        wait(dve, s_ready, i * HT + j + 1)
                        wait(dve, V_done, i * HT + j + 1)
                        wait(dve, o_done, i)
                        mul(nc, hq[j][:, :], k.bank[2 + j % 2][:, :], s[:, j % 2, :]).then_inc(hq_ready, 1)
                    wait(dve, xb_ready, i + 1)
                    wait(dve, o_done, i + 1)
                    nc.vector.tensor_tensor(tiles_of(k.x, i), k.bank[4][:, :].rearrange("p (t c) -> p t c", t=CT),
                                            xb[:, :, :], ALU.add).then_inc(x_ready, 1)
                wait(dve, x_ready, CHUNKS)


def expert_weights_phase(k, f):
    nc, d = k.nc, k.dram
    vec_loaded, w_loaded, bias_loaded = k.sem("ln_vectors_loaded"), k.sem("experts_loaded"), k.sem("b_loaded")
    vecT_done, vecT_copied, lnb_ready = k.sem("vecT_done"), k.sem("vecT_copied"), k.sem("lnb_spread")
    w1T_done, w1T_copied, b1_done, b1_ready = (k.sem("w1T_done"), k.sem("w1T_copied"), k.sem("b1_done"),
                                               k.sem("b1_ready"))
    w2T_done, w2T_copied, scaled = k.sem("w2T_done"), k.sem("w2T_copied"), k.sem("w1_scaled")
    with ExitStack() as ctx:
        vec = k.sb(ctx, "centroids_g_b", [3 * E, P])
        w1n = k.sb(ctx, "w1_natural", [P, E * HT, P])
        w2n = k.sb(ctx, "w2_natural", [P, E, HID])
        lnb = [k.sb(ctx, f"ln_b_spread{a}", [P, P]) for a in range(2)]
        with nc.Block() as block:
            @block.sync
            def _(sp):
                for n, name in enumerate(("centroids", "ln_g", "ln_b")):
                    sp.dma_start(vec[n * E:(n + 1) * E, :], d["L0_ffn_" + name]).then_inc(vec_loaded, 16)
                for e in range(E):
                    sp.dma_start(w1n[:, e * HT:(e + 1) * HT, :], d["L0_ffn_w1"][e, :, :].rearrange("(j p) c -> p j c", p=P)
                                 ).then_inc(w_loaded, 16)
                    sp.dma_start(w2n[:, e, :], d["L0_ffn_w2"][e, :, :]).then_inc(w_loaded, 16)
                    sp.dma_start(f.b1[:, e, :], spread(d["L0_ffn_b1"][e, :])).then_inc(bias_loaded, 16)
                    sp.dma_start(f.b2[:, e, :], spread(d["L0_ffn_b2"][e, :])).then_inc(bias_loaded, 16)
                sp.wait_ge(bias_loaded, 32 * E)

            @block.tensor
            def _(pe):
                pe.wait_ge(vec_loaded, 48)
                nc.tensor.transpose(k.bank[4][:, 0:3 * E], vec[:, :], k.ident[0:3 * E, 0:3 * E]).then_inc(vecT_done, 1)
                pe.wait_ge(w_loaded, 32 * E)
                for e in range(E):
                    wait(pe, w1T_copied, e)
                    for j in range(HT):
                        last = nc.tensor.transpose(k.bank[0][:, j * P:(j + 1) * P], w1n[:, e * HT + j, :], k.ident)
                    last.then_inc(w1T_done, 1)
                    wait(pe, w2T_copied, e)
                    for j in range(HT):
                        last = nc.tensor.transpose(k.bank[1][:, j * P:(j + 1) * P], w2n[:, e, j * P:(j + 1) * P], k.ident)
                    last.then_inc(w2T_done, 1)
                    pe.wait_ge(w1T_copied, e + 1)
                    pe.wait_ge(lnb_ready, e + 1)
                    wait(pe, b1_ready, e)
                    nc.tensor.matmul(k.bank[2][:, :], lnb[e % 2][:, :], f.w1[:, e, :], start=True, stop=True
                                     ).then_inc(b1_done, 1)

            @block.scalar
            def _(act):
                act.wait_ge(vecT_done, 1)
                nc.scalar.copy(f.vecT[:, :], k.bank[4][:, 0:3 * E]).then_inc(vecT_copied, 1)
                for e in range(E):
                    act.wait_ge(w1T_done, e + 1)
                    nc.scalar.copy(f.w1[:, e, :], k.bank[0][:, :]).then_inc(w1T_copied, 1)
                    act.wait_ge(w2T_done, e + 1)
                    nc.scalar.copy(f.w2[:, e, :], k.bank[1][:, :]).then_inc(w2T_copied, 1)
                act.wait_ge(w2T_copied, E)

            @block.vector
            def _(dve):
                dve.wait_ge(vecT_copied, 1)
                dve.wait_ge(bias_loaded, 32 * E)

                def spread_ln_b(e):
                    wait(dve, b1_done, e - 1)
                    nc.vector.tensor_scalar(lnb[e % 2][:, :], k.c("ones"), f.vecT[:, 2 * E + e:2 * E + e + 1], None,
                                            ALU.mult).then_inc(lnb_ready, 1)

                spread_ln_b(0)
                for e in range(E):
                    if e + 1 < E:
                        spread_ln_b(e + 1)
                    dve.wait_ge(b1_done, e + 1)
                    nc.vector.tensor_tensor(f.b1[:, e, :], k.bank[2][:, :], f.b1[:, e, :], ALU.add).then_inc(b1_ready, 1)
                    nc.vector.tensor_scalar(f.w1[:, e, :], f.w1[:, e, :], f.vecT[:, E + e:E + e + 1], None,
                                            ALU.mult).then_inc(scaled, 1)
                dve.wait_ge(b1_ready, E)
                dve.wait_ge(scaled, E)


def affinity_phase(k, f):
    nc = k.nc
    order_p, xl_ready, xlT_done, xlT_copied = k.sem("aff_order"), k.sem("xl_ready"), k.sem("xlT_done"), k.sem("xlT_copied")
    xl_kept, aff_done, aff_copied = k.sem("xl_kept"), k.sem("aff_done"), k.sem("aff_copied")
    max_ready, alpha_ready, order_v, count_done = (k.sem("aff_max_ready"), k.sem("alpha_ready"), k.sem("route_order"),
                                                   k.sem("count_done"))
    oh_ready = k.sem("onehot_ready")
    with ExitStack() as ctx:
        xc = k.sb(ctx, "aff_xc", [P, CT, P])
        xl = k.sb(ctx, "aff_xl", [P, CT, P])
        xT = k.sb(ctx, "aff_xT", [P, SEQ])
        aff = k.sb(ctx, "aff", [P, TILES, E])
        oh = k.sb(ctx, "onehot", [P, TILES, E])
        key = k.sb(ctx, "route_key", [P, TILES, E])
        top = k.sb(ctx, "route_max", [P, TILES])
        rank = k.sb(ctx, "route_rank", [P, TILES])
        total = k.sb(ctx, "totals", [P, E, TILES])
        incl = k.sb(ctx, "inclusive", [P, E, TILES])
        cmp = k.sb(ctx, "tile_starts_used", [P, E, TILES])
        ntile = k.sb(ctx, "tiles_of_expert", [P, E])
        ends = k.sb(ctx, "expert_ends", [P, E])
        firsts = k.sb(ctx, "expert_firsts", [P, E])
        pos = k.sb(ctx, "positions", [P, TILES])
        scmp = k.sb(ctx, "slot_compare", [P, PADDED, E - 1])
        sexp = k.sb(ctx, "slot_expert_f", [P, PADDED])
        with nc.Block() as block:
            @block.gpsimd
            def _(pool):
                @rounds(pool, CHUNKS)
                def _(i):
                    c = Chain(pool, order_p, i)
                    wait(pool, xl_ready, i)
                    c.link(nc.gpsimd.tensor_tensor(xc[:, :, :], tiles_of(k.x, i), per_token(k.mean, i), ALU.subtract))
                    wait(pool, xlT_done, i)
                    wait(pool, xl_kept, i)
                    nc.gpsimd.tensor_tensor(xl[:, :, :], xc[:, :, :], per_token(k.rstd, i), ALU.mult).then_inc(xl_ready, 1)

            @block.scalar
            def _(act):
                @rounds(act, CHUNKS)
                def _(i):
                    act.wait_ge(xl_ready, i + 1)
                    nc.scalar.copy(tiles_of(f.xl, i), xl[:, :, :]).then_inc(xl_kept, 1)
                    act.wait_ge(xlT_done, i + 1)
                    wait(act, aff_done, i)
                    nc.scalar.copy(xT[:, :], k.bank[2][:, :]).then_inc(xlT_copied, 1)
                act.wait_ge(max_ready, 1)
                nc.scalar.activation(f.alpha[:, :], top[:, :], ACT.Sigmoid).then_inc(alpha_ready, 1)
                act.wait_ge(alpha_ready, 1)
                act.wait_ge(xl_kept, CHUNKS)

            @block.tensor
            def _(pe):
                @rounds(pe, CHUNKS)
                def _(i):
                    pe.wait_ge(xl_ready, i + 1)
                    wait(pe, xlT_copied, i)
                    for j in range(CT):
                        last = nc.tensor.transpose(k.bank[2][:, j * P:(j + 1) * P], xl[:, j, :], k.ident)
                    last.then_inc(xlT_done, 1)
                    pe.wait_ge(xlT_copied, i + 1)
                    wait(pe, aff_copied, i)
                    for j in range(CT):
                        last = nc.tensor.matmul(k.bank[3][:, j * E:(j + 1) * E], xT[:, j * P:(j + 1) * P],
                                                f.vecT[:, 0:E], start=True, stop=True)
                    last.then_inc(aff_done, 1)
                flat = oh[:, :, :].rearrange("p t e -> p (t e)")
                pe.wait_ge(oh_ready, 1)
                nc.tensor.matmul(k.bank[4][:, 0:TILES * E], k.c("before"), flat, start=True, stop=True)
                nc.tensor.matmul(k.bank[5][:, 0:TILES * E], k.c("ones"), flat, start=True, stop=True
                                 ).then_inc(count_done, 1)

            @block.vector
            def _(dve):
                @rounds(dve, CHUNKS)
                def _(i):
                    dve.wait_ge(aff_done, i + 1)
                    nc.vector.tensor_copy(tiles_of(aff, i), k.bank[3][:, 0:CT * E].rearrange("p (t e) -> p t e", e=E)
                                          ).then_inc(aff_copied, 1)
                dve.wait_ge(aff_copied, CHUNKS)

                def over_e(t):
                    return t.unsqueeze(2).to_broadcast([P, TILES, E])
                nc.vector.tensor_reduce(top[:, :], aff[:, :, :], AXX, ALU.max).then_inc(max_ready, 1)
                dve.wait_ge(max_ready, 1)
                c = Chain(dve, order_v)
                rank8 = k.c("rank8").unsqueeze(1).to_broadcast([P, TILES, E])
                c.link(nc.vector.tensor_tensor(key[:, :, :], aff[:, :, :], over_e(top[:, :]), ALU.is_equal))
                c.link(mul(nc, key[:, :, :], key[:, :, :], rank8))
                c.link(nc.vector.tensor_reduce(rank[:, :], key[:, :, :], AXX, ALU.max))
                nc.vector.tensor_tensor(oh[:, :, :], key[:, :, :], over_e(rank[:, :]), ALU.is_equal).then_inc(oh_ready, 1)
                dve.wait_ge(count_done, 1)
                tot_ps = k.bank[5][:, 0:TILES * E].rearrange("p (t e) -> p e t", e=E)
                pre_ps = k.bank[4][:, 0:TILES * E].rearrange("p (t e) -> p t e", e=E)
                c.link(nc.vector.tensor_copy(total[:, :, :], tot_ps))

                def flat(t):
                    return t[:, :, :].rearrange("p e t -> p (e t)")
                c.link(nc.vector.tensor_tensor_scan(flat(incl), k.c("starts"), flat(total), 0.0, ALU.mult, ALU.add))
                c.mark(nc.vector.tensor_tensor(total[:, :, :], incl[:, :, :], total[:, :, :], ALU.subtract))
                c.link(nc.vector.tensor_tensor(cmp[:, :, :], incl[:, :, TILES - 1:TILES].to_broadcast([P, E, TILES]),
                                               k.c("tilestart").unsqueeze(1).to_broadcast([P, E, TILES]), ALU.is_gt))
                c.link(nc.vector.tensor_reduce(ntile[:, :], cmp[:, :, :], AXX, ALU.add))
                c.link(nc.vector.tensor_tensor_scan(ends[:, :], k.c("ones")[:, 0:E], ntile[:, :], 0.0, ALU.mult, ALU.add))
                c.mark(nc.vector.tensor_tensor(scmp[:, :, :], k.c("slot").unsqueeze(2).to_broadcast([P, PADDED, E - 1]),
                                               ends[:, 0:E - 1].unsqueeze(1).to_broadcast([P, PADDED, E - 1]), ALU.is_ge))
                c.link(nc.vector.tensor_tensor(firsts[:, :], ends[:, :], ntile[:, :], ALU.subtract))
                c.link(nc.vector.tensor_reduce(sexp[:, :], scmp[:, :, :], AXX, ALU.add))
                c.mark(nc.vector.tensor_copy(f.slot_expert[:, :], sexp[:, :]))
                c.link(nc.vector.tensor_scalar(firsts[:, :], firsts[:, :], float(P), None, ALU.mult))
                c.link(nc.vector.tensor_tensor(total[:, :, :], total[:, :, :],
                                               firsts[:, :].unsqueeze(2).to_broadcast([P, E, TILES]), ALU.add))
                c.link(nc.vector.tensor_tensor(key[:, :, :], pre_ps, total[:, :, :].rearrange("p e t -> p t e"), ALU.add))
                c.link(mul(nc, key[:, :, :], key[:, :, :], oh[:, :, :]))
                c.link(nc.vector.tensor_reduce(pos[:, :], key[:, :, :], AXX, ALU.add))
                c.link(nc.vector.tensor_copy(f.pos[:, :], pos[:, :]))


def sort_phase(k, f):
    nc = k.nc
    scattered, loaded = k.sem("xl_scattered"), k.sem("sorted_loaded")
    R = PADDED // 3
    with nc.Block() as block:
        @block.gpsimd
        def _(pool):
            for t in range(TILES):
                pool.indirect_dma_start(out=f.sorted_in, out_offset=bass.IndirectOffsetOnAxis(ap=f.pos[:, t:t + 1], axis=0),
                                        in_=f.xl[:, t, :], in_offset=None).then_inc(scattered, 16)

        @block.sync
        def _(sp):
            sp.wait_ge(scattered, 16 * TILES)
            for t in range(0, PADDED, R):
                sp.dma_start(f.sorted[:, t:t + R, :], f.sorted_in[t * P:(t + R) * P, :].rearrange("(t p) c -> p t c", p=P)
                             ).then_inc(loaded, 16)
            sp.wait_ge(loaded, 16 * (PADDED // R))


def experts_phase(k, f):
    nc = k.nc
    R = 3
    assert PADDED % R == 0
    LAST = PADDED // R - 1
    STORES = 3
    m = {n: k.sem(f"moe_{n}") for n in ("x_ready", "xT_done", "xT_copied", "h_done", "h_ready", "hT_done", "hT_ready",
                                        "y_done", "y_ready", "y_stored", "xl_added", "combined", "counted")}
    y_fetched = [k.sem(f"y_fetched{c}") for c in range(CHUNKS)]
    with ExitStack() as ctx:
        xs = [k.sb(ctx, f"xs{a}", [P, P]) for a in range(R)]
        xT = k.sb(ctx, "xsT", [P, P])
        h = k.sb(ctx, "moe_h", [P, HID])
        hT = k.sb(ctx, "moe_hT", [P, HID])
        w1 = f.w1[:, :, :].rearrange("p e c -> p (e c)")
        w2 = f.w2[:, :, :].rearrange("p e c -> p (e c)")
        b1 = f.b1[:, :, :].rearrange("p e c -> p (e c)")
        b2 = f.b2[:, :, :].rearrange("p e c -> p (e c)")
        fetched = f.sorted
        XT_BANK, H_BANK, HT_BANK, Y_BANK = k.bank[0:4]

        def experts(engine, t, n):
            return nc.values_load_multi_w_load_instructions(f.slot_expert[0:1, bass.ds(t, n)], [engine],
                                                            min_val=0, max_val=E - 1)[1]

        def one(t3, t):
            return t3[:, bass.ds(t, 1), :].rearrange("p a c -> p (a c)")

        def each_tile(eng, step, engine=None):
            def group(t, last=False):
                es = experts(engine, t, R if last else R + 1) if engine else [None] * (R + 1)
                for a in range(R):
                    step(t + a, a, R - 1 - a if last else R, es[a:a + 2])
            group(0)
            with eng.Fori(1, LAST) as i:
                group(i * R)
            group(LAST * R, last=True)

        with nc.Block() as block:
            @block.sync
            def _(sp):
                S = PADDED // STORES
                for n in range(STORES):
                    sp.wait_ge(m["y_ready"], (n + 1) * S)
                    sp.dma_start(f.sorted_out[n * S * P:(n + 1) * S * P, :].rearrange("(t p) c -> p t c", p=P),
                                 f.ys[:, n * S:(n + 1) * S, :]).then_inc(m["y_stored"], 16)
                sp.wait_ge(m["y_stored"], 16 * STORES)

            @block.gpsimd
            def _(pool):
                for c in range(CHUNKS):
                    at = slice(c * CT, (c + 1) * CT)
                    nc.gpsimd.tensor_tensor(k.x[:, at, :], k.x[:, at, :], f.xl[:, at, :], ALU.add).then_inc(m["xl_added"], 1)
                pool.wait_ge(m["x_ready"], PADDED)
                pool.wait_ge(m["y_stored"], 16 * STORES)
                for t in range(TILES):
                    pool.indirect_dma_start(out=fetched[:, t, :], out_offset=None, in_=f.sorted_out,
                                            in_offset=bass.IndirectOffsetOnAxis(ap=f.pos[:, t:t + 1], axis=0)
                                            ).then_inc(y_fetched[t // CT], 16)

            @block.tensor
            def _(pe):
                def transpose_x(t, a):
                    pe.wait_ge(m["x_ready"], t + 1)
                    wait(pe, m["xT_copied"], t)
                    nc.tensor.transpose(XT_BANK[:, 0:P], xs[a][:, :], k.ident).then_inc(m["xT_done"], 1)

                def hidden(t, e):
                    pe.wait_ge(m["xT_copied"], t + 1)
                    wait(pe, m["h_ready"], t)
                    nc.tensor.matmul(H_BANK[:, :], xT[:, :], w1[:, bass.ds(e * HID, HID)], start=True, stop=True
                                     ).then_inc(m["h_done"], 1)

                def finish(t, a, left, es):
                    pe.wait_ge(m["h_ready"], t + 1)
                    wait(pe, m["hT_ready"], t)
                    for j in range(HT):
                        last = nc.tensor.transpose(HT_BANK[:, j * P:(j + 1) * P], h[:, j * P:(j + 1) * P], k.ident)
                    last.then_inc(m["hT_done"], 1)
                    if left >= 1:
                        hidden(t + 1, es[1])
                    if left >= 2:
                        transpose_x(t + 2, (a + 2) % R)
                    pe.wait_ge(m["hT_ready"], t + 1)
                    wait(pe, m["y_ready"], t)
                    for j in range(HT):
                        last = nc.tensor.matmul(Y_BANK[:, 0:P], hT[:, j * P:(j + 1) * P],
                                                w2[:, bass.ds(es[0] * HID + j * P, P)], start=j == 0, stop=j == HT - 1)
                    last.then_inc(m["y_done"], 1)

                transpose_x(0, 0)
                hidden(0, experts(mybir.EngineType.PE, 0, 1)[0])
                transpose_x(1, 1)
                each_tile(pe, finish, mybir.EngineType.PE)

            @block.scalar
            def _(act):
                def copy_x(t):
                    act.wait_ge(m["xT_done"], t + 1)
                    wait(act, m["h_done"], t)
                    nc.scalar.copy(xT[:, :], XT_BANK[:, 0:P]).then_inc(m["xT_copied"], 1)

                def step(t, a, left, es):
                    act.wait_ge(m["hT_done"], t + 1)
                    wait(act, m["y_done"], t)
                    nc.scalar.activation(hT[:, :], HT_BANK[:, :], ACT.Relu).then_inc(m["hT_ready"], 1)
                    if left >= 2:
                        copy_x(t + 2)

                copy_x(0)
                copy_x(1)
                each_tile(act, step)

            @block.vector
            def _(dve):
                def normalise(t, a):
                    wait(dve, m["xT_done"], t - R + 1)
                    nc.vector.tensor_scalar(xs[a][:, :], one(f.sorted, t), f.mean[:, bass.ds(t, 1)],
                                            f.rstd[:, bass.ds(t, 1)], ALU.subtract, ALU.mult).then_inc(m["x_ready"], 1)

                def bias_h(t, e):
                    dve.wait_ge(m["h_done"], t + 1)
                    wait(dve, m["hT_done"], t)
                    nc.vector.tensor_tensor(h[:, :], H_BANK[:, :], b1[:, bass.ds(e * HID, HID)], ALU.add
                                            ).then_inc(m["h_ready"], 1)

                def step(t, a, left, es):
                    if left >= 3:
                        normalise(t + 3, a)
                    if left >= 1:
                        bias_h(t + 1, es[1])
                    dve.wait_ge(m["y_done"], t + 1)
                    nc.vector.tensor_tensor(one(f.ys, t), Y_BANK[:, 0:P], b2[:, bass.ds(es[0] * P, P)], ALU.add
                                            ).then_inc(m["y_ready"], 1)

                for t in range(R):
                    normalise(t, t)
                bias_h(0, experts(mybir.EngineType.DVE, 0, 1)[0])
                each_tile(dve, step, mybir.EngineType.DVE)
                dve.wait_ge(m["xl_added"], CHUNKS)
                for t in range(TILES):
                    if t % CT == 0:
                        dve.wait_ge(y_fetched[t // CT], 16 * CT)
                    nc.vector.scalar_tensor_tensor(out=k.x[:, t, :], in0=fetched[:, t, :], scalar=f.alpha[:, t:t + 1],
                                                   in1=k.x[:, t, :], op0=ALU.mult, op1=ALU.add).then_inc(m["combined"], 1)
                    dve.wait_ge(m["combined"], t + 1)
                    count_tile(nc, k.st, k.x, t).then_inc(m["counted"], 1)
                dve.wait_ge(m["counted"], TILES)


def diagonal_attention_phase(k):
    nc, d = k.nc, k.dram
    G = CT * HEADS
    loaded, order_p = k.sem("wqkv_loaded"), k.sem("da_order_p")
    prep_done, prep_ready = k.sem("blockdiag_done"), k.sem("blockdiag_ready")
    xn_ready, xT_done, xT_copied = k.sem("da_xn_ready"), k.sem("da_xT_done"), k.sem("da_xT_copied")
    form_done, form_used, score_ready = k.sem("form_done"), k.sem("form_used"), k.sem("score_ready")
    sum_done, sum_copied, vsum_done, vsum_copied = k.sem("xsum_done"), k.sem("xsum_copied"), k.sem("vsum_done"), k.sem("vsum_copied")
    order, shifted, exp_ready = k.sem("da_order"), k.sem("scores_shifted"), k.sem("da_exp_ready")
    probs_ready, term_ready, x_ready = k.sem("da_probs_ready"), k.sem("da_term_ready"), k.sem("x3_ready")
    counted = k.sem("x3_counted")
    with ExitStack() as ctx:
        wq = k.sb(ctx, "wq", [HD, HD])
        wkr = k.sb(ctx, "wk_repeated", [HD, HEADS, HD])
        wvr = k.sb(ctx, "wv_repeated", [HD, HEADS, HD])
        a1 = k.sb(ctx, "wq_wk", [HD, P])
        form = k.sb(ctx, "qk_form", [P, P])
        bdv = k.sb(ctx, "wv_blocks", [P, P])
        xc = k.sb(ctx, "da_xc", [P, CT, P])
        xn = [k.sb(ctx, f"da_xn{a}", [P, CT, P]) for a in range(2)]
        xT = k.sb(ctx, "da_xT", [P, SEQ])
        xsum = k.sb(ctx, "da_xsum", [P, P])
        prod = k.sb(ctx, "da_prod", [P, SEQ])
        sc = k.sb(ctx, "da_scores", [P, CHUNKS, G])
        top = k.sb(ctx, "da_max", [P, G])
        den = k.sb(ctx, "da_den", [P, G])
        vs = k.sb(ctx, "da_vsum", [P, CHUNKS, P])
        term = [k.sb(ctx, f"da_term{a}", [P, CT, P]) for a in range(2)]
        CH2 = CHUNKS // 2

        def pairs(eng):
            def run(body):
                body(0, 0)
                body(0, 1)
                with eng.Fori(1, CH2) as i:
                    body(i, 0)
                    body(i, 1)
            return run

        with nc.Block() as block:
            @block.sync
            def _(sp):
                sp.dma_start(wq[:, :], d["L1_attn_Wq"]).then_inc(loaded, 16)
                for h in range(HEADS):
                    sp.dma_start(wkr[:, h, :], d["L1_attn_Wk"]).then_inc(loaded, 16)
                    sp.dma_start(wvr[:, h, :], d["L1_attn_Wv"]).then_inc(loaded, 16)

            @block.gpsimd
            def _(pool):
                @pairs(pool)
                def _(i, a):
                    t = i * 2 + a
                    c = Chain(pool, order_p, t)
                    wait(pool, xn_ready, t)
                    c.link(nc.gpsimd.tensor_tensor(xc[:, :, :], tiles_of(k.x, t), per_token(k.mean, t), ALU.subtract))
                    wait(pool, score_ready, t - 1)
                    wait(pool, vsum_done, t - 1)
                    nc.gpsimd.tensor_tensor(xn[a][:, :, :], xc[:, :, :], per_token(k.rstd, t), ALU.mult
                                            ).then_inc(xn_ready, 1)
                for c in range(CHUNKS):
                    pool.wait_ge(term_ready, c + 1)
                    at = slice(c * CT, (c + 1) * CT)
                    nc.gpsimd.tensor_tensor(k.x[:, at, :], k.x[:, at, :], term[c % 2][:, :, :], ALU.add).then_inc(x_ready, 1)

            @block.tensor
            def _(pe):
                pe.wait_ge(loaded, 16 * (1 + 2 * HEADS))
                nc.tensor.matmul(k.bank[0][0:HD, 0:P], wq[:, :], wkr[:, :, :].rearrange("e h d -> e (h d)"),
                                 start=True, stop=True).then_inc(prep_done, 1)
                nc.tensor.matmul(k.bank[1][:, 0:P], wvr[:, :, :].rearrange("e h d -> e (h d)"), k.c("headtile")[0:HD, :],
                                 start=True, stop=True).then_inc(prep_done, 1)
                pe.wait_ge(prep_ready, 1)
                nc.tensor.matmul(k.bank[2][:, 0:P], k.c("headtile")[0:HD, :], a1[:, :], start=True, stop=True
                                 ).then_inc(prep_done, 1)
                pe.wait_ge(prep_ready, 3)

                @pairs(pe)
                def _(i, a):
                    t = i * 2 + a
                    pe.wait_ge(xn_ready, t + 1)
                    wait(pe, xT_copied, t)
                    for j in range(CT):
                        last = nc.tensor.transpose(k.bank[0][:, j * P:(j + 1) * P], xn[a][:, j, :], k.ident)
                    last.then_inc(xT_done, 1)
                    pe.wait_ge(xT_copied, t + 1)
                    wait(pe, form_used, t)
                    for j in range(CT):
                        last = nc.tensor.matmul(k.bank[1][:, j * P:(j + 1) * P], xT[:, j * P:(j + 1) * P], form[:, :],
                                                start=True, stop=True)
                    last.then_inc(form_done, 1)
                    wait(pe, sum_copied, t)
                    for j in range(CT):
                        last = nc.tensor.matmul(k.bank[3][:, 0:P], xn[a][:, j, :], k.c("ones"),
                                                start=j == 0, stop=j == CT - 1)
                    last.then_inc(sum_done, 1)
                    pe.wait_ge(sum_copied, t + 1)
                    wait(pe, vsum_copied, t)
                    nc.tensor.matmul(k.bank[2][:, 0:P], xsum[:, :], bdv[:, :], start=True, stop=True).then_inc(vsum_done, 1)

            @block.scalar
            def _(act):
                @pairs(act)
                def _(i, a):
                    t = i * 2 + a
                    act.wait_ge(xT_done, t + 1)
                    wait(act, form_done, t)
                    nc.scalar.copy(xT[:, :], k.bank[0][:, :]).then_inc(xT_copied, 1)
                    act.wait_ge(sum_done, t + 1)
                    wait(act, vsum_done, t)
                    nc.scalar.copy(xsum[:, :], k.bank[3][:, 0:P]).then_inc(sum_copied, 1)
                    act.wait_ge(vsum_done, t + 1)
                    nc.scalar.copy(vs[:, bass.ds(t, 1), :].rearrange("p a c -> p (a c)"), k.bank[2][:, 0:P]
                                   ).then_inc(vsum_copied, 1)
                act.wait_ge(shifted, 1)
                nc.scalar.activation(sc[:, :, :], sc[:, :, :], ACT.Exp, scale=float(P) ** -0.5).then_inc(exp_ready, 1)

            @block.vector
            def _(dve):
                dve.wait_ge(prep_done, 2)
                nc.vector.tensor_copy(a1[:, :], k.bank[0][0:HD, 0:P]).then_inc(prep_ready, 1)
                mul(nc, bdv[:, :], k.bank[1][:, 0:P], k.c("headmask")).then_inc(prep_ready, 1)
                dve.wait_ge(prep_done, 3)
                mul(nc, form[:, :], k.bank[2][:, 0:P], k.c("headmask")).then_inc(prep_ready, 1)

                @pairs(dve)
                def _(i, a):
                    t = i * 2 + a
                    dve.wait_ge(form_done, t + 1)
                    wait(dve, score_ready, t)
                    mul(nc, prod[:, :], k.bank[1][:, :], xn[a][:, :, :].rearrange("p t c -> p (t c)")).then_inc(form_used, 1)
                    dve.wait_ge(form_used, t + 1)
                    nc.vector.tensor_reduce(sc[:, bass.ds(t, 1), :].rearrange("p a g -> p (a g)"),
                                            prod[:, :].rearrange("p (g e) -> p g e", e=HD), AXX, ALU.add
                                            ).then_inc(score_ready, 1)
                dve.wait_ge(score_ready, CHUNKS)
                dve.wait_ge(vsum_copied, CHUNKS)
                c = Chain(dve, order)
                by_group = sc[:, :, :].rearrange("p c g -> p g c")

                def over_c(t):
                    return t.unsqueeze(1).to_broadcast([P, CHUNKS, G])
                c.link(nc.vector.tensor_reduce(top[:, :], by_group, AXX, ALU.max))
                nc.vector.tensor_tensor(sc[:, :, :], sc[:, :, :], over_c(top[:, :]), ALU.subtract).then_inc(shifted, 1)
                dve.wait_ge(exp_ready, 1)
                c.link(nc.vector.tensor_reduce(den[:, :], by_group, AXX, ALU.add))
                c.link(nc.vector.reciprocal(den[:, :], den[:, :]))
                c.link(mul(nc, sc[:, :, :], sc[:, :, :], over_c(den[:, :])))

                def count(s):
                    dve.wait_ge(x_ready, s + 1)
                    for t in range(s * CT, (s + 1) * CT):
                        count_tile(nc, k.st, k.x, t).then_inc(counted, 1)

                for s in range(CHUNKS):
                    if s >= 2:
                        count(s - 2)
                    mul(nc, term[s % 2][:, :, :].rearrange("p t (h e) -> p t h e", e=HD),
                        sc[:, s, :].rearrange("p (t h) -> p t h", h=HEADS).unsqueeze(3).to_broadcast([P, CT, HEADS, HD]),
                        vs[:, s, :].rearrange("p (h e) -> p h e", e=HD).unsqueeze(1).to_broadcast([P, CT, HEADS, HD])
                        ).then_inc(term_ready, 1)
                count(CHUNKS - 2)
                count(CHUNKS - 1)
                dve.wait_ge(counted, TILES)


def router_phase(k, g):
    nc, d = k.nc, k.dram
    loaded, order_p, xf_ready = k.sem("router_loaded"), k.sem("r_order_p"), k.sem("xf_ready")
    xf_kept, xT_done, xT_copied = k.sem("xf_kept"), k.sem("r_xT_done"), k.sem("r_xT_copied")
    hid_done, hid_ready, log_done, log_copied = k.sem("r_hid_done"), k.sem("r_hid_ready"), k.sem("log_done"), k.sem("log_copied")
    sw_ready, shifted, exp_ready, order = k.sem("sw_ready"), k.sem("r_shifted"), k.sem("r_exp_ready"), k.sem("r_order")
    with ExitStack() as ctx:
        w1 = k.sb(ctx, "router_w1", [P, RH])
        b1 = k.sb(ctx, "router_b1", [RH, 1])
        w2 = k.sb(ctx, "router_w2", [RH, E])
        b2 = k.sb(ctx, "router_b2", [P, E])
        sw = k.sb(ctx, "shared_weight", [P, 2])
        xc = k.sb(ctx, "r_xc", [P, CT, P])
        xf = k.sb(ctx, "r_xf", [P, CT, P])
        hid = k.sb(ctx, "r_hid", [RH, SEQ])
        lg = k.sb(ctx, "logits", [P, TILES, E])
        key = k.sb(ctx, "r_key", [P, TILES, E])
        one = k.sb(ctx, "r_one", [P, TILES])
        best = k.sb(ctx, "r_best", [P, 2, TILES])
        with nc.Block() as block:
            @block.sync
            def _(sp):
                sp.dma_start(w1[:, :], d["L1_ffn_router_w1"]).then_inc(loaded, 16)
                sp.dma_start(b1[:, :], d["L1_ffn_router_b1"].rearrange("(p a) -> p a", a=1)).then_inc(loaded, 16)
                sp.dma_start(w2[:, :], d["L1_ffn_router_w2"]).then_inc(loaded, 16)
                sp.dma_start(b2[:, :], spread(d["L1_ffn_router_b2"])).then_inc(loaded, 16)
                sp.dma_start(sw[:, 0:1], spread(d["L1_ffn_shared_weight"])).then_inc(loaded, 16)

            @block.gpsimd
            def _(pool):
                @rounds(pool, CHUNKS)
                def _(i):
                    c = Chain(pool, order_p, i)
                    wait(pool, xf_ready, i)
                    c.link(nc.gpsimd.tensor_tensor(xc[:, :, :], tiles_of(k.x, i), per_token(k.mean, i), ALU.subtract))
                    wait(pool, xT_done, i)
                    wait(pool, xf_kept, i)
                    nc.gpsimd.tensor_tensor(xf[:, :, :], xc[:, :, :], per_token(k.rstd, i), ALU.mult).then_inc(xf_ready, 1)

            @block.tensor
            def _(pe):
                pe.wait_ge(loaded, 80)

                @rounds(pe, CHUNKS)
                def _(i):
                    pe.wait_ge(xf_ready, i + 1)
                    wait(pe, xT_copied, i)
                    for j in range(CT):
                        last = nc.tensor.transpose(k.bank[0][:, j * P:(j + 1) * P], xf[:, j, :], k.ident)
                    last.then_inc(xT_done, 1)
                    pe.wait_ge(xT_copied, i + 1)
                    wait(pe, hid_ready, i)
                    nc.tensor.matmul(k.bank[1][0:RH, :], w1[:, :], g.xfT[:, bass.ds(i * SEQ, SEQ)], start=True, stop=True
                                     ).then_inc(hid_done, 1)
                    pe.wait_ge(hid_ready, i + 1)
                    wait(pe, log_copied, i)
                    for j in range(CT):
                        last = nc.tensor.matmul(k.bank[2][:, j * E:(j + 1) * E], hid[:, j * P:(j + 1) * P], w2[:, :],
                                                start=True, stop=True)
                    last.then_inc(log_done, 1)

            @block.scalar
            def _(act):
                act.wait_ge(loaded, 80)
                nc.scalar.activation(sw[:, 0:1], sw[:, 0:1], ACT.Sigmoid).then_inc(sw_ready, 1)

                @rounds(act, CHUNKS)
                def _(i):
                    act.wait_ge(xf_ready, i + 1)
                    nc.scalar.copy(tiles_of(g.xf, i), xf[:, :, :]).then_inc(xf_kept, 1)
                    act.wait_ge(xT_done, i + 1)
                    nc.scalar.copy(g.xfT[:, bass.ds(i * SEQ, SEQ)], k.bank[0][:, :]).then_inc(xT_copied, 1)
                    act.wait_ge(hid_done, i + 1)
                    wait(act, log_done, i)
                    nc.scalar.activation(hid[:, :], k.bank[1][0:RH, :], ACT.Gelu, bias=b1[:, 0:1]).then_inc(hid_ready, 1)
                act.wait_ge(shifted, 1)
                nc.scalar.activation(lg[:, :, :], lg[:, :, :], ACT.Exp).then_inc(exp_ready, 1)
                act.wait_ge(exp_ready, 1)

            @block.vector
            def _(dve):
                dve.wait_ge(loaded, 80)

                @rounds(dve, CHUNKS)
                def _(i):
                    dve.wait_ge(log_done, i + 1)
                    nc.vector.tensor_tensor(tiles_of(lg, i), k.bank[2][:, 0:CT * E].rearrange("p (t e) -> p t e", e=E),
                                            b2[:, :].unsqueeze(1).to_broadcast([P, CT, E]), ALU.add).then_inc(log_copied, 1)
                dve.wait_ge(log_copied, CHUNKS)
                c = Chain(dve, order)

                def over_e(t):
                    return t.unsqueeze(2).to_broadcast([P, TILES, E])
                rank8 = k.c("rank8").unsqueeze(1).to_broadcast([P, TILES, E])
                c.link(nc.vector.tensor_reduce(one[:, :], lg[:, :, :], AXX, ALU.max))
                nc.vector.tensor_tensor(lg[:, :, :], lg[:, :, :], over_e(one[:, :]), ALU.subtract).then_inc(shifted, 1)
                dve.wait_ge(exp_ready, 1)
                c.link(nc.vector.tensor_reduce(one[:, :], lg[:, :, :], AXX, ALU.add))
                c.link(nc.vector.reciprocal(one[:, :], one[:, :]))
                c.link(mul(nc, lg[:, :, :], lg[:, :, :], over_e(one[:, :])))
                for s in range(2):
                    oh = g.onehot[:, :, s * E:(s + 1) * E]
                    c.link(nc.vector.tensor_reduce(best[:, s, :], lg[:, :, :], AXX, ALU.max))
                    c.link(nc.vector.tensor_tensor(key[:, :, :], lg[:, :, :], over_e(best[:, s, :]), ALU.is_equal))
                    c.link(mul(nc, key[:, :, :], key[:, :, :], rank8))
                    c.link(nc.vector.tensor_reduce(one[:, :], key[:, :, :], AXX, ALU.max))
                    c.link(nc.vector.tensor_tensor(oh, key[:, :, :], over_e(one[:, :]), ALU.is_equal))
                    if s == 0:
                        c.link(nc.vector.scalar_tensor_tensor(out=lg[:, :, :], in0=oh, scalar=-2.0, in1=lg[:, :, :],
                                                              op0=ALU.mult, op1=ALU.add))
                c.link(nc.vector.tensor_tensor(one[:, :], best[:, 0, :], best[:, 1, :], ALU.add))
                c.link(nc.vector.reciprocal(one[:, :], one[:, :]))
                dve.wait_ge(sw_ready, 1)
                c.link(nc.vector.tensor_scalar(sw[:, 1:2], sw[:, 0:1], -1.0, 1.0, ALU.mult, ALU.add))
                c.link(nc.vector.tensor_scalar(one[:, :], one[:, :], sw[:, 1:2], None, ALU.mult))
                c.link(nc.vector.tensor_scalar(g.weight[:, 0, :], k.c("ones")[:, 0:TILES], sw[:, 0:1], None, ALU.mult))
                for s in range(2):
                    c.link(mul(nc, g.weight[:, 1 + s, :], best[:, s, :], one[:, :]))


def dynamics_weights_phase(k, g):
    nc, d = k.nc, k.dram
    loaded, cut, order, placed = k.sem("dyn_loaded"), k.sem("b2_cut"), k.sem("dyn_order"), k.sem("b2_placed")
    H2 = 2 * EH
    loads = []

    def load(sp, to, of):
        loads.append(sp.dma_start(to, of))
        loads[-1].then_inc(loaded, 16)

    with ExitStack() as ctx:
        b2 = k.sb(ctx, "expert_b2_sb", [E, CTRL])
        rest = k.sb(ctx, "b2_rest", [E, CTRL])
        back = k.sb(ctx, "b2_back", [E, CTRL])
        part = k.sb(ctx, "b2_parts", [E, 3, CTRL], BF16)
        with nc.Block() as block:
            @block.sync
            def _(sp):
                sp.wait_ge(order, 3)
                load(sp, b2[:, :], d["L1_ffn_expert_b2"])
                for kt in range(2):
                    rows = slice(kt * P, (kt + 1) * P)
                    load(sp, g.w1[:, kt, 0:E * EH].rearrange("p (e h) -> p e h", h=EH),
                         d["L1_ffn_expert_w1"][:, rows, :].rearrange("e p h -> p e h"))
                    load(sp, g.w1s[:, kt, 0:EH], d["L1_ffn_shared_w1"][rows, :])
                load(sp, g.w2[:, :, :], d["L1_ffn_expert_w2"].rearrange("(q t) h c -> (t h) q c", t=2))
                load(sp, g.w2s[0:EH, 0:CTRL], d["L1_ffn_shared_w2"])
                load(sp, g.w2s[ONE:ONE + 1, 0:CTRL], row(d["L1_ffn_shared_b2"]))
                for q in range(PAIRS):
                    load(sp, g.b1[:, q:q + 1], d["L1_ffn_expert_b1"][2 * q:2 * q + 2, :].rearrange("t (h a) -> (t h) a", a=1))
                load(sp, g.b1s[0:EH, :], d["L1_ffn_shared_b1"].rearrange("(p a) -> p a", a=1))
                load(sp, g.w1s[:, 0, EH:ONE], d["L1_ffn_halt_w1"])
                load(sp, g.b1s[EH:ONE, :], d["L1_ffn_halt_b1"].rearrange("(p a) -> p a", a=1))
                load(sp, g.w2s[EH:ONE, CTRL:CTRL + 1], d["L1_ffn_halt_w2"])
                load(sp, g.w2s[ONE:ONE + 1, CTRL:CTRL + 1], row(d["L1_ffn_halt_b2"]))
                load(sp, g.rw1[:, :], d["L1_ffn_refine_w1"])
                load(sp, g.rw2[:, :, :], d["L1_ffn_refine_w2"].rearrange("(j p) c -> p j c", p=P))
                for j in range(2):
                    load(sp, g.rb1[:, j:j + 1], d["L1_ffn_refine_b1"][j * P:(j + 1) * P].rearrange("(p a) -> p a", a=1))
                load(sp, g.rb2[:, :], spread(d["L1_ffn_refine_b2"]))
                load(sp, g.iw[:, :], spread(d["L1_ffn_integration_weight"]))
                load(sp, g.mu[:, :], spread(d["L1_ffn_mu"]))
                sp.wait_ge(cut, 3)
                for n in range(3):
                    for s in range(2):
                        at = n * 2 * E + s * E
                        sp.dma_start(g.b2[at:at + E, s, :], part[:, n, :]).then_inc(placed, 16)
                sp.wait_ge(placed, 96)
                sp.wait_ge(loaded, 16 * len(loads))

            @block.vector
            def _(dve):
                nc.vector.memset(g.b2[:, :, :], 0.0).then_inc(order, 1)
                nc.vector.memset(g.w1s[:, :, :], 0.0).then_inc(order, 1)
                nc.vector.memset(g.w2s[:, :], 0.0).then_inc(order, 1)
                for u in range(2):
                    nc.vector.memset(g.hs[u][:, :], 1.0)
                nc.vector.tensor_copy(g.sel[:, :], k.c("sel")[0:2 * E, :])
                dve.wait_ge(loaded, 16 * len(loads))
                nc.vector.tensor_copy(part[:, 0, :], b2[:, :]).then_inc(cut, 1)
                dve.wait_ge(cut, 1)
                c = Chain(dve, order, 3)
                c.link(nc.vector.tensor_copy(back[:, :], part[:, 0, :]))
                c.link(nc.vector.tensor_tensor(rest[:, :], b2[:, :], back[:, :], ALU.subtract))
                nc.vector.tensor_copy(part[:, 1, :], rest[:, :]).then_inc(cut, 1)
                dve.wait_ge(cut, 2)
                c.link(nc.vector.tensor_copy(back[:, :], part[:, 1, :]))
                c.link(nc.vector.tensor_tensor(rest[:, :], rest[:, :], back[:, :], ALU.subtract))
                nc.vector.tensor_copy(part[:, 2, :], rest[:, :]).then_inc(cut, 1)
                dve.wait_ge(cut, 3)


def dynamics_phase(k, g, out):
    nc = k.nc
    ROUNDS = CHUNKS // 2
    Z = k.bank[0]
    HB = k.bank[1:3]
    MB = k.bank[3:5]
    CB = k.bank[5:8]
    Z_PER, H_PER, STEP_H = 10, 24, 5
    m = {n: k.sem(n) for n in (
        "oh_staged", "z_done", "z_read", "hid_done", "hid_ready", "mask_done", "masked", "ctrl_done",
        "ctrl_read", "absb_ready", "exp_ready", "ln_ready", "xm_ready", "state_ready", "order",
        "out_order", "out_ready", "ref_order")}
    stored = [k.sem(f"out_stored{u}") for u in range(2)]

    def z_index(i, what, u, n=0):
        first = isinstance(i, int) and i == 0
        final = isinstance(i, int) and i == ROUNDS - 1
        return {"onehot": i * Z_PER + u - (0 if first else 2), "it1": i * Z_PER + 2 + 2 * u + n,
                "refine": i * Z_PER + (6 if u == 0 else 8 if final else 10) + n}[what]

    def step_hidden(i, n, q):
        shift = 2 if n == 0 and not (isinstance(i, int) and i == 0) else 0
        return i * H_PER + n * STEP_H + q - shift, HB[(n * STEP_H + q) % 2]

    def refine_hidden(i, u, j):
        final = isinstance(i, int) and i == ROUNDS - 1
        at = 4 * STEP_H if u == 0 else (H_PER - 2 if final else H_PER + STEP_H - 2)
        return i * H_PER + at + j, HB[(at + j) % 2]

    def steps_and_refinements(eng, start, step, refine, after_last=lambda: None):
        def body(i):
            start(i)
            step(i, 0)
            if not (isinstance(i, int) and i == 0):
                refine(i - 1, 1)
            for n in range(1, 4):
                step(i, n)
            refine(i, 0)
        rounds(eng, ROUNDS)(body)
        after_last()
        refine(ROUNDS - 1, 1)

    with ExitStack() as ctx:
        def two(n, shape, dt=FP32):
            return [k.sb(ctx, f"{n}{u}", shape, dt) for u in range(2)]
        ohs = two("onehot_copies", [P, CT, P // (2 * E), 2 * E])
        ohT = two("ohT", [6 * E, SEQ], BF16)
        state, vel, xT, vT = two("state", [P, SEQ]), two("vel", [P, SEQ]), two("stateT", [P, SEQ]), two("velT", [P, SEQ])
        hp = two("pair_hidden", [P, SEQ])
        hm = two("masked_hidden", [P, 2, PAIRS, SEQ])
        tt = two("tanh_a_g", [P, 2, 3, SEQ])
        bb = two("ctrl_b", [P, 3, SEQ])
        xm = two("x_minus_mu", [P, SEQ])
        th = two("halt", [P, CT])
        xx = two("x_plus_xf", [P, SEQ])
        L = k.sb(ctx, "softplus", [P, 3, SEQ])
        s1 = k.sb(ctx, "sum_v", [P, SEQ])
        s2 = k.sb(ctx, "sum_g", [P, SEQ])

        def tiles(t):
            return t.rearrange("p (t c) -> p t c", c=P)

        def state_in(i, u, it):
            return tiles_of(g.xf, i * 2 + u) if it == 0 else tiles(state[u][:, :])

        STEPS = [(it, u) for it in range(2) for u in range(2)]

        def each_round(eng):
            return rounds(eng, ROUNDS)

        with nc.Block() as block:
            @block.sync
            def _(sp):
                @each_round(sp)
                def _(i):
                    for u in range(2):
                        to = out[bass.ds(i * 2 + u, 1), :, :].rearrange("s (t p) c -> p (s t) c", p=P)
                        sp.wait_ge(m["out_ready"], i * 2 + u + 1)
                        sp.dma_start(to, tiles(xx[u][:, :])).then_inc(stored[u], 16)
                for u in range(2):
                    sp.wait_ge(stored[u], 16 * ROUNDS)

            @block.gpsimd
            def _(pool):
                def spread_row(t):
                    return t[:, :].unsqueeze(1).to_broadcast([P, CT, P])

                def output(i, u):
                    t = i * 2 + u
                    wait(pool, stored[u], i * 16)
                    nc.gpsimd.tensor_tensor(tiles(xx[u][:, :]), tiles_of(k.x, t), tiles_of(g.xf, t), ALU.add
                                            ).then_inc(m["out_order"], 1)
                    pool.wait_ge(m["z_read"], z_index(i, "refine", u) + 2)
                    ro = tiles(xT[u][:, :])
                    nc.gpsimd.tensor_tensor(ro, ro, spread_row(g.rb2), ALU.add).then_inc(m["out_order"], 1)
                    pool.wait_ge(m["out_order"], t * 3 + 2)
                    nc.gpsimd.tensor_tensor(ro, ro, spread_row(g.iw), ALU.mult).then_inc(m["out_order"], 1)
                    pool.wait_ge(m["out_order"], t * 3 + 3)
                    nc.gpsimd.tensor_tensor(tiles(xx[u][:, :]), tiles(xx[u][:, :]), ro, ALU.add).then_inc(m["out_ready"], 1)

                @each_round(pool)
                def _(i):
                    first = isinstance(i, int) and i == 0
                    if not first:
                        pool.wait_ge(m["z_done"], z_index(i - 1, "it1", 0) + 1)
                    for u in range(2):
                        nc.gpsimd.tensor_copy(ohs[u][:, :, :, :], tiles_of(g.onehot, i * 2 + u).unsqueeze(2).to_broadcast(
                            [P, CT, P // (2 * E), 2 * E])).then_inc(m["oh_staged"], 1)
                    for n, (it, u) in enumerate(STEPS):
                        o = i * 4 + n
                        wait(pool, m["state_ready"], o - 1)
                        nc.gpsimd.tensor_tensor(tiles(xm[u][:, :]), state_in(i, u, it), spread_row(g.mu), ALU.subtract
                                                ).then_inc(m["xm_ready"], 1)
                        if n < 2 and not first:
                            output(i - 1, n)
                output(ROUNDS - 1, 0)
                output(ROUNDS - 1, 1)

            def masks_of(pe, o, q, u):
                for s in range(2):
                    wait(pe, m["masked"], o * 8 + q * 2 + s - 1)
                    nc.tensor.matmul(MB[s][:, :], g.sel[:, (s * PAIRS + q) * P:(s * PAIRS + q + 1) * P],
                                     ohT[u][0:2 * E, :], start=True, stop=True).then_inc(m["mask_done"], 1)

            @block.tensor
            def _(pe):
                def use_z(z):
                    wait(pe, m["z_read"], z)

                def transposed(z, src, ident=None):
                    use_z(z)
                    for j in range(CT):
                        last = nc.tensor.transpose(Z[:, j * P:(j + 1) * P], src[:, j * P:(j + 1) * P], k.ident)
                    last.then_inc(m["z_done"], 1)

                def start(i):
                    for u in range(2):
                        pe.wait_ge(m["oh_staged"], i * 2 + u + 1)
                        use_z(z_index(i, "onehot", u))
                        for j in range(CT):
                            last = nc.tensor.transpose(Z[:, j * P:(j + 1) * P],
                                                       ohs[u][:, j, :, :].rearrange("p n c -> p (n c)"), k.ident)
                        last.then_inc(m["z_done"], 1)

                def step(i, n):
                    (it, u), o = STEPS[n], i * 4 + n
                    if it == 0:
                        moving = [g.xfT[:, bass.ds((i * 2 + u) * SEQ, SEQ)]]
                    else:
                        pe.wait_ge(m["state_ready"], o - 1)
                        z = z_index(i, "it1", u)
                        transposed(z, state[u])
                        transposed(z + 1, vel[u])
                        pe.wait_ge(m["z_read"], z + 2)
                        moving = [xT[u][:, :], vT[u][:, :]]

                    def hidden(q, weights):
                        h, hb = step_hidden(i, n, q)
                        wait(pe, m["hid_ready"], h - 1)
                        for kt, x in enumerate(moving):
                            last = nc.tensor.matmul(hb[:, :], weights[:, kt, :], x,
                                                    start=kt == 0, stop=kt == len(moving) - 1)
                        last.then_inc(m["hid_done"], 1)

                    for q in range(PAIRS):
                        hidden(q, g.w1[:, :, q * P:(q + 1) * P])
                        if q >= 1:
                            masks_of(pe, o, q - 1, u)
                    hidden(4, g.w1s)
                    masks_of(pe, o, PAIRS - 1, u)
                    pe.wait_ge(m["hid_ready"], step_hidden(i, n, STEP_H - 1)[0] + 1)
                    for t in range(CT):
                        cols = slice(t * P, (t + 1) * P)
                        for s in range(3):
                            wait(pe, m["ctrl_read"], o * 12 + t * 3 + s - 2)
                            if s == 0:
                                last = nc.tensor.matmul(CB[s][:, 0:CTRL + 1], g.hs[u][:, cols], g.w2s[:, :],
                                                        start=True, stop=True)
                            else:
                                nc.tensor.matmul(CB[s][:, 0:CTRL], ohT[u][:, cols], g.b2[:, s - 1, :],
                                                 start=True, stop=False)
                                if t == 0 and s == 1:
                                    pe.wait_ge(m["masked"], o * 8 + 8)
                                for q in range(PAIRS):
                                    last = nc.tensor.matmul(CB[s][:, 0:CTRL], hm[u][:, s - 1, q, cols],
                                                            g.w2[:, q, :], start=False, stop=q == PAIRS - 1)
                            last.then_inc(m["ctrl_done"], 1)

                def refine(i, u):
                    pe.wait_ge(m["state_ready"], i * 4 + 2 + u + 1)
                    z = z_index(i, "refine", u)
                    transposed(z, state[u])
                    pe.wait_ge(m["z_read"], z + 1)
                    for j in range(2):
                        h, hb = refine_hidden(i, u, j)
                        wait(pe, m["hid_ready"], h - 1)
                        nc.tensor.matmul(hb[:, :], g.rw1[:, j * P:(j + 1) * P], xT[u][:, :], start=True, stop=True
                                         ).then_inc(m["hid_done"], 1)
                    pe.wait_ge(m["hid_ready"], refine_hidden(i, u, 1)[0] + 1)
                    for t in range(CT):
                        for j in range(2):
                            last = nc.tensor.matmul(Z[:, t * P:(t + 1) * P], hm[u][:, 0, j, t * P:(t + 1) * P],
                                                    g.rw2[:, j, :], start=j == 0, stop=j == 1)
                    last.then_inc(m["z_done"], 1)

                steps_and_refinements(pe, start, step, refine)

            @block.scalar
            def _(act):
                def read_z(z, to, of=Z[:, :]):
                    act.wait_ge(m["z_done"], z + 1)
                    nc.scalar.copy(to, of).then_inc(m["z_read"], 1)

                def softplus(o, u):
                    act.wait_ge(m["absb_ready"], o + 1)
                    nc.scalar.activation(L[:, :, :], L[:, :, :], ACT.Exp).then_inc(m["exp_ready"], 1)
                    act.wait_ge(m["exp_ready"], o + 1)
                    nc.scalar.activation(L[:, :, :], L[:, :, :], ACT.Ln, bias=1.0).then_inc(m["ln_ready"], 1)

                def start(i):
                    for u in range(2):
                        z = z_index(i, "onehot", u)
                        act.wait_ge(m["z_done"], z + 1)
                        nc.scalar.copy(ohT[u][:, :], Z[0:6 * E, :]).then_inc(m["z_read"], 1)

                def step(i, n):
                    (it, u), o = STEPS[n], i * 4 + n
                    if it == 1:
                        if not (isinstance(i, int) and i == 0):
                            act.wait_ge(m["out_ready"], i * 2 - 1 + u)
                        z = z_index(i, "it1", u)
                        read_z(z, xT[u][:, :])
                        read_z(z + 1, vT[u][:, :])

                    def gelu(q, to, rows, bias):
                        h, hb = step_hidden(i, n, q)
                        act.wait_ge(m["hid_done"], h + 1)
                        nc.scalar.activation(to, hb[0:rows, :], ACT.Gelu, bias=bias).then_inc(m["hid_ready"], 1)

                    for q in range(PAIRS):
                        wait(act, m["masked"], o * 8 + 2 * (q - 1))
                        gelu(q, hp[q % 2][:, :], P, g.b1[:, q:q + 1])
                    gelu(4, g.hs[u][0:ONE, :], ONE, g.b1s[:, 0:1])
                    if not (isinstance(o, int) and o == 0):
                        softplus(o - 1, 1 - u)
                    for t in range(CT):
                        cols = slice(t * P, (t + 1) * P)
                        for s in range(3):
                            act.wait_ge(m["ctrl_done"], o * 12 + t * 3 + s + 1)
                            if t == 0 and s == 0:
                                wait(act, m["state_ready"], o - 1)
                            if s == 0:
                                nc.scalar.activation(th[u][:, t:t + 1], CB[s][:, CTRL:CTRL + 1], ACT.Tanh, scale=0.5)
                            nc.scalar.activation(tt[u][:, :, s, cols], CB[s][:, 0:CTRL].rearrange("p (n c) -> p n c", c=P)[:, 0:3:2, :],
                                                 ACT.Tanh, scale=0.5)
                            nc.scalar.copy(bb[u][:, s, cols], CB[s][:, P:2 * P]).then_inc(m["ctrl_read"], 1)

                def refine(i, u):
                    z = z_index(i, "refine", u)
                    read_z(z, xT[u][:, :])
                    for j in range(2):
                        h, hb = refine_hidden(i, u, j)
                        act.wait_ge(m["hid_done"], h + 1)
                        nc.scalar.activation(hm[u][:, 0, j, :], hb[:, :], ACT.Gelu, bias=g.rb1[:, j:j + 1]
                                             ).then_inc(m["hid_ready"], 1)
                    act.wait_ge(m["z_done"], z + 2)
                    nc.scalar.copy(xT[u][:, :], Z[:, :]).then_inc(m["z_read"], 1)

                steps_and_refinements(act, start, step, refine, lambda: softplus(ROUNDS * 4 - 1, 1))

            @block.vector
            def _(dve):
                LINKS = {0: 6, 1: 8}
                PER = 2 * (LINKS[0] + LINKS[1])

                def abs_b(o, u):
                    dve.wait_ge(m["ctrl_read"], o * 12 + 12)
                    wait(dve, m["state_ready"], o)
                    nc.vector.scalar_tensor_tensor(out=L[:, :, :], in0=bb[u][:, :, :], scalar=-1.0, in1=bb[u][:, :, :],
                                                   op0=ALU.mult, op1=ALU.min).then_inc(m["absb_ready"], 1)

                def mask(o, u, hid_base):
                    for q in range(PAIRS):
                        for s in range(2):
                            dve.wait_ge(m["mask_done"], o * 8 + q * 2 + s + 1)
                            if s == 0:
                                dve.wait_ge(m["hid_ready"], hid_base + q + 1)
                            mul(nc, hm[u][:, s, q, :], hp[q % 2][:, :], MB[s][:, :]).then_inc(m["masked"], 1)

                def integrate(i, it, u):
                    o = i * 4 + it * 2 + u
                    c = Chain(dve, m["order"], i * PER + it * 2 * LINKS[0] + u * LINKS[it])
                    a, gg = tt[u][:, 0, :, :], tt[u][:, 1, :, :]
                    weight = g.weight[:, :, bass.ds((i * 2 + u) * CT, CT)].unsqueeze(3).to_broadcast([P, 3, CT, P])

                    def sets(t):
                        return t.rearrange("p s (t c) -> p s t c", c=P)

                    def over_sets(t):
                        return t.unsqueeze(1).to_broadcast([P, 3, SEQ])
                    dve.wait_ge(m["ln_ready"], o + 1)
                    c.link(nc.vector.scalar_tensor_tensor(out=L[:, :, :], in0=bb[u][:, :, :], scalar=0.0, in1=L[:, :, :],
                                                          op0=ALU.max, op1=ALU.add))
                    dve.wait_ge(m["xm_ready"], o + 1)
                    if it == 1:
                        c.mark(nc.vector.scalar_tensor_tensor(out=a, in0=a, scalar=1.0, in1=over_sets(vel[u][:, :]),
                                                              op0=ALU.add, op1=ALU.mult))
                    c.link(mul(nc, L[:, :, :], L[:, :, :], over_sets(xm[u][:, :])))
                    if it == 1:
                        c.link(nc.vector.scalar_tensor_tensor(out=L[:, :, :], in0=L[:, :, :], scalar=-2.0, in1=a,
                                                              op0=ALU.mult, op1=ALU.add))
                    c.link(mul(nc, sets(L[:, :, :]), sets(L[:, :, :]), weight))
                    c.link(nc.vector.scalar_tensor_tensor(out=gg, in0=gg, scalar=1.0, in1=L[:, :, :],
                                                          op0=ALU.add, op1=ALU.mult))
                    factor = -1.0 if it == 0 else 0.5
                    c.link(nc.vector.tensor_tensor(s2[:, :], gg[:, 0, :], gg[:, 1, :], ALU.add))
                    if it == 0:
                        nc.vector.tensor_tensor(s1[:, :], L[:, 0, :], L[:, 1, :], ALU.add)
                    c.link(nc.vector.tensor_scalar(th[u][:, :], th[u][:, :], 0.5, 0.5, ALU.mult, ALU.add))
                    nc.vector.tensor_tensor(s2[:, :], s2[:, :], gg[:, 2, :], ALU.add).then_inc(m["ref_order"], 1)
                    halt = th[u][:, :].unsqueeze(2).to_broadcast([P, CT, P])
                    if it == 0:
                        nc.vector.tensor_tensor(s1[:, :], s1[:, :], L[:, 2, :], ALU.add).then_inc(m["ref_order"], 1)
                    n_ref = (i * 12 + u * 4) if it == 0 else (i * 12 + 8 + u * 2)
                    dve.wait_ge(m["ref_order"], n_ref + (2 if it == 0 else 1))
                    mul(nc, tiles(s2[:, :]), tiles(s2[:, :]), halt).then_inc(m["ref_order"], 1)
                    if it == 0:
                        nc.vector.scalar_tensor_tensor(out=tiles(vel[u][:, :]), in0=tiles(s1[:, :]), scalar=factor,
                                                       in1=halt, op0=ALU.mult, op1=ALU.mult).then_inc(m["ref_order"], 1)
                    dve.wait_ge(m["ref_order"], n_ref + (4 if it == 0 else 2))
                    nc.vector.scalar_tensor_tensor(out=tiles(state[u][:, :]), in0=tiles(s2[:, :]), scalar=factor * DT / 2,
                                                   in1=state_in(i, u, it), op0=ALU.mult, op1=ALU.add
                                                   ).then_inc(m["state_ready"], 1)
                    assert c.n == LINKS[it], (it, c.n)

                @each_round(dve)
                def _(i):
                    for n, (it, u) in enumerate(STEPS):
                        o = i * 4 + n
                        started = not (isinstance(o, int) and o == 0)
                        if started:
                            abs_b(o - 1, 1 - u)
                        mask(o, u, step_hidden(i, n, 0)[0])
                        if started:
                            integrate(i if n else i - 1, *STEPS[n - 1])
                abs_b(ROUNDS * 4 - 1, 1)
                integrate(ROUNDS - 1, *STEPS[3])



def emit(nc, dram, cols, out):
    with ExitStack() as ctx:
        k = Core(nc, ctx, dram)
        k.x = k.sb(ctx, "x_res", [P, TILES, P])
        k.const = k.sb(ctx, "const_sb", list(dram["const"].shape))
        k.zeros = k.sb(ctx, "zeros", [P, 512], BF16)
        k.mean = k.sb(ctx, "mean", [P, TILES])
        k.rstd = k.sb(ctx, "rstd", [P, TILES])
        k.st = k.sb(ctx, "bn_stats_of_x", [P, TILES, 6])

        def const(name):
            a, b = cols[name]
            return k.const[:, a:b]

        k.c = const
        k.ident = const("ident")
        f = lambda: None
        f.sorted_in = nc.dram_tensor("sorted_in", (PADDED * P, P), FP32, kind="Internal").ap()
        load_phase(k, f.sorted_in)
        mean, rstd = k.mean[:, :], k.rstd[:, :]
        statistics_phase(k, "ln1", mean, rstd, k.st, k.x)
        with ExitStack() as ttt:
            k.kT = k.sb(ttt, "kT", [P, TOKENS])
            k.qT = k.sb(ttt, "qT", [P, TOKENS])
            k.vT = k.sb(ttt, "vT", [P, TOKENS])
            k.ktok = k.sb(ttt, "ktok", [P, TILES, P])
            k.theta_gate = k.sb(ttt, "theta_gate", [P, HID])
            k.theta_val = k.sb(ttt, "theta_val", [P, HID])
            k.theta_proj = k.sb(ttt, "theta_proj", [P, HT, P])
            k.theta_projT = k.sb(ttt, "theta_projT", [P, HID])
            qkv_phase(k)
            gradient_phase(k, "grad1")
            muon_phase(k, "muon1")
            gradient_phase(k, "grad2")
            muon_phase(k, "muon2")
            query_phase(k)
        k.clear_semaphores()
        f.sorted_out = nc.dram_tensor("sorted_out", (PADDED * P, P), FP32, kind="Internal").ap()
        with ExitStack() as moe:
            f.xl = k.sb(moe, "xl", [P, TILES, P])
            f.sorted = k.sb(moe, "sorted_tokens", [P, PADDED, P])
            f.ys = k.sb(moe, "expert_outputs", [P, PADDED, P])
            f.mean, f.rstd = k.sb(moe, "sorted_mean", [P, PADDED]), k.sb(moe, "sorted_rstd", [P, PADDED])
            f.st = k.sb(moe, "bn_stats_of_sorted", [P, PADDED, 6])
            f.w1 = k.sb(moe, "w1T", [P, E, HID])
            f.w2 = k.sb(moe, "w2T", [P, E, HID])
            f.b1 = k.sb(moe, "b1_spread", [P, E, HID])
            f.b2 = k.sb(moe, "b2_spread", [P, E, P])
            f.vecT = k.sb(moe, "centroids_g_b_T", [P, 3 * E])
            f.alpha = k.sb(moe, "alpha", [P, TILES])
            f.slot_expert = k.sb(moe, "slot_expert", [P, PADDED], I32)
            f.pos = k.sb(moe, "pos", [P, TILES], U32)
            expert_weights_phase(k, f)
            statistics_phase(k, "ln2", mean, rstd, k.st, k.x)
            affinity_phase(k, f)
            sort_phase(k, f)
            statistics_phase(k, "ln2b", f.mean[:, :], f.rstd[:, :], f.st, f.sorted)
            experts_phase(k, f)
        statistics_phase(k, "ln3", mean, rstd, k.st)
        diagonal_attention_phase(k)
        statistics_phase(k, "ln4", mean, rstd, k.st)
        k.clear_semaphores()
        g = lambda: None
        with ExitStack() as dyn:
            g.xf = k.sb(dyn, "xf", [P, TILES, P])
            g.xfT = k.sb(dyn, "xfT", [P, TOKENS])
            g.onehot = k.sb(dyn, "slot_onehot", [P, TILES, 2 * E])
            g.weight = k.sb(dyn, "control_weight", [P, 3, TILES])
            router_phase(k, g)
            g.w1 = k.sb(dyn, "dyn_w1", [P, 2, E * EH])
            g.w1s = k.sb(dyn, "dyn_w1_shared_halt", [P, 2, P])
            g.w2 = k.sb(dyn, "dyn_w2", [P, PAIRS, CTRL])
            g.w2s = k.sb(dyn, "dyn_w2_shared_halt", [ONE + 1, CTRL + 1])
            g.b1 = k.sb(dyn, "dyn_b1", [P, PAIRS])
            g.b1s = k.sb(dyn, "dyn_b1_shared_halt", [ONE, 1])
            g.b2 = k.sb(dyn, "dyn_b2", [6 * E, 2, CTRL], BF16)
            g.sel = k.sb(dyn, "pair_rows", [2 * E, 2 * PAIRS * P], BF16)
            g.hs = [k.sb(dyn, f"shared_halt_hidden{u}", [ONE + 1, SEQ]) for u in range(2)]
            g.rw1 = k.sb(dyn, "refine_w1", [P, 2 * P])
            g.rw2 = k.sb(dyn, "refine_w2", [P, 2, P])
            g.rb1 = k.sb(dyn, "refine_b1", [P, 2])
            g.rb2 = k.sb(dyn, "refine_b2", [P, P])
            g.iw = k.sb(dyn, "integration_weight", [P, P])
            g.mu = k.sb(dyn, "mu", [P, P])
            dynamics_weights_phase(k, g)
            dynamics_phase(k, g, out)


def kernel(**inputs):
    import concourse.bacc as _bacc
    from concourse.bass_utils import run_bass_kernel_spmd as _run

    nc = _bacc.Bacc("TRN2", target_bir_lowering=False, num_devices=1)
    const, cols = constant_columns()
    arrays = {name: np.ascontiguousarray(a) for name, a in inputs.items()}
    arrays["const"] = const
    dram = {n: nc.dram_tensor(n, a.shape if a.ndim else (1,), mybir.dt.from_np(a.dtype), kind="ExternalInput").ap()
            for n, a in arrays.items()}
    arrays = {n: a.reshape(a.shape or (1,)) for n, a in arrays.items()}
    out = nc.dram_tensor("out", (SEQS, SEQ, P), FP32, kind="ExternalOutput").ap()
    emit(nc, dram, cols, out)
    r = _run(nc, [arrays], core_ids=[0])
    return r.results[0]["out"]
```

```python
from contextlib import ExitStack

import concourse.bass as bass
import numpy as np
from concourse import mybir

FP32 = mybir.dt.float32
BF16 = mybir.dt.bfloat16
F32R = mybir.dt.float32r
I32 = mybir.dt.int32
U32 = mybir.dt.uint32
ALU = mybir.AluOpType
ACT = mybir.ActivationFunctionType
AXX = mybir.AxisListType.X

P = 128
SEQS, SEQ = 8, 512
TOKENS = SEQS * SEQ
TILES = TOKENS // P
CT = SEQ // P
CHUNKS = TOKENS // SEQ
HEADS, HD = 16, 8
LN_EPS = 1e-5
HID = 512
HT = HID // P
E = 8
PADDED = TILES + E - 1
NS_A, NS_B, NS_C = 3.4445, -4.775, 2.0315
NS_ITERS, LR = 5, 0.1
GRAD_SCALE = 2.0 / (TOKENS * P)
EH = 64
PAIRS = E // 2
CTRL = 3 * P
RH = 32
DT = 0.1
ONE = EH + RH


def constant_columns():
    row = np.arange(P)[:, None]
    col = np.arange(P)[None, :]
    sel = np.zeros((P, 2 * PAIRS, P))
    for k in range(2):
        for q in range(PAIRS):
            sel[k * E + 2 * q, k * PAIRS + q, :EH] = 1
            sel[k * E + 2 * q + 1, k * PAIRS + q, EH:] = 1
    starts = np.ones((P, E, TILES))
    starts[:, :, 0] = 0
    parts = {
        "ident": row == col,
        "before": row < col,
        "ones": np.ones((P, P)),
        "headmask": row // HD == col // HD,
        "headtile": (row == col % HD),
        "sel": sel.reshape(P, -1),
        "starts": starts.reshape(P, -1),
        "rank8": np.tile(E - np.arange(E), (P, 1)),
        "tilestart": np.tile(P * np.arange(TILES), (P, 1)),
        "slot": np.tile(np.arange(PADDED), (P, 1)),
    }
    sel = parts.pop("sel").astype(np.float32)
    at, cols, out = 0, {}, []
    for name, a in parts.items():
        a = np.asarray(a, np.float32)
        cols[name] = (at, at + a.shape[1])
        at += a.shape[1]
        out.append(a)
    return np.ascontiguousarray(np.concatenate(out, 1)), np.ascontiguousarray(sel[0:2 * E]), cols


class Chain:

    def __init__(self, eng, sem, base=0):
        self.eng, self.sem, self.base, self.n = eng, sem, base, 0

    def mark(self, ins):
        ins.then_inc(self.sem, 1)
        self.n += 1
        return self.base + self.n

    def link(self, ins):
        self.eng.wait_ge(self.sem, self.mark(ins))


def wait(eng, sem, n):
    if not (isinstance(n, int) and n <= 0):
        eng.wait_ge(sem, n)


def rounds(eng, n):
    def run(body):
        body(0)
        with eng.Fori(1, n) as i:
            body(i)
    return run


def pairs(eng):
    def run(body):
        body(0, 0)
        body(0, 1)
        with eng.Fori(1, CHUNKS // 2) as i:
            body(i, 0)
            body(i, 1)
    return run


class Core:

    def __init__(self, nc, ctx, dram):
        self.nc, self.dram, self.sems = nc, dram, []
        self.bank = [ctx.enter_context(nc.psum_tensor(f"bank{i}", [P, 512], FP32)) for i in range(8)]

    def sb(self, ctx, name, shape, dt=FP32):
        return ctx.enter_context(self.nc.sbuf_tensor(name, shape, dt))

    def sem(self, name):
        self.sems.append(self.nc.alloc_semaphore(name=name))
        return self.sems[-1]

    def clear_semaphores(self):
        self.nc.clear_and_free_semaphores(self.sems)
        self.nc.all_engine_barrier()
        self.sems = []


def mul(nc, out, a, b):
    return nc.vector.tensor_tensor(out, a, b, ALU.mult)


def row(ap):
    return ap.rearrange("(a n) -> a n", a=1)


def spread(ap, n=P):
    return row(ap).to_broadcast([n, ap.shape[0]])


def count_tile(nc, st, src, t):
    return nc.vector.bn_stats(st[:, bass.ds(t, 1), :].rearrange("p a s -> p (a s)"),
                              src[:, bass.ds(t, 1), :].rearrange("p a c -> p (a c)"))


def load_phase(k, clear):
    nc, d = k.nc, k.dram
    loaded, ready, cleared, counted = k.sem("const_loaded"), k.sem("zeros_ready"), k.sem("sorted_cleared"), k.sem("x_counted")
    x_loaded = [k.sem(f"x_loaded{c}") for c in range(CHUNKS)]
    R = 13
    assert PADDED % R == 0
    with ExitStack() as ctx, nc.Block() as block:
        blank = k.sb(ctx, "blank", [P, R * P])

        @block.sync
        def _(sp):
            for c in range(CHUNKS):
                sp.dma_start(k.x[:, c * CT:(c + 1) * CT, :], d["L0_attn_x"][c, :, :].rearrange("(t p) c -> p t c", p=P)
                             ).then_inc(x_loaded[c], 16)
            sp.dma_start(k.const[:, :], d["const"]).then_inc(loaded, 16)
            sp.wait_ge(ready, 2)
            for t in range(0, PADDED, R):
                sp.dma_start(clear[t * P:(t + R) * P, :].rearrange("(p a) c -> p (a c)", p=P), blank[:, :]
                             ).then_inc(cleared, 16)
            sp.wait_ge(cleared, 16 * (PADDED // R))

        @block.vector
        def _(dve):
            dve.memset(blank[:, :], 0.0).then_inc(ready, 1)
            dve.memset(k.zeros[:, :], 0.0).then_inc(ready, 1)
            for c in range(CHUNKS):
                dve.wait_ge(x_loaded[c], 16)
                for j in range(CT):
                    count_tile(nc, k.st, k.x, c * CT + j).then_inc(counted, 1)
            dve.wait_ge(loaded, 16)
            nc.vector.tensor_copy(k.ident_r[:, :], k.ident).then_inc(ready, 1)
            dve.wait_ge(ready, 3)
            dve.wait_ge(counted, TILES)


def statistics_phase(k, name, mean, rstd, st, src=None):
    nc = k.nc
    counted, order = k.sem(f"{name}_rows_counted"), k.sem(f"{name}_order")
    var_ready, std_ready = k.sem(f"{name}_var_ready"), k.sem(f"{name}_std_ready")
    n = mean.shape[1]
    group = n // CHUNKS if n % CHUNKS == 0 else 13
    assert n % group == 0
    with ExitStack() as ctx:
        tmp = k.sb(ctx, f"{name}_tmp", [P, 4, n])
        diff, var, std, fix = (tmp[:, m, :] for m in range(4))
        with nc.Block() as block:
            @block.vector
            def _(dve):
                if src is not None:
                    @rounds(dve, n // group)
                    def _(i):
                        for j in range(group):
                            count_tile(nc, st, src, i * group + j).then_inc(counted, 1)
                    wait(dve, counted, n)
                c = Chain(dve, order)
                c.mark(nc.vector.tensor_tensor(mean, st[:, :, 1], st[:, :, 4], ALU.add))
                c.mark(nc.vector.tensor_tensor(diff, st[:, :, 1], st[:, :, 4], ALU.subtract))
                c.link(nc.vector.tensor_tensor(var, st[:, :, 2], st[:, :, 5], ALU.add))
                c.mark(nc.vector.tensor_scalar(mean, mean, 0.5, None, ALU.mult))
                c.mark(mul(nc, diff, diff, diff))
                c.link(nc.vector.tensor_scalar(var, var, 1.0 / P, LN_EPS, ALU.mult, ALU.add))
                nc.vector.scalar_tensor_tensor(out=var, in0=diff, scalar=0.25, in1=var,
                                               op0=ALU.mult, op1=ALU.add).then_inc(var_ready, 1)
                wait(dve, std_ready, 1)
                c.link(nc.vector.reciprocal(rstd, std))
                c.link(mul(nc, fix, rstd, rstd))
                c.link(mul(nc, fix, fix, var))
                c.link(nc.vector.tensor_scalar(fix, fix, -0.5, 1.5, ALU.mult, ALU.add))
                c.link(mul(nc, rstd, rstd, fix))

            @block.scalar
            def _(act):
                wait(act, var_ready, 1)
                nc.scalar.activation(std, var, ACT.Sqrt).then_inc(std_ready, 1)
                wait(act, std_ready, 1)


def tiles_of(t, i, n=CT):
    return t[:, bass.ds(i * n, n), :]


def per_token(t, i, width=P):
    return t[:, bass.ds(i * CT, CT)].unsqueeze(2).to_broadcast([P, CT, width])


def qkv_phase(k):
    nc, d = k.nc, k.dram
    W_LOADS = 8
    loaded, theta_loaded, xc_ready, ks_ready = (k.sem("qkv_w_loaded"), k.sem("theta_loaded"), k.sem("xc_ready"),
                                                k.sem("k_scaled"))
    xn_ready, xn_transposed, xT_copied = k.sem("xn_ready"), k.sem("xn_transposed"), k.sem("xT_copied")
    qk_done, v_done, v_copied = k.sem("qk_done"), k.sem("v_done"), k.sem("v_copied")
    qk_copied, squared, ss_ready, norm_ready = k.sem("qk_copied"), k.sem("qk_squared"), k.sem("ss_ready"), k.sem("norm_ready")
    unit_ready, unit_transposed, ktok_ready = k.sem("unit_ready"), k.sem("unit_transposed"), k.sem("ktok_ready")
    qT_copied, kT_copied, order_v = k.sem("qT_copied"), k.sem("kT_copied"), k.sem("qkv_dve_order")
    kT_cleared = k.sem("kT_cleared")
    kT_hi, kT_lo, kt_hi, kt_lo = k.sem("kT_high_ready"), k.sem("kT_low_ready"), k.sem("ktok_high_ready"), k.sem("ktok_low_ready")
    head_done, head_copied = k.sem("head_vectors_done"), k.sem("head_vectors_copied")
    G = CT * 2 * HEADS
    with ExitStack() as ctx:
        w = k.sb(ctx, "qkv_w_sb", [P, 3 * P])
        bqk = k.sb(ctx, "qk_bias", [P, 2 * P])
        bv = k.sb(ctx, "v_bias", [P, 1])
        kh = k.sb(ctx, "k_scale_bias", [P, 2, HD])
        hv = k.sb(ctx, "head_vectors", [HD, 4])
        hc = k.sb(ctx, "head_vectors_by_channel", [P, 4])
        xc = k.sb(ctx, "xc", [P, CT, P])
        xn = k.sb(ctx, "xn_chunk", [P, CT, P])
        xT = k.sb(ctx, "xT_chunk", [P, SEQ])
        qk = [k.sb(ctx, f"qk_chunk{a}", [P, CT, 2 * P]) for a in range(2)]
        sq = k.sb(ctx, "qk_squares", [P, CT * 2 * P])
        ss = [k.sb(ctx, f"qk_ss{a}", [P, G]) for a in range(2)]
        nrm = [k.sb(ctx, f"qk_norm{a}", [P, G]) for a in range(2)]
        inv = k.sb(ctx, "qk_inv", [P, G])
        unit = [k.sb(ctx, f"qk_unit{a}", [P, CT, 2 * P]) for a in range(2)]
        ks = k.sb(ctx, "k_scaled", [P, CT, P])
        ktok = [k.sb(ctx, f"k_by_token{a}", [P, CT, P]) for a in range(2)]
        kT = [k.sb(ctx, f"k_by_feature{a}", [P, SEQ]) for a in range(2)]

        def flat(t):
            return t.rearrange("p t c -> p (t c)")

        def part(t, i, n):
            return t[:, bass.ds(i * CT, CT), n, :]

        kT_tiles = [t[:, :].rearrange("p (t c) -> p t c", c=P) for t in kT]

        def heads(t):
            return t.rearrange("p (g e) -> p g e", e=HD)

        def by_head(t):
            return t.rearrange("p t (h e) -> p t h e", e=HD)

        def k_vector(n):
            return kh[:, n:n + 1, :].unsqueeze(1).to_broadcast([P, CT, HEADS, HD])

        def pipelined(eng, cycle, drain):
            for t in range(4):
                cycle(t, t % 2)
            with eng.Fori(2, CHUNKS // 2) as i:
                cycle(i * 2, 0)
                cycle(i * 2 + 1, 1)
            drain()

        def from_cycle(t, n):
            return not (isinstance(t, int) and t < n)

        with nc.Block() as block:
            @block.sync
            def _(sp):
                sp.dma_start(w[:, :], d["L0_attn_qkv_w"]).then_inc(loaded, 16)
                sp.dma_start(bqk[:, :], spread(d["L0_attn_qkv_b"][0:2 * P])).then_inc(loaded, 16)
                sp.dma_start(bv[:, :], d["L0_attn_qkv_b"][2 * P:3 * P].rearrange("(p a) -> p a", a=1)).then_inc(loaded, 16)
                for n, name in enumerate(("qn_scale", "kn_scale", "qn_bias", "kn_bias")):
                    sp.dma_start(hv[:, n:n + 1], d["L0_attn_" + name].rearrange("(p a) -> p a", a=1)).then_inc(loaded, 16)
                sp.dma_start(kh[:, 0, :], spread(d["L0_attn_kn_scale"])).then_inc(loaded, 16)
                sp.dma_start(kh[:, 1, :], spread(d["L0_attn_kn_bias"])).then_inc(loaded, 16)
                sp.dma_start(k.theta_gate[:, :], d["L0_attn_ttt_gate"]).then_inc(theta_loaded, 16)
                sp.dma_start(k.theta_val[:, :], d["L0_attn_ttt_val"]).then_inc(theta_loaded, 16)
                sp.dma_start(k.theta_proj[:, :, :], d["L0_attn_ttt_proj"].rearrange("(j p) c -> p j c", p=P)
                             ).then_inc(theta_loaded, 16)
                wait(sp, theta_loaded, 48)

            @block.gpsimd
            def _(pool):
                def finish_k(i, a):
                    wait(pool, unit_ready, i + 1)
                    wait(pool, ktok_ready, i)
                    nc.gpsimd.tensor_tensor(by_head(ks[:, :, :]), by_head(unit[a][:, :, P:2 * P]), k_vector(0), ALU.mult
                                            ).then_inc(ks_ready, 1)
                    wait(pool, ks_ready, i + 1)
                    wait(pool, kt_lo, i - 1)
                    nc.gpsimd.tensor_tensor(by_head(ktok[a][:, :, :]), by_head(ks[:, :, :]), k_vector(1), ALU.add
                                            ).then_inc(ktok_ready, 1)

                def cycle(t, a):
                    wait(pool, xn_ready, t)
                    nc.gpsimd.tensor_tensor(xc[:, :, :], tiles_of(k.x, t), per_token(k.mean, t), ALU.subtract
                                            ).then_inc(xc_ready, 1)
                    wait(pool, xc_ready, t + 1)
                    wait(pool, xn_transposed, t)
                    nc.gpsimd.tensor_tensor(xn[:, :, :], xc[:, :, :], per_token(k.rstd, t), ALU.mult
                                            ).then_inc(xn_ready, 1)
                    if from_cycle(t, 2):
                        finish_k(t - 2, a)

                wait(pool, loaded, 16 * (W_LOADS + 1))

                def drain():
                    finish_k(CHUNKS - 2, 0)
                    finish_k(CHUNKS - 1, 1)
                pipelined(pool, cycle, drain)

            @block.tensor
            def _(pe):
                def front(i):
                    wait(pe, xn_ready, i + 1)
                    wait(pe, xT_copied, i)
                    for j in range(CT):
                        last = nc.tensor.transpose(k.bank[0][:, j * P:(j + 1) * P], xn[:, j, :], k.ident)
                    last.then_inc(xn_transposed, 1)
                    wait(pe, xT_copied, i + 1)
                    wait(pe, qk_copied, 2 * i)
                    for j in range(CT):
                        last = nc.tensor.matmul(k.bank[1 + j // 2][:, (j % 2) * 2 * P:(j % 2 + 1) * 2 * P],
                                                xT[:, j * P:(j + 1) * P], w[:, 0:2 * P], start=True, stop=True)
                        if j % 2:
                            last.then_inc(qk_done, 1)
                    wait(pe, v_copied, i)
                    nc.tensor.matmul(k.bank[3][:, :], w[:, 2 * P:3 * P], xT[:, :], start=True, stop=True).then_inc(v_done, 1)

                def back(i, a):
                    wait(pe, unit_ready, i + 1)
                    for n, copied in ((0, qT_copied), (1, kT_copied)):
                        wait(pe, copied, i)
                        for j in range(CT):
                            last = nc.tensor.transpose(k.bank[4 + n][:, j * P:(j + 1) * P],
                                                       unit[a][:, j, n * P:(n + 1) * P], k.ident)
                        last.then_inc(unit_transposed, 1)

                wait(pe, loaded, 16 * (W_LOADS + 1))
                nc.tensor.matmul(k.bank[6][:, 0:4], k.c("headtile")[0:HD, :], hv[:, :], start=True, stop=True
                                 ).then_inc(head_done, 1)

                def cycle(t, a):
                    front(t)
                    if from_cycle(t, 2):
                        back(t - 2, a)

                def drain():
                    back(CHUNKS - 2, 0)
                    back(CHUNKS - 1, 1)
                pipelined(pe, cycle, drain)
                wait(pe, theta_loaded, 48)
                for j in range(HT):
                    last = nc.tensor.transpose(k.bank[7][:, j * P:(j + 1) * P], k.theta_proj[:, j, :], k.ident)
                last.then_inc(head_done, 1)

            @block.scalar
            def _(act):
                def front(i, a):
                    wait(act, xn_transposed, i + 1)
                    wait(act, v_done, i)
                    nc.scalar.copy(xT[:, :], k.bank[0][:, :]).then_inc(xT_copied, 1)
                    wait(act, v_done, i + 1)
                    nc.scalar.activation(k.vT[:, bass.ds(i * SEQ, SEQ)], k.bank[3][:, :], ACT.Identity,
                                         bias=bv[:, 0:1]).then_inc(v_copied, 1)
                    wait(act, qk_copied, 2 * i + 2)
                    wait(act, ss_ready, i)
                    nc.scalar.activation(sq[:, :], flat(qk[a][:, :, :]), ACT.Square).then_inc(squared, 1)

                def root(i, a):
                    wait(act, ss_ready, i + 1)
                    nc.scalar.activation(nrm[a][:, :], ss[a][:, :], ACT.Sqrt).then_inc(norm_ready, 1)

                def back(i, a):
                    for n, to, copied in ((0, k.qT[:, bass.ds(i * SEQ, SEQ)], qT_copied), (1, kT[a][:, :], kT_copied)):
                        wait(act, unit_transposed, 2 * i + n + 1)
                        if n:
                            wait(act, kT_lo, i - 1)
                        nc.scalar.activation(to, k.bank[4 + n][:, :], ACT.Identity,
                                             scale=hc[:, n:n + 1], bias=hc[:, n + 2:n + 3]).then_inc(copied, 1)
                    wait(act, kT_copied, i + 1)
                    nc.scalar.copy(part(k.kT, i, 0), kT_tiles[a]).then_inc(kT_hi, 1)
                    wait(act, ktok_ready, i + 1)
                    nc.scalar.copy(part(k.ktok, i, 0), ktok[a][:, :, :]).then_inc(kt_hi, 1)

                wait(act, loaded, 16 * (W_LOADS + 1))
                wait(act, head_done, 1)
                nc.scalar.copy(hc[:, :], k.bank[6][:, 0:4]).then_inc(head_copied, 1)
                wait(act, head_copied, 1)

                def cycle(t, a):
                    front(t, a)
                    if from_cycle(t, 2):
                        back(t - 2, a)
                    root(t, a)

                def drain():
                    back(CHUNKS - 2, 0)
                    back(CHUNKS - 1, 1)
                pipelined(act, cycle, drain)
                wait(act, head_done, 2)
                nc.scalar.copy(k.theta_projT[:, :], k.bank[7][:, :]).then_inc(head_copied, 1)
                wait(act, head_copied, 2)

            @block.vector
            def _(dve):
                nc.vector.memset(k.qT[:, TOKENS:], 0.0).then_inc(kT_cleared, 1)
                nc.vector.memset(k.kT[:, TILES, :, :].bitcast(FP32), 0.0).then_inc(kT_cleared, 1)
                wait(dve, loaded, 16 * (W_LOADS + 1))
                LINKS = 6

                def low_parts(i, a):
                    wait(dve, kT_hi, i + 1)
                    nc.vector.tensor_tensor(part(k.kT, i, 1), kT_tiles[a], part(k.kT, i, 0), ALU.subtract).then_inc(kT_lo, 1)
                    wait(dve, kt_hi, i + 1)
                    nc.vector.tensor_tensor(part(k.ktok, i, 1), ktok[a][:, :, :], part(k.ktok, i, 0), ALU.subtract
                                            ).then_inc(kt_lo, 1)

                def normalise(i, a):
                    c = Chain(dve, order_v, i * LINKS)
                    wait(dve, norm_ready, i + 1)
                    c.link(nc.vector.tensor_scalar(inv[:, :], nrm[a][:, :], 1e-30, None, ALU.max))
                    c.link(nc.vector.reciprocal(inv[:, :], inv[:, :]))
                    c.link(mul(nc, inv[:, :], inv[:, :], ss[a][:, :]))
                    c.link(nc.vector.tensor_tensor(inv[:, :], inv[:, :], nrm[a][:, :], ALU.add))
                    c.link(nc.vector.tensor_scalar(inv[:, :], inv[:, :], 0.5, 1e-6, ALU.mult, ALU.add))
                    c.link(nc.vector.reciprocal(inv[:, :], inv[:, :]))
                    assert c.n == LINKS
                    wait(dve, unit_transposed, 2 * (i - 1))
                    wait(dve, ks_ready, i - 1)
                    mul(nc, heads(flat(unit[a][:, :, :])), heads(flat(qk[a][:, :, :])),
                        inv[:, :].unsqueeze(2).to_broadcast([P, G, HD])).then_inc(unit_ready, 1)

                def cycle(t, a):
                    wait(dve, unit_ready, t - 1)
                    for h in range(2):
                        wait(dve, qk_done, 2 * t + h + 1)
                        nc.vector.tensor_tensor(qk[a][:, 2 * h:2 * h + 2, :],
                                                k.bank[1 + h][:, :].rearrange("p (j c) -> p j c", j=2),
                                                bqk[:, :].unsqueeze(1).to_broadcast([P, 2, 2 * P]), ALU.add
                                                ).then_inc(qk_copied, 1)
                    if from_cycle(t, 1):
                        normalise(t - 1, 1 - a)
                    wait(dve, squared, t + 1)
                    nc.vector.tensor_reduce(ss[a][:, :], heads(sq[:, :]), AXX, ALU.add).then_inc(ss_ready, 1)
                    if from_cycle(t, 2):
                        low_parts(t - 2, a)

                def drain():
                    normalise(CHUNKS - 1, 1)
                    low_parts(CHUNKS - 2, 0)
                    low_parts(CHUNKS - 1, 1)
                pipelined(dve, cycle, drain)


def product(nc, out, a, b, start=True, stop=True):
    nc.tensor.matmul(out, a[0], b[0], start=start, stop=False)
    nc.tensor.matmul(out, a[1], b[0], start=False, stop=False)
    return nc.tensor.matmul(out, a[0], b[1], start=False, stop=stop)


def gradient_phase(k, name):
    nc = k.nc
    m = {n: k.sem(f"{name}_{n}") for n in (
        "kT_loaded0", "kT_loaded1", "k_loaded0", "k_loaded1", "theta_high", "theta_low", "G_done", "V_done",
        "sig_ready", "V_copied", "s_ready", "h_ready", "h_high", "h_low", "hT_done", "hT_copied", "pred_done", "rT_ready", "rT_high", "rT_low", "r_done", "r_copied", "dh_done",
        "dval_ready", "dval_high", "dval_low", "dgate_ready", "dgate_high", "dgate_low", "order", "dact_ready",
        "dproj_added", "dgate_added", "closed")}
    G_BANK, V_BANK, HT_BANK, R_BANK, DH_BANK, PROJ_BANK, VAL_BANK, GATE_BANK = k.bank
    LAST = TILES - 1
    with ExitStack() as ctx:
        def sb(n, shape, dt=FP32):
            return k.sb(ctx, f"{name}_{n}", shape, dt)

        def two(n, shape, dt=FP32):
            return [sb(f"{n}{a}", shape, dt) for a in range(2)]
        gate_w, val_w, projT_w = (sb(n, [P, 2, HID], F32R) for n in ("gate_hl", "val_hl", "projT_hl"))
        kT, kt = two("kT", [P, 2, P], F32R), two("k", [P, 2, P], F32R)
        sig, s, hv = (two(n, [P, HID]) for n in ("sig", "s", "hv"))
        h = sb("h", [P, HID])
        hp = two("h_hl", [P, 2, HID], F32R)
        hT = sb("hT", [P, HID])
        rT = sb("rT", [P, P])
        rTp, rp = sb("rT_hl", [P, 2, P], F32R), sb("r_hl", [P, 2, P], F32R)
        u, dact = sb("u", [P, HID]), sb("dact", [P, HID])
        dval, dgate = sb("dval", [P, HID]), sb("dgate", [P, HID])
        dvalp, dgatep = sb("dval_hl", [P, 2, HID], F32R), sb("dgate_hl", [P, 2, HID], F32R)
        ident = k.ident_r[:, :]
        thetas = ((gate_w, k.theta_gate[:, :]), (val_w, k.theta_val[:, :]), (projT_w, k.theta_projT[:, :]))

        def hl(t, cols=slice(None)):
            return [t[:, n, cols] for n in range(2)]

        def cycles(eng, cycle):
            cycle(0, 0, False, True)
            cycle(1, 1, True, True)
            cycle(2, 0, True, True)
            with eng.Fori(1, (TILES - 2) // 2) as i:
                cycle(i * 2 + 1, 1, True, True)
                cycle(i * 2 + 2, 0, True, True)
            cycle(LAST, 1, True, False)

        with nc.Block() as block:
            @block.sync
            def _(sp):
                def tile(of, t):
                    return of[:, :, :, :].bitcast(FP32).rearrange("p t n c -> p (t n c)")[:, bass.ds(t * 2 * P, 2 * P)]

                def parts(to):
                    return to[:, :, :].bitcast(FP32).rearrange("p n c -> p (n c)")

                def cycle(t, a, before, after):
                    source = tile(k.ktok, t)
                    if not (isinstance(t, int) and t < 2):
                        sp.wait_ge(m["dgate_added"], t - 1)
                    sp.dma_start(parts(kt[a]), source).then_inc(m[f"k_loaded{a}"], 16)
                    if after:
                        source = tile(k.kT, t + 2)
                        sp.wait_ge(m["V_done"], t + 1)
                        sp.dma_start(parts(kT[a]), source).then_inc(m[f"kT_loaded{a}"], 16)

                for a in range(2):
                    sp.dma_start(parts(kT[a]), tile(k.kT, a)).then_inc(m[f"kT_loaded{a}"], 16)
                cycles(sp, cycle)

            @block.gpsimd
            def _(pool):
                def cut_dval(t):
                    pool.wait_ge(m["dval_high"], t + 1)
                    nc.gpsimd.tensor_tensor(dvalp[:, 1, :], dval[:, :], dvalp[:, 0, :], ALU.subtract).then_inc(m["dval_low"], 1)

                def cut_dgate(t):
                    pool.wait_ge(m["dgate_high"], t + 1)
                    nc.gpsimd.tensor_tensor(dgatep[:, 1, :], dgate[:, :], dgatep[:, 0, :], ALU.subtract
                                            ).then_inc(m["dgate_low"], 1)

                def cut_h(t, a):
                    pool.wait_ge(m["h_high"], t + 1)
                    nc.gpsimd.tensor_tensor(hp[a][:, 1, :], h[:, :], hp[a][:, 0, :], ALU.subtract).then_inc(m["h_low"], 1)

                def cycle(t, a, before, after):
                    if before:
                        cut_dval(t - 1)
                        cut_dgate(t - 1)
                    if after:
                        cut_h(t + 1, 1 - a)

                cut_h(0, 0)
                cycles(pool, cycle)
                cut_dval(LAST)
                cut_dgate(LAST)

            @block.tensor
            def _(pe):
                def open_or_close(start):
                    for b in (PROJ_BANK, VAL_BANK, GATE_BANK):
                        last = nc.tensor.matmul(b[:, :], k.zeros[:, 0:P], k.zeros[:, :], start=start, stop=not start)
                    return last

                def loads_of(t, a):
                    return (t - a) * 8 + 16

                def gate(t, a):
                    pe.wait_ge(m[f"kT_loaded{a}"], loads_of(t, a))
                    wait(pe, m["s_ready"], t)
                    product(nc, G_BANK[:, :], hl(kT[a]), hl(gate_w)).then_inc(m["G_done"], 1)

                def val(t, a):
                    wait(pe, m["V_copied"], t)
                    product(nc, V_BANK[:, :], hl(kT[a]), hl(val_w)).then_inc(m["V_done"], 1)

                def sum_proj(t, a):
                    pe.wait_ge(m["r_copied"], t + 1)
                    pe.wait_ge(m["h_low"], t + 1)
                    product(nc, PROJ_BANK[:, :], hl(rp), hl(hp[a]), False, False).then_inc(m["dproj_added"], 1)

                def sum_val(t, a):
                    pe.wait_ge(m[f"k_loaded{a}"], loads_of(t, a))
                    pe.wait_ge(m["dval_low"], t + 1)
                    product(nc, VAL_BANK[:, :], hl(kt[a]), hl(dvalp), False, False)

                def sum_gate(t, a):
                    pe.wait_ge(m["dgate_low"], t + 1)
                    product(nc, GATE_BANK[:, :], hl(kt[a]), hl(dgatep), False, False).then_inc(m["dgate_added"], 1)

                def cycle(t, a, before, after):
                    pe.wait_ge(m["h_ready"], t + 1)
                    wait(pe, m["hT_copied"], t)
                    for j in range(HT):
                        cols = slice(j * P, (j + 1) * P)
                        x = nc.tensor.transpose(HT_BANK[:, cols], h[:, cols], k.ident)
                    x.then_inc(m["hT_done"], 1)
                    if after:
                        gate(t + 1, 1 - a)
                        val(t + 1, 1 - a)
                    if before:
                        sum_proj(t - 1, 1 - a)
                    pe.wait_ge(m["hT_copied"], t + 1)
                    wait(pe, m["r_copied"], t)
                    for j in range(HT):
                        x = nc.tensor.matmul(R_BANK[:, 0:P], k.theta_proj[:, j, :], hT[:, j * P:(j + 1) * P],
                                             start=j == 0, stop=j == HT - 1)
                    x.then_inc(m["pred_done"], 1)
                    if before:
                        sum_val(t - 1, 1 - a)
                        sum_gate(t - 1, 1 - a)
                    pe.wait_ge(m["rT_low"], t + 1)
                    for n in range(2):
                        x = nc.tensor.transpose(R_BANK[:, (n + 1) * P:(n + 2) * P].bitcast(F32R), rTp[:, n, :], ident)
                    x.then_inc(m["r_done"], 1)
                    wait(pe, m["dgate_ready"], t)
                    product(nc, DH_BANK[:, :], hl(rTp), hl(projT_w)).then_inc(m["dh_done"], 1)

                open_or_close(True)
                pe.wait_ge(m["theta_low"], len(thetas))
                gate(0, 0)
                val(0, 0)
                cycles(pe, cycle)
                sum_proj(LAST, 1)
                sum_val(LAST, 1)
                sum_gate(LAST, 1)
                open_or_close(False).then_inc(m["closed"], 1)
                wait(pe, m["closed"], 1)

            @block.scalar
            def _(act):
                def high_dval(t):
                    act.wait_ge(m["dval_ready"], t + 1)
                    nc.scalar.copy(dvalp[:, 0, :], dval[:, :]).then_inc(m["dval_high"], 1)

                def high_dgate(t):
                    act.wait_ge(m["dgate_ready"], t + 1)
                    nc.scalar.copy(dgatep[:, 0, :], dgate[:, :]).then_inc(m["dgate_high"], 1)

                def gate(t, a, old):
                    act.wait_ge(m["G_done"], t + 1)
                    if old:
                        act.wait_ge(m["dact_ready"], t - 1)
                    nc.scalar.activation(sig[a][:, :], G_BANK[:, :], ACT.Sigmoid).then_inc(m["sig_ready"], 1)

                def hidden(t, a, old):
                    act.wait_ge(m["V_done"], t + 1)
                    nc.scalar.copy(hv[a][:, :], V_BANK[:, :]).then_inc(m["V_copied"], 1)
                    if old:
                        act.wait_ge(m["dproj_added"], t - 1)
                    act.wait_ge(m["h_ready"], t + 1)
                    nc.scalar.copy(hp[a][:, 0, :], h[:, :]).then_inc(m["h_high"], 1)

                def cycle(t, a, before, after):
                    act.wait_ge(m["hT_done"], t + 1)
                    wait(act, m["pred_done"], t)
                    nc.scalar.copy(hT[:, :], HT_BANK[:, :]).then_inc(m["hT_copied"], 1)
                    if before:
                        if not (isinstance(t, int) and t < 2):
                            act.wait_ge(m["dgate_added"], t - 1)
                        high_dval(t - 1)
                    if after:
                        gate(t + 1, 1 - a, before)
                    if before:
                        high_dgate(t - 1)
                    if after:
                        hidden(t + 1, 1 - a, before)
                    act.wait_ge(m["r_done"], t + 1)
                    wait(act, m["dproj_added"], t)
                    nc.scalar.copy(rp[:, :, :].rearrange("p n c -> p (n c)"), R_BANK[:, P:3 * P].bitcast(F32R)
                                   ).then_inc(m["r_copied"], 1)

                for to, x in thetas:
                    nc.scalar.copy(to[:, 0, :], x).then_inc(m["theta_high"], 1)
                gate(0, 0, False)
                hidden(0, 0, False)
                cycles(act, cycle)
                high_dval(LAST)
                high_dgate(LAST)

            @block.vector
            def _(dve):
                def activate(t, a):
                    dve.wait_ge(m["sig_ready"], t + 1)
                    mul(nc, s[a][:, :], G_BANK[:, :], sig[a][:, :]).then_inc(m["s_ready"], 1)

                def hidden(t, a):
                    dve.wait_ge(m["V_copied"], t + 1)
                    dve.wait_ge(m["s_ready"], t + 1)
                    wait(dve, m["h_low"], t)
                    wait(dve, m["hT_done"], t)
                    mul(nc, h[:, :], s[a][:, :], hv[a][:, :]).then_inc(m["h_ready"], 1)

                def backward(t, a):
                    dve.wait_ge(m["dh_done"], t + 1)
                    wait(dve, m["dval_low"], t)
                    mul(nc, dval[:, :], DH_BANK[:, :], s[a][:, :]).then_inc(m["dval_ready"], 1)
                    dve.wait_ge(m["dact_ready"], t + 1)
                    wait(dve, m["dgate_low"], t)
                    mul(nc, dgate[:, :], DH_BANK[:, :], dact[:, :]).then_inc(m["dgate_ready"], 1)

                def cycle(t, a, before, after):
                    if before:
                        backward(t - 1, 1 - a)
                    wait(dve, m["dact_ready"], t)
                    nc.vector.scalar_tensor_tensor(out=u[:, :], in0=sig[a][:, :], scalar=1.0, in1=s[a][:, :],
                                                   op0=ALU.subtract, op1=ALU.mult).then_inc(m["order"], 1)
                    if after:
                        activate(t + 1, 1 - a)
                    dve.wait_ge(m["order"], t * 2 + 1)
                    nc.vector.tensor_tensor(u[:, :], sig[a][:, :], u[:, :], ALU.subtract).then_inc(m["order"], 1)
                    if after:
                        hidden(t + 1, 1 - a)
                    dve.wait_ge(m["pred_done"], t + 1)
                    wait(dve, m["rT_low"], t)
                    nc.vector.tensor_tensor(rT[:, :], R_BANK[:, 0:P], k.vT[:, bass.ds(t * P, P)], ALU.subtract
                                            ).then_inc(m["rT_ready"], 1)
                    dve.wait_ge(m["rT_ready"], t + 1)
                    wait(dve, m["dh_done"], t)
                    nc.vector.tensor_copy(rTp[:, 0, :], rT[:, :]).then_inc(m["rT_high"], 1)
                    dve.wait_ge(m["rT_high"], t + 1)
                    nc.vector.tensor_tensor(rTp[:, 1, :], rT[:, :], rTp[:, 0, :], ALU.subtract).then_inc(m["rT_low"], 1)
                    dve.wait_ge(m["order"], t * 2 + 2)
                    wait(dve, m["dgate_ready"], t)
                    mul(nc, dact[:, :], u[:, :], hv[a][:, :]).then_inc(m["dact_ready"], 1)

                for n, (to, x) in enumerate(thetas):
                    dve.wait_ge(m["theta_high"], n + 1)
                    nc.vector.tensor_tensor(to[:, 1, :], x, to[:, 0, :], ALU.subtract).then_inc(m["theta_low"], 1)
                activate(0, 0)
                hidden(0, 0)
                cycles(dve, cycle)
                backward(LAST, 1)


def muon_phase(k, name):
    nc = k.nc
    grads = [k.bank[7], k.bank[6], k.bank[5]]
    xbank = [k.bank[0], k.bank[1], k.bank[2]]
    tbank = [k.bank[3], k.bank[4], k.bank[5]]
    M = 3
    m = {n: k.sem(f"{name}_{n}") for n in (
        "grad_copied", "squares_summed", "total_done", "norm_ready", "scaled", "xT_first", "xT_copied",
        "A_done", "A_copied", "AA_done", "poly_ready", "X_done", "X_copied", "XT_done", "order", "scaled_A",
        "updated")}
    with ExitStack() as ctx:
        X = [k.sb(ctx, f"{name}_X{n}", [P, HID]) for n in range(M)]
        XT = [k.sb(ctx, f"{name}_XT{n}", [P, HID]) for n in range(M)]
        A = [k.sb(ctx, f"{name}_A{n}", [P, P]) for n in range(M)]
        poly = [k.sb(ctx, f"{name}_poly{n}", [P, P]) for n in range(M)]
        aI = k.sb(ctx, f"{name}_aI", [P, P])
        squares = k.sb(ctx, f"{name}_squares", [P, HID])
        ssq = k.sb(ctx, f"{name}_ssq", [P, M])
        tot = k.sb(ctx, f"{name}_tot", [P, M])
        nrm = k.sb(ctx, f"{name}_nrm", [P, M])
        inv = k.sb(ctx, f"{name}_inv", [P, M])
        with nc.Block() as block:
            @block.tensor
            def _(pe):
                wait(pe, m["squares_summed"], M)
                nc.tensor.matmul(xbank[0][:, 0:M], k.c("ones"), ssq[:, :], start=True, stop=True
                                 ).then_inc(m["total_done"], 1)
                for n in range(M):
                    wait(pe, m["scaled"], n + 1)
                    for j in range(HT):
                        last = nc.tensor.transpose(tbank[n][:, j * P:(j + 1) * P], X[n][:, j * P:(j + 1) * P], k.ident)
                    last.then_inc(m["XT_done"], 1)
                @rounds(pe, NS_ITERS)
                def _(i):
                    for n in range(M):
                        wait(pe, m["xT_copied"], i * M + n + 1)
                        wait(pe, m["X_copied"], i * M)
                        for j in range(HT):
                            xt = XT[n][:, j * P:(j + 1) * P]
                            last = nc.tensor.matmul(xbank[n][:, 0:P], xt, xt, start=j == 0, stop=j == HT - 1)
                        last.then_inc(m["A_done"], 1)
                    for n in range(M):
                        wait(pe, m["A_copied"], i * M + n + 1)
                        nc.tensor.matmul(xbank[n][:, P:2 * P], A[n][:, :], A[n][:, :], start=True, stop=True
                                         ).then_inc(m["AA_done"], 1)
                    for n in range(M):
                        wait(pe, m["poly_ready"], i * M + n + 1)
                        for j in range(HT):
                            last = nc.tensor.matmul(tbank[n][:, j * P:(j + 1) * P], X[n][:, j * P:(j + 1) * P],
                                                    poly[n][:, :], start=True, stop=True)
                        last.then_inc(m["XT_done"], 1)
                        nc.tensor.matmul(xbank[n][:, :], poly[n][:, :], X[n][:, :], start=True, stop=True
                                         ).then_inc(m["X_done"], 1)

            @block.scalar
            def _(act):
                for n in range(M):
                    nc.scalar.copy(X[n][:, :], grads[n][:, :]).then_inc(m["grad_copied"], 1)
                for n in range(M):
                    wait(act, m["grad_copied"], n + 1)
                    if n:
                        wait(act, m["squares_summed"], n)
                    nc.scalar.activation(squares[:, :], X[n][:, :], ACT.Square, accum_out=ssq[:, n:n + 1]
                                         ).then_inc(m["squares_summed"], 1)
                wait(act, m["total_done"], 1)
                nc.scalar.copy(tot[:, :], xbank[0][:, 0:M]).then_inc(m["order"], 1)
                wait(act, m["order"], 1)
                nc.scalar.activation(nrm[:, :], tot[:, :], ACT.Sqrt).then_inc(m["norm_ready"], 1)
                for n in range(M):
                    wait(act, m["XT_done"], n + 1)
                    nc.scalar.copy(XT[n][:, :], tbank[n][:, :]).then_inc(m["xT_copied"], 1)
                @rounds(act, NS_ITERS)
                def _(i):
                    for n in range(M):
                        wait(act, m["XT_done"], (i + 1) * M + n + 1)
                        nc.scalar.copy(XT[n][:, :], tbank[n][:, :]).then_inc(m["xT_copied"], 1)
                wait(act, m["xT_copied"], (NS_ITERS + 1) * M)

            @block.vector
            def _(dve):
                nc.vector.tensor_scalar(aI[:, :], k.ident, NS_A, None, ALU.mult).then_inc(m["scaled_A"], 1)
                wait(dve, m["norm_ready"], 1)
                c = Chain(dve, m["updated"])
                c.link(nc.vector.tensor_scalar(inv[:, :], nrm[:, :], 1e-30, None, ALU.max))
                c.link(nc.vector.reciprocal(inv[:, :], inv[:, :]))
                c.link(mul(nc, inv[:, :], inv[:, :], tot[:, :]))
                c.link(nc.vector.tensor_tensor(inv[:, :], inv[:, :], nrm[:, :], ALU.add))
                c.link(nc.vector.tensor_scalar(inv[:, :], inv[:, :], 0.5, 1e-7 / GRAD_SCALE, ALU.mult, ALU.add))
                c.link(nc.vector.reciprocal(inv[:, :], inv[:, :]))
                for n in range(M):
                    nc.vector.tensor_scalar(X[n][:, :], X[n][:, :], inv[:, n:n + 1], None, ALU.mult
                                            ).then_inc(m["scaled"], 1)
                wait(dve, m["scaled"], M)
                @rounds(dve, NS_ITERS)
                def _(i):
                    for n in range(M):
                        wait(dve, m["A_done"], i * M + n + 1)
                        nc.vector.tensor_copy(A[n][:, :], xbank[n][:, 0:P]).then_inc(m["A_copied"], 1)
                    for n in range(M):
                        wait(dve, m["A_copied"], i * M + n + 1)
                        nc.vector.scalar_tensor_tensor(out=poly[n][:, :], in0=A[n][:, :], scalar=NS_B, in1=aI[:, :],
                                                       op0=ALU.mult, op1=ALU.add).then_inc(m["scaled_A"], 1)
                        wait(dve, m["scaled_A"], i * M + n + 2)
                        wait(dve, m["AA_done"], i * M + n + 1)
                        nc.vector.scalar_tensor_tensor(out=poly[n][:, :], in0=xbank[n][:, P:2 * P], scalar=NS_C,
                                                       in1=poly[n][:, :], op0=ALU.mult, op1=ALU.add
                                                       ).then_inc(m["poly_ready"], 1)
                    for n in range(M):
                        wait(dve, m["X_done"], i * M + n + 1)
                        nc.vector.tensor_copy(X[n][:, :], xbank[n][:, :]).then_inc(m["X_copied"], 1)
                wait(dve, m["X_copied"], NS_ITERS * M)
                wait(dve, m["xT_copied"], (NS_ITERS + 1) * M)
                for theta, step in ((k.theta_gate[:, :], X[0][:, :]), (k.theta_val[:, :], X[1][:, :]),
                                    (k.theta_projT[:, :], X[2][:, :]),
                                    (k.theta_proj[:, :, :].rearrange("p j c -> p (j c)"), XT[2][:, :])):
                    c.mark(nc.vector.scalar_tensor_tensor(out=theta, in0=step, scalar=-LR, in1=theta,
                                                          op0=ALU.mult, op1=ALU.add))
                wait(dve, m["updated"], c.n)


def query_phase(k):
    nc, d = k.nc, k.dram
    loaded, pp_done, pp_copied = k.sem("proj_w_loaded"), k.sem("pp_done"), k.sem("pp_copied")
    theta_high, theta_low, q_high, q_low = k.sem("q_theta_high"), k.sem("q_theta_low"), k.sem("q_high"), k.sem("q_low")
    G_done, V_done, s_ready, hq_ready = k.sem("qG_done"), k.sem("qV_done"), k.sem("qs_ready"), k.sem("hq_ready")
    o_done, xb_ready, x_ready, counted = k.sem("o_done"), k.sem("xb_ready"), k.sem("x1_ready"), k.sem("x1_counted")
    with ExitStack() as ctx:
        pw = k.sb(ctx, "proj_w_sb", [P, P])
        pb = k.sb(ctx, "proj_b_sb", [P, P])
        pp = k.sb(ctx, "proj_proj_w", [P, HT, P])
        gate_w, val_w = (k.sb(ctx, n, [P, 2, HID], F32R) for n in ("q_gate_hl", "q_val_hl"))
        q = [k.sb(ctx, f"q_hl{a}", [P, 2, SEQ], F32R) for a in range(2)]
        s = k.sb(ctx, "q_s", [P, 2, SEQ])
        hq = [k.sb(ctx, f"hq{a}", [P, HT, SEQ]) for a in range(2)]
        xb = k.sb(ctx, "x_plus_b", [P, CT, P])

        def chunk(i):
            return k.qT[:, bass.ds(i * SEQ, SEQ)]

        with nc.Block() as block:
            @block.sync
            def _(sp):
                sp.dma_start(pw[:, :], d["L0_attn_proj_w"]).then_inc(loaded, 16)
                sp.dma_start(pb[:, :], spread(d["L0_attn_proj_b"])).then_inc(loaded, 16)

            @block.tensor
            def _(pe):
                wait(pe, loaded, 32)
                for j in range(HT):
                    last = nc.tensor.matmul(k.bank[0][:, j * P:(j + 1) * P], k.theta_projT[:, j * P:(j + 1) * P],
                                            pw[:, :], start=True, stop=True)
                last.then_inc(pp_done, 1)
                wait(pe, pp_copied, 1)
                pe.wait_ge(theta_low, 2)

                def output(i, a):
                    pe.wait_ge(hq_ready, (i + 1) * HT)
                    wait(pe, x_ready, i)
                    for t in range(CT):
                        for j in range(HT):
                            last = nc.tensor.matmul(k.bank[4][:, t * P:(t + 1) * P], hq[a][:, j, t * P:(t + 1) * P],
                                                    pp[:, j, :], start=j == 0, stop=j == HT - 1)
                    last.then_inc(o_done, 1)

                @pairs(pe)
                def _(i2, a):
                    i = i2 * 2 + a
                    pe.wait_ge(q_low, i + 1)
                    for j in range(HT):
                        cols = slice(j * P, (j + 1) * P)
                        wait(pe, s_ready, i * HT + j - 1)
                        product(nc, k.bank[j % 2][:, :], [gate_w[:, n, cols] for n in range(2)],
                                [q[a][:, n, :] for n in range(2)]).then_inc(G_done, 1)
                        wait(pe, hq_ready, i * HT + j - 1)
                        product(nc, k.bank[2 + j % 2][:, :], [val_w[:, n, cols] for n in range(2)],
                                [q[a][:, n, :] for n in range(2)]).then_inc(V_done, 1)
                        if j == 1 and not (isinstance(i, int) and i == 0):
                            output(i - 1, 1 - a)
                output(CHUNKS - 1, 1)

            @block.scalar
            def _(act):
                def high_q(i, a):
                    wait(act, V_done, (i - 1) * HT)
                    nc.scalar.copy(q[a][:, 0, :], chunk(i)).then_inc(q_high, 1)

                for to, x in ((gate_w, k.theta_gate), (val_w, k.theta_val)):
                    nc.scalar.copy(to[:, 0, :], x[:, :]).then_inc(theta_high, 1)
                high_q(0, 0)
                high_q(1, 1)
                wait(act, pp_done, 1)
                nc.scalar.copy(pp[:, :, :].rearrange("p j c -> p (j c)"), k.bank[0][:, :]).then_inc(pp_copied, 1)

                @pairs(act)
                def _(i2, a):
                    i = i2 * 2 + a
                    for j in range(HT):
                        wait(act, G_done, i * HT + j + 1)
                        wait(act, hq_ready, i * HT + j - 1)
                        nc.scalar.activation(s[:, j % 2, :], k.bank[j % 2][:, :], ACT.Silu).then_inc(s_ready, 1)
                        if j == 1 and not (isinstance(i, int) and i == 0):
                            high_q(i + 1, 1 - a)

            @block.gpsimd
            def _(pool):
                def low_q(i, a):
                    pool.wait_ge(q_high, i + 1)
                    nc.gpsimd.tensor_tensor(q[a][:, 1, :], chunk(i), q[a][:, 0, :], ALU.subtract).then_inc(q_low, 1)

                low_q(0, 0)
                low_q(1, 1)
                wait(pool, loaded, 32)

                @pairs(pool)
                def _(i2, a):
                    i = i2 * 2 + a
                    if not (isinstance(i, int) and i == 0):
                        low_q(i + 1, 1 - a)
                    wait(pool, x_ready, i)
                    nc.gpsimd.tensor_tensor(xb[:, :, :], tiles_of(k.x, i),
                                            pb[:, :].unsqueeze(1).to_broadcast([P, CT, P]), ALU.add
                                            ).then_inc(xb_ready, 1)

            @block.vector
            def _(dve):
                for n, (to, x) in enumerate(((gate_w, k.theta_gate), (val_w, k.theta_val))):
                    dve.wait_ge(theta_high, n + 1)
                    nc.vector.tensor_tensor(to[:, 1, :], x[:, :], to[:, 0, :], ALU.subtract).then_inc(theta_low, 1)

                def add(i):
                    dve.wait_ge(xb_ready, i + 1)
                    dve.wait_ge(o_done, i + 1)
                    nc.vector.tensor_tensor(tiles_of(k.x, i), k.bank[4][:, :].rearrange("p (t c) -> p t c", t=CT),
                                            xb[:, :, :], ALU.add).then_inc(x_ready, 1)
                    dve.wait_ge(x_ready, i + 1)
                    for j in range(CT):
                        count_tile(nc, k.st, k.x, i * CT + j).then_inc(counted, 1)

                @pairs(dve)
                def _(i2, a):
                    i = i2 * 2 + a
                    wait(dve, o_done, i - 1)
                    for j in range(HT):
                        dve.wait_ge(s_ready, i * HT + j + 1)
                        dve.wait_ge(V_done, i * HT + j + 1)
                        mul(nc, hq[a][:, j, :], k.bank[2 + j % 2][:, :], s[:, j % 2, :]).then_inc(hq_ready, 1)
                        if j == 2 and not (isinstance(i, int) and i == 0):
                            add(i - 1)
                add(CHUNKS - 1)
                dve.wait_ge(counted, TILES)


def affinity_phase(k, f):
    nc = k.nc
    order_p, xl_ready, xlT_done, xlT_copied = k.sem("aff_order"), k.sem("xl_ready"), k.sem("xlT_done"), k.sem("xlT_copied")
    xl_kept, aff_done, aff_copied = k.sem("xl_kept"), k.sem("aff_done"), k.sem("aff_copied")
    max_ready, alpha_ready, order_v, count_done = (k.sem("aff_max_ready"), k.sem("alpha_ready"), k.sem("route_order"),
                                                   k.sem("count_done"))
    oh_ready = k.sem("onehot_ready")
    vec_loaded, vecT_done, vecT_copied = k.sem("ln_vectors_loaded"), k.sem("vecT_done"), k.sem("vecT_copied")
    with ExitStack() as ctx:
        vec = k.sb(ctx, "centroids_g_b", [3 * E, P])
        xc = k.sb(ctx, "aff_xc", [P, CT, P])
        xl = [k.sb(ctx, f"aff_xl{a}", [P, CT, P]) for a in range(2)]
        xT = k.sb(ctx, "aff_xT", [P, SEQ])
        aff = k.sb(ctx, "aff", [P, TILES, E])
        oh = k.sb(ctx, "onehot", [P, TILES, E])
        key = k.sb(ctx, "route_key", [P, TILES, E])
        top = k.sb(ctx, "route_max", [P, TILES])
        rank = k.sb(ctx, "route_rank", [P, TILES])
        total = k.sb(ctx, "totals", [P, E, TILES])
        incl = k.sb(ctx, "inclusive", [P, E, TILES])
        cmp = k.sb(ctx, "tile_starts_used", [P, E, TILES])
        ntile = k.sb(ctx, "tiles_of_expert", [P, E])
        ends = k.sb(ctx, "expert_ends", [P, E])
        firsts = k.sb(ctx, "expert_firsts", [P, E])
        pos = k.sb(ctx, "positions", [P, TILES])
        scmp = k.sb(ctx, "slot_compare", [P, PADDED, E - 1])
        sexp = k.sb(ctx, "slot_expert_f", [P, PADDED])
        with nc.Block() as block:
            @block.sync
            def _(sp):
                for n, name in enumerate(("centroids", "ln_g", "ln_b")):
                    sp.dma_start(vec[n * E:(n + 1) * E, :], k.dram["L0_ffn_" + name]).then_inc(vec_loaded, 16)

            @block.gpsimd
            def _(pool):
                @pairs(pool)
                def _(i, a):
                    t = i * 2 + a
                    c = Chain(pool, order_p, t)
                    wait(pool, xl_ready, t)
                    c.link(nc.gpsimd.tensor_tensor(xc[:, :, :], tiles_of(k.x, t), per_token(k.mean, t), ALU.subtract))
                    wait(pool, xlT_done, t - 1)
                    wait(pool, xl_kept, t - 1)
                    nc.gpsimd.tensor_tensor(xl[a][:, :, :], xc[:, :, :], per_token(k.rstd, t), ALU.mult).then_inc(xl_ready, 1)

            @block.scalar
            def _(act):
                act.wait_ge(vecT_done, 1)
                nc.scalar.copy(f.vecT[:, :], k.bank[4][:, 0:3 * E]).then_inc(vecT_copied, 1)

                @pairs(act)
                def _(i, a):
                    t = i * 2 + a
                    act.wait_ge(xlT_done, t + 1)
                    wait(act, aff_done, t)
                    nc.scalar.copy(xT[:, :], k.bank[2][:, :]).then_inc(xlT_copied, 1)
                    nc.scalar.copy(tiles_of(f.xl, t), xl[a][:, :, :]).then_inc(xl_kept, 1)
                act.wait_ge(max_ready, 1)
                nc.scalar.activation(f.alpha[:, :], top[:, :], ACT.Sigmoid).then_inc(alpha_ready, 1)
                act.wait_ge(alpha_ready, 1)
                act.wait_ge(xl_kept, CHUNKS)

            @block.tensor
            def _(pe):
                pe.wait_ge(vec_loaded, 48)
                nc.tensor.transpose(k.bank[4][:, 0:3 * E], vec[:, :], k.ident[0:3 * E, 0:3 * E]).then_inc(vecT_done, 1)
                pe.wait_ge(vecT_copied, 1)

                @pairs(pe)
                def _(i, a):
                    t = i * 2 + a
                    pe.wait_ge(xl_ready, t + 1)
                    wait(pe, xlT_copied, t)
                    for j in range(CT):
                        last = nc.tensor.transpose(k.bank[2][:, j * P:(j + 1) * P], xl[a][:, j, :], k.ident)
                    last.then_inc(xlT_done, 1)
                    pe.wait_ge(xlT_copied, t + 1)
                    wait(pe, aff_copied, t)
                    for j in range(CT):
                        last = nc.tensor.matmul(k.bank[3][:, j * E:(j + 1) * E], xT[:, j * P:(j + 1) * P],
                                                f.vecT[:, 0:E], start=True, stop=True)
                    last.then_inc(aff_done, 1)
                flat = oh[:, :, :].rearrange("p t e -> p (t e)")
                pe.wait_ge(oh_ready, 1)
                nc.tensor.matmul(k.bank[4][:, 0:TILES * E], k.c("before"), flat, start=True, stop=True)
                nc.tensor.matmul(k.bank[5][:, 0:TILES * E], k.c("ones"), flat, start=True, stop=True
                                 ).then_inc(count_done, 1)

            @block.vector
            def _(dve):
                @rounds(dve, CHUNKS)
                def _(i):
                    dve.wait_ge(aff_done, i + 1)
                    nc.vector.tensor_copy(tiles_of(aff, i), k.bank[3][:, 0:CT * E].rearrange("p (t e) -> p t e", e=E)
                                          ).then_inc(aff_copied, 1)
                dve.wait_ge(aff_copied, CHUNKS)

                def over_e(t):
                    return t.unsqueeze(2).to_broadcast([P, TILES, E])
                nc.vector.tensor_reduce(top[:, :], aff[:, :, :], AXX, ALU.max).then_inc(max_ready, 1)
                dve.wait_ge(max_ready, 1)
                c = Chain(dve, order_v)
                rank8 = k.c("rank8").unsqueeze(1).to_broadcast([P, TILES, E])
                c.link(nc.vector.tensor_tensor(key[:, :, :], aff[:, :, :], over_e(top[:, :]), ALU.is_equal))
                c.link(mul(nc, key[:, :, :], key[:, :, :], rank8))
                c.link(nc.vector.tensor_reduce(rank[:, :], key[:, :, :], AXX, ALU.max))
                nc.vector.tensor_tensor(oh[:, :, :], key[:, :, :], over_e(rank[:, :]), ALU.is_equal).then_inc(oh_ready, 1)
                dve.wait_ge(count_done, 1)
                tot_ps = k.bank[5][:, 0:TILES * E].rearrange("p (t e) -> p e t", e=E)
                pre_ps = k.bank[4][:, 0:TILES * E].rearrange("p (t e) -> p t e", e=E)
                c.link(nc.vector.tensor_copy(total[:, :, :], tot_ps))

                def flat(t):
                    return t[:, :, :].rearrange("p e t -> p (e t)")
                c.link(nc.vector.tensor_tensor_scan(flat(incl), k.c("starts"), flat(total), 0.0, ALU.mult, ALU.add))
                c.mark(nc.vector.tensor_tensor(total[:, :, :], incl[:, :, :], total[:, :, :], ALU.subtract))
                c.link(nc.vector.tensor_tensor(cmp[:, :, :], incl[:, :, TILES - 1:TILES].to_broadcast([P, E, TILES]),
                                               k.c("tilestart").unsqueeze(1).to_broadcast([P, E, TILES]), ALU.is_gt))
                c.link(nc.vector.tensor_reduce(ntile[:, :], cmp[:, :, :], AXX, ALU.add))
                c.link(nc.vector.tensor_tensor_scan(ends[:, :], k.c("ones")[:, 0:E], ntile[:, :], 0.0, ALU.mult, ALU.add))
                c.mark(nc.vector.tensor_tensor(scmp[:, :, :], k.c("slot").unsqueeze(2).to_broadcast([P, PADDED, E - 1]),
                                               ends[:, 0:E - 1].unsqueeze(1).to_broadcast([P, PADDED, E - 1]), ALU.is_ge))
                c.link(nc.vector.tensor_tensor(firsts[:, :], ends[:, :], ntile[:, :], ALU.subtract))
                c.link(nc.vector.tensor_reduce(sexp[:, :], scmp[:, :, :], AXX, ALU.add))
                c.mark(nc.vector.tensor_copy(f.slot_expert[:, :], sexp[:, :]))
                c.link(nc.vector.tensor_scalar(firsts[:, :], firsts[:, :], float(P), None, ALU.mult))
                c.link(nc.vector.tensor_tensor(total[:, :, :], total[:, :, :],
                                               firsts[:, :].unsqueeze(2).to_broadcast([P, E, TILES]), ALU.add))
                c.link(nc.vector.tensor_tensor(key[:, :, :], pre_ps, total[:, :, :].rearrange("p e t -> p t e"), ALU.add))
                c.link(mul(nc, key[:, :, :], key[:, :, :], oh[:, :, :]))
                c.link(nc.vector.tensor_reduce(pos[:, :], key[:, :, :], AXX, ALU.add))
                c.link(nc.vector.tensor_copy(f.pos[:, :], pos[:, :]))


def sort_phase(k, f):
    nc, d = k.nc, k.dram
    w_loaded, bias_loaded, lnb_ready = k.sem("experts_loaded"), k.sem("b_loaded"), k.sem("lnb_spread")
    scattered, sorted_loaded = k.sem("xl_scattered"), k.sem("sorted_loaded")
    R = PADDED // 3
    w1T_done, w1T_copied, b1_done, b1_ready = (k.sem("w1T_done"), k.sem("w1T_copied"), k.sem("b1_done"),
                                               k.sem("b1_ready"))
    w2T_done, w2T_copied, scaled = k.sem("w2T_done"), k.sem("w2T_copied"), k.sem("w1_scaled")
    with ExitStack() as ctx:
        w1n = k.sb(ctx, "w1_natural", [P, E * HT, P])
        w2n = k.sb(ctx, "w2_natural", [P, E, HID])
        lnb = [k.sb(ctx, f"ln_b_spread{a}", [P, P]) for a in range(2)]
        with nc.Block() as block:
            @block.sync
            def _(sp):
                for e in range(E):
                    sp.dma_start(w1n[:, e * HT:(e + 1) * HT, :], d["L0_ffn_w1"][e, :, :].rearrange("(j p) c -> p j c", p=P)
                                 ).then_inc(w_loaded, 16)
                    sp.dma_start(w2n[:, e, :], d["L0_ffn_w2"][e, :, :]).then_inc(w_loaded, 16)
                    sp.dma_start(f.b1[:, e, :], spread(d["L0_ffn_b1"][e, :])).then_inc(bias_loaded, 16)
                    sp.dma_start(f.b2[:, e, :], spread(d["L0_ffn_b2"][e, :])).then_inc(bias_loaded, 16)
                sp.wait_ge(bias_loaded, 32 * E)
                sp.wait_ge(scattered, 16 * TILES)
                for t in range(0, PADDED, R):
                    sp.dma_start(f.sorted[:, t:t + R, :], f.sorted_in[t * P:(t + R) * P, :].rearrange("(t p) c -> p t c", p=P)
                                 ).then_inc(sorted_loaded, 16)
                sp.wait_ge(sorted_loaded, 16 * (PADDED // R))

            @block.gpsimd
            def _(pool):
                for t in range(TILES):
                    pool.indirect_dma_start(out=f.sorted_in, out_offset=bass.IndirectOffsetOnAxis(ap=f.pos[:, t:t + 1], axis=0),
                                            in_=f.xl[:, t, :], in_offset=None).then_inc(scattered, 16)

            @block.tensor
            def _(pe):
                pe.wait_ge(w_loaded, 32 * E)
                for e in range(E):
                    wait(pe, w1T_copied, e)
                    for j in range(HT):
                        last = nc.tensor.transpose(k.bank[0][:, j * P:(j + 1) * P], w1n[:, e * HT + j, :], k.ident)
                    last.then_inc(w1T_done, 1)
                    wait(pe, w2T_copied, e)
                    for j in range(HT):
                        last = nc.tensor.transpose(k.bank[1][:, j * P:(j + 1) * P], w2n[:, e, j * P:(j + 1) * P], k.ident)
                    last.then_inc(w2T_done, 1)
                    pe.wait_ge(w1T_copied, e + 1)
                    pe.wait_ge(lnb_ready, e + 1)
                    wait(pe, b1_ready, e)
                    nc.tensor.matmul(k.bank[2][:, :], lnb[e % 2][:, :], f.w1[:, e, :], start=True, stop=True
                                     ).then_inc(b1_done, 1)

            @block.scalar
            def _(act):
                for e in range(E):
                    act.wait_ge(w1T_done, e + 1)
                    nc.scalar.copy(f.w1[:, e, :], k.bank[0][:, :]).then_inc(w1T_copied, 1)
                    act.wait_ge(w2T_done, e + 1)
                    nc.scalar.copy(f.w2[:, e, :], k.bank[1][:, :]).then_inc(w2T_copied, 1)
                act.wait_ge(w2T_copied, E)

            @block.vector
            def _(dve):
                dve.wait_ge(bias_loaded, 32 * E)

                def spread_ln_b(e):
                    wait(dve, b1_done, e - 1)
                    nc.vector.tensor_scalar(lnb[e % 2][:, :], k.c("ones"), f.vecT[:, 2 * E + e:2 * E + e + 1], None,
                                            ALU.mult).then_inc(lnb_ready, 1)

                spread_ln_b(0)
                for e in range(E):
                    if e + 1 < E:
                        spread_ln_b(e + 1)
                    dve.wait_ge(b1_done, e + 1)
                    nc.vector.tensor_tensor(f.b1[:, e, :], k.bank[2][:, :], f.b1[:, e, :], ALU.add).then_inc(b1_ready, 1)
                    nc.vector.tensor_scalar(f.w1[:, e, :], f.w1[:, e, :], f.vecT[:, E + e:E + e + 1], None,
                                            ALU.mult).then_inc(scaled, 1)
                dve.wait_ge(b1_ready, E)
                dve.wait_ge(scaled, E)


def experts_phase(k, f):
    nc = k.nc
    R = 3
    assert PADDED % R == 0
    LAST = PADDED // R - 1
    STORES = 3
    m = {n: k.sem(f"moe_{n}") for n in ("x_ready", "xT_done", "xT_copied", "h_done", "h_ready", "hT_done", "hT_ready",
                                        "y_done", "y_ready", "y_stored", "xl_added", "combined", "counted")}
    y_fetched = [k.sem(f"y_fetched{c}") for c in range(CHUNKS)]
    with ExitStack() as ctx:
        xs = [k.sb(ctx, f"xs{a}", [P, P]) for a in range(R)]
        xT = k.sb(ctx, "xsT", [P, P])
        h = k.sb(ctx, "moe_h", [P, HID])
        hT = k.sb(ctx, "moe_hT", [P, HID])
        w1 = f.w1[:, :, :].rearrange("p e c -> p (e c)")
        w2 = f.w2[:, :, :].rearrange("p e c -> p (e c)")
        b1 = f.b1[:, :, :].rearrange("p e c -> p (e c)")
        b2 = f.b2[:, :, :].rearrange("p e c -> p (e c)")
        fetched = f.sorted
        XT_BANK, H_BANK, HT_BANK, Y_BANK = k.bank[0:4]

        def experts(engine, t, n):
            return nc.values_load_multi_w_load_instructions(f.slot_expert[0:1, bass.ds(t, n)], [engine],
                                                            min_val=0, max_val=E - 1,
                                                            skip_runtime_bounds_check_because="it counts which of E - 1 comparisons hold")[1]

        def one(t3, t):
            return t3[:, bass.ds(t, 1), :].rearrange("p a c -> p (a c)")

        def each_tile(eng, step, engine=None):
            def group(t, last=False):
                es = experts(engine, t, R if last else R + 1) if engine else [None] * (R + 1)
                for a in range(R):
                    step(t + a, a, R - 1 - a if last else R, es[a:a + 2])
            group(0)
            with eng.Fori(1, LAST) as i:
                group(i * R)
            group(LAST * R, last=True)

        with nc.Block() as block:
            @block.sync
            def _(sp):
                S = PADDED // STORES
                for n in range(STORES):
                    sp.wait_ge(m["y_ready"], (n + 1) * S)
                    sp.dma_start(f.sorted_out[n * S * P:(n + 1) * S * P, :].rearrange("(t p) c -> p t c", p=P),
                                 f.ys[:, n * S:(n + 1) * S, :]).then_inc(m["y_stored"], 16)
                sp.wait_ge(m["y_stored"], 16 * STORES)

            @block.gpsimd
            def _(pool):
                for c in range(CHUNKS):
                    at = slice(c * CT, (c + 1) * CT)
                    nc.gpsimd.tensor_tensor(k.x[:, at, :], k.x[:, at, :], f.xl[:, at, :], ALU.add).then_inc(m["xl_added"], 1)
                pool.wait_ge(m["x_ready"], PADDED)
                pool.wait_ge(m["y_stored"], 16 * STORES)
                for t in range(TILES):
                    pool.indirect_dma_start(out=fetched[:, t, :], out_offset=None, in_=f.sorted_out,
                                            in_offset=bass.IndirectOffsetOnAxis(ap=f.pos[:, t:t + 1], axis=0)
                                            ).then_inc(y_fetched[t // CT], 16)

            @block.tensor
            def _(pe):
                def transpose_x(t, a):
                    pe.wait_ge(m["x_ready"], t + 1)
                    wait(pe, m["xT_copied"], t)
                    nc.tensor.transpose(XT_BANK[:, 0:P], xs[a][:, :], k.ident).then_inc(m["xT_done"], 1)

                def hidden(t, e):
                    pe.wait_ge(m["xT_copied"], t + 1)
                    wait(pe, m["h_ready"], t)
                    nc.tensor.matmul(H_BANK[:, :], xT[:, :], w1[:, bass.ds(e * HID, HID)], start=True, stop=True
                                     ).then_inc(m["h_done"], 1)

                def finish(t, a, left, es):
                    pe.wait_ge(m["h_ready"], t + 1)
                    wait(pe, m["hT_ready"], t)
                    for j in range(HT):
                        last = nc.tensor.transpose(HT_BANK[:, j * P:(j + 1) * P], h[:, j * P:(j + 1) * P], k.ident)
                    last.then_inc(m["hT_done"], 1)
                    if left >= 1:
                        hidden(t + 1, es[1])
                    if left >= 2:
                        transpose_x(t + 2, (a + 2) % R)
                    pe.wait_ge(m["hT_ready"], t + 1)
                    wait(pe, m["y_ready"], t)
                    for j in range(HT):
                        last = nc.tensor.matmul(Y_BANK[:, 0:P], hT[:, j * P:(j + 1) * P],
                                                w2[:, bass.ds(es[0] * HID + j * P, P)], start=j == 0, stop=j == HT - 1)
                    last.then_inc(m["y_done"], 1)

                transpose_x(0, 0)
                hidden(0, experts(mybir.EngineType.PE, 0, 1)[0])
                transpose_x(1, 1)
                each_tile(pe, finish, mybir.EngineType.PE)

            @block.scalar
            def _(act):
                def copy_x(t):
                    act.wait_ge(m["xT_done"], t + 1)
                    wait(act, m["h_done"], t)
                    nc.scalar.copy(xT[:, :], XT_BANK[:, 0:P]).then_inc(m["xT_copied"], 1)

                def step(t, a, left, es):
                    act.wait_ge(m["hT_done"], t + 1)
                    wait(act, m["y_done"], t)
                    nc.scalar.activation(hT[:, :], HT_BANK[:, :], ACT.Relu).then_inc(m["hT_ready"], 1)
                    if left >= 2:
                        copy_x(t + 2)

                copy_x(0)
                copy_x(1)
                each_tile(act, step)

            @block.vector
            def _(dve):
                def normalise(t, a):
                    wait(dve, m["xT_done"], t - R + 1)
                    nc.vector.tensor_scalar(xs[a][:, :], one(f.sorted, t), f.mean[:, bass.ds(t, 1)],
                                            f.rstd[:, bass.ds(t, 1)], ALU.subtract, ALU.mult).then_inc(m["x_ready"], 1)

                def bias_h(t, e):
                    dve.wait_ge(m["h_done"], t + 1)
                    wait(dve, m["hT_done"], t)
                    nc.vector.tensor_tensor(h[:, :], H_BANK[:, :], b1[:, bass.ds(e * HID, HID)], ALU.add
                                            ).then_inc(m["h_ready"], 1)

                def step(t, a, left, es):
                    if left >= 3:
                        normalise(t + 3, a)
                    if left >= 1:
                        bias_h(t + 1, es[1])
                    dve.wait_ge(m["y_done"], t + 1)
                    nc.vector.tensor_tensor(one(f.ys, t), Y_BANK[:, 0:P], b2[:, bass.ds(es[0] * P, P)], ALU.add
                                            ).then_inc(m["y_ready"], 1)

                for t in range(R):
                    normalise(t, t)
                bias_h(0, experts(mybir.EngineType.DVE, 0, 1)[0])
                each_tile(dve, step, mybir.EngineType.DVE)
                dve.wait_ge(m["xl_added"], CHUNKS)
                for t in range(TILES):
                    if t % CT == 0:
                        dve.wait_ge(y_fetched[t // CT], 16 * CT)
                    nc.vector.scalar_tensor_tensor(out=k.x[:, t, :], in0=fetched[:, t, :], scalar=f.alpha[:, t:t + 1],
                                                   in1=k.x[:, t, :], op0=ALU.mult, op1=ALU.add).then_inc(m["combined"], 1)
                    dve.wait_ge(m["combined"], t + 1)
                    count_tile(nc, k.st, k.x, t).then_inc(m["counted"], 1)
                dve.wait_ge(m["counted"], TILES)


def diagonal_attention_phase(k):
    nc, d = k.nc, k.dram
    G = CT * HEADS
    loaded, order_p = k.sem("wqkv_loaded"), k.sem("da_order_p")
    prep_done, prep_ready = k.sem("blockdiag_done"), k.sem("blockdiag_ready")
    xn_ready, xT_done, xT_copied = k.sem("da_xn_ready"), k.sem("da_xT_done"), k.sem("da_xT_copied")
    form_done, form_used, score_ready = k.sem("form_done"), k.sem("form_used"), k.sem("score_ready")
    sum_done, sum_copied, vsum_done, vsum_copied = k.sem("xsum_done"), k.sem("xsum_copied"), k.sem("vsum_done"), k.sem("vsum_copied")
    order, shifted, exp_ready = k.sem("da_order"), k.sem("scores_shifted"), k.sem("da_exp_ready")
    probs_ready, term_ready, x_ready = k.sem("da_probs_ready"), k.sem("da_term_ready"), k.sem("x3_ready")
    counted, repeated = k.sem("x3_counted"), k.sem("wkv_repeated")
    with ExitStack() as ctx:
        wq, wk, wv = (k.sb(ctx, n, [HD, HD]) for n in ("wq", "wk", "wv"))
        wkr = k.sb(ctx, "wk_repeated", [HD, HEADS, HD])
        wvr = k.sb(ctx, "wv_repeated", [HD, HEADS, HD])
        a1 = k.sb(ctx, "wq_wk", [HD, P])
        form = k.sb(ctx, "qk_form", [P, P])
        bdv = k.sb(ctx, "wv_blocks", [P, P])
        xc = k.sb(ctx, "da_xc", [P, CT, P])
        xn = [k.sb(ctx, f"da_xn{a}", [P, CT, P]) for a in range(2)]
        xT = k.sb(ctx, "da_xT", [P, SEQ])
        xsum = k.sb(ctx, "da_xsum", [P, P])
        prod = k.sb(ctx, "da_prod", [P, SEQ])
        sc = k.sb(ctx, "da_scores", [P, CHUNKS, G])
        top = k.sb(ctx, "da_max", [P, G])
        den = k.sb(ctx, "da_den", [P, G])
        vs = k.sb(ctx, "da_vsum", [P, CHUNKS, P])
        term = [k.sb(ctx, f"da_term{a}", [P, CT, P]) for a in range(2)]
        with nc.Block() as block:
            @block.sync
            def _(sp):
                sp.dma_start(wq[:, :], d["L1_attn_Wq"]).then_inc(loaded, 16)
                sp.dma_start(wk[:, :], d["L1_attn_Wk"]).then_inc(loaded, 16)
                sp.dma_start(wv[:, :], d["L1_attn_Wv"]).then_inc(loaded, 16)

            @block.gpsimd
            def _(pool):
                @pairs(pool)
                def _(i, a):
                    t = i * 2 + a
                    c = Chain(pool, order_p, t)
                    wait(pool, xn_ready, t)
                    c.link(nc.gpsimd.tensor_tensor(xc[:, :, :], tiles_of(k.x, t), per_token(k.mean, t), ALU.subtract))
                    wait(pool, score_ready, t - 1)
                    wait(pool, sum_done, t - 1)
                    nc.gpsimd.tensor_tensor(xn[a][:, :, :], xc[:, :, :], per_token(k.rstd, t), ALU.mult
                                            ).then_inc(xn_ready, 1)
                for c in range(CHUNKS):
                    pool.wait_ge(term_ready, c + 1)
                    at = slice(c * CT, (c + 1) * CT)
                    nc.gpsimd.tensor_tensor(k.x[:, at, :], k.x[:, at, :], term[c % 2][:, :, :], ALU.add).then_inc(x_ready, 1)

            @block.tensor
            def _(pe):
                pe.wait_ge(loaded, 48)
                pe.wait_ge(repeated, 2)
                nc.tensor.matmul(k.bank[0][0:HD, 0:P], wq[:, :], wkr[:, :, :].rearrange("e h d -> e (h d)"),
                                 start=True, stop=True).then_inc(prep_done, 1)
                nc.tensor.matmul(k.bank[1][:, 0:P], wvr[:, :, :].rearrange("e h d -> e (h d)"), k.c("headtile")[0:HD, :],
                                 start=True, stop=True).then_inc(prep_done, 1)
                pe.wait_ge(prep_ready, 1)
                nc.tensor.matmul(k.bank[2][:, 0:P], k.c("headtile")[0:HD, :], a1[:, :], start=True, stop=True
                                 ).then_inc(prep_done, 1)
                pe.wait_ge(prep_ready, 3)

                def v_sum(t):
                    pe.wait_ge(sum_copied, t + 1)
                    wait(pe, vsum_copied, t)
                    nc.tensor.matmul(k.bank[2][:, 0:P], xsum[:, :], bdv[:, :], start=True, stop=True).then_inc(vsum_done, 1)

                @pairs(pe)
                def _(i, a):
                    t = i * 2 + a
                    pe.wait_ge(xn_ready, t + 1)
                    wait(pe, xT_copied, t)
                    for j in range(CT):
                        last = nc.tensor.transpose(k.bank[0][:, j * P:(j + 1) * P], xn[a][:, j, :], k.ident)
                    last.then_inc(xT_done, 1)
                    if not (isinstance(t, int) and t == 0):
                        v_sum(t - 1)
                    wait(pe, sum_copied, t)
                    for j in range(CT):
                        last = nc.tensor.matmul(k.bank[3][:, 0:P], xn[a][:, j, :], k.c("ones"),
                                                start=j == 0, stop=j == CT - 1)
                    last.then_inc(sum_done, 1)
                    pe.wait_ge(xT_copied, t + 1)
                    wait(pe, form_used, t)
                    for j in range(CT):
                        last = nc.tensor.matmul(k.bank[1][:, j * P:(j + 1) * P], xT[:, j * P:(j + 1) * P], form[:, :],
                                                start=True, stop=True)
                    last.then_inc(form_done, 1)
                v_sum(CHUNKS - 1)

            @block.scalar
            def _(act):
                def copy_v_sum(t):
                    act.wait_ge(vsum_done, t + 1)
                    nc.scalar.copy(vs[:, bass.ds(t, 1), :].rearrange("p a c -> p (a c)"), k.bank[2][:, 0:P]
                                   ).then_inc(vsum_copied, 1)

                @pairs(act)
                def _(i, a):
                    t = i * 2 + a
                    act.wait_ge(xT_done, t + 1)
                    wait(act, form_done, t)
                    nc.scalar.copy(xT[:, :], k.bank[0][:, :]).then_inc(xT_copied, 1)
                    if not (isinstance(t, int) and t == 0):
                        copy_v_sum(t - 1)
                    act.wait_ge(sum_done, t + 1)
                    nc.scalar.copy(xsum[:, :], k.bank[3][:, 0:P]).then_inc(sum_copied, 1)
                copy_v_sum(CHUNKS - 1)
                act.wait_ge(shifted, 1)
                nc.scalar.activation(sc[:, :, :], sc[:, :, :], ACT.Exp, scale=float(P) ** -0.5).then_inc(exp_ready, 1)

            @block.vector
            def _(dve):
                dve.wait_ge(loaded, 48)
                for to, of in ((wkr, wk), (wvr, wv)):
                    nc.vector.tensor_copy(to[:, :, :], of[:, :].unsqueeze(1).to_broadcast([HD, HEADS, HD])
                                          ).then_inc(repeated, 1)
                dve.wait_ge(prep_done, 2)
                nc.vector.tensor_copy(a1[:, :], k.bank[0][0:HD, 0:P]).then_inc(prep_ready, 1)
                mul(nc, bdv[:, :], k.bank[1][:, 0:P], k.c("headmask")).then_inc(prep_ready, 1)
                dve.wait_ge(prep_done, 3)
                mul(nc, form[:, :], k.bank[2][:, 0:P], k.c("headmask")).then_inc(prep_ready, 1)

                @pairs(dve)
                def _(i, a):
                    t = i * 2 + a
                    dve.wait_ge(form_done, t + 1)
                    wait(dve, score_ready, t)
                    mul(nc, prod[:, :], k.bank[1][:, :], xn[a][:, :, :].rearrange("p t c -> p (t c)")).then_inc(form_used, 1)
                    dve.wait_ge(form_used, t + 1)
                    nc.vector.tensor_reduce(sc[:, bass.ds(t, 1), :].rearrange("p a g -> p (a g)"),
                                            prod[:, :].rearrange("p (g e) -> p g e", e=HD), AXX, ALU.add
                                            ).then_inc(score_ready, 1)
                dve.wait_ge(score_ready, CHUNKS)
                dve.wait_ge(vsum_copied, CHUNKS)
                c = Chain(dve, order)
                by_group = sc[:, :, :].rearrange("p c g -> p g c")

                def over_c(t):
                    return t.unsqueeze(1).to_broadcast([P, CHUNKS, G])
                c.link(nc.vector.tensor_reduce(top[:, :], by_group, AXX, ALU.max))
                nc.vector.tensor_tensor(sc[:, :, :], sc[:, :, :], over_c(top[:, :]), ALU.subtract).then_inc(shifted, 1)
                dve.wait_ge(exp_ready, 1)
                c.link(nc.vector.tensor_reduce(den[:, :], by_group, AXX, ALU.add))
                c.link(nc.vector.reciprocal(den[:, :], den[:, :]))
                c.link(mul(nc, sc[:, :, :], sc[:, :, :], over_c(den[:, :])))

                def count(s):
                    dve.wait_ge(x_ready, s + 1)
                    for t in range(s * CT, (s + 1) * CT):
                        count_tile(nc, k.st, k.x, t).then_inc(counted, 1)

                for s in range(CHUNKS):
                    if s >= 2:
                        count(s - 2)
                    mul(nc, term[s % 2][:, :, :].rearrange("p t (h e) -> p t h e", e=HD),
                        sc[:, s, :].rearrange("p (t h) -> p t h", h=HEADS).unsqueeze(3).to_broadcast([P, CT, HEADS, HD]),
                        vs[:, s, :].rearrange("p (h e) -> p h e", e=HD).unsqueeze(1).to_broadcast([P, CT, HEADS, HD])
                        ).then_inc(term_ready, 1)
                count(CHUNKS - 2)
                count(CHUNKS - 1)
                dve.wait_ge(counted, TILES)


def router_phase(k, g):
    nc, d = k.nc, k.dram
    loaded, order_p, xf_ready = k.sem("router_loaded"), k.sem("r_order_p"), k.sem("xf_ready")
    xf_kept, xT_done, xT_copied = k.sem("xf_kept"), k.sem("r_xT_done"), k.sem("r_xT_copied")
    hid_done, hid_ready, log_done, log_copied = k.sem("r_hid_done"), k.sem("r_hid_ready"), k.sem("log_done"), k.sem("log_copied")
    dyn_loaded, cut, cut_order, placed = k.sem("dyn_loaded"), k.sem("b2_cut"), k.sem("b2_cut_order"), k.sem("b2_placed")
    zeroed = k.sem("dyn_zeroed")
    loads = []

    def load(sp, to, of):
        loads.append(sp.dma_start(to, of))
        loads[-1].then_inc(dyn_loaded, 16)

    sw_ready, shifted, exp_ready, order = k.sem("sw_ready"), k.sem("r_shifted"), k.sem("r_exp_ready"), k.sem("r_order")
    with ExitStack() as ctx:
        b2e = k.sb(ctx, "expert_b2_sb", [E, CTRL])
        sel = k.sb(ctx, "pair_rows_f32", [2 * E, 2 * PAIRS * P])
        rest = k.sb(ctx, "b2_rest", [E, CTRL])
        back = k.sb(ctx, "b2_back", [E, CTRL])
        part = k.sb(ctx, "b2_parts", [E, 3, CTRL], BF16)
        w1 = k.sb(ctx, "router_w1", [P, RH])
        b1 = k.sb(ctx, "router_b1", [RH, 1])
        w2 = k.sb(ctx, "router_w2", [RH, E])
        b2 = k.sb(ctx, "router_b2", [P, E])
        sw = k.sb(ctx, "shared_weight", [P, 2])
        xc = k.sb(ctx, "r_xc", [P, CT, P])
        xf = [k.sb(ctx, f"r_xf{a}", [P, CT, P]) for a in range(2)]
        hid = k.sb(ctx, "r_hid", [RH, SEQ])
        lg = k.sb(ctx, "logits", [P, TILES, E])
        key = k.sb(ctx, "r_key", [P, TILES, E])
        one = k.sb(ctx, "r_one", [P, TILES])
        best = k.sb(ctx, "r_best", [P, 2, TILES])
        with nc.Block() as block:
            @block.sync
            def _(sp):
                sp.dma_start(w1[:, :], d["L1_ffn_router_w1"]).then_inc(loaded, 16)
                sp.dma_start(b1[:, :], d["L1_ffn_router_b1"].rearrange("(p a) -> p a", a=1)).then_inc(loaded, 16)
                sp.dma_start(w2[:, :], d["L1_ffn_router_w2"]).then_inc(loaded, 16)
                sp.dma_start(b2[:, :], spread(d["L1_ffn_router_b2"])).then_inc(loaded, 16)
                sp.dma_start(sw[:, 0:1], spread(d["L1_ffn_shared_weight"])).then_inc(loaded, 16)
                sp.wait_ge(zeroed, 3)
                load(sp, b2e[:, :], d["L1_ffn_expert_b2"])
                load(sp, sel[:, :], d["sel"])
                for kt in range(2):
                    rows = slice(kt * P, (kt + 1) * P)
                    load(sp, g.w1[:, kt, 0:E * EH].rearrange("p (e h) -> p e h", h=EH),
                         d["L1_ffn_expert_w1"][:, rows, :].rearrange("e p h -> p e h"))
                    load(sp, g.w1s[:, kt, 0:EH], d["L1_ffn_shared_w1"][rows, :])
                load(sp, g.w2[:, :, :], d["L1_ffn_expert_w2"].rearrange("(q t) h c -> (t h) q c", t=2))
                load(sp, g.w2s[0:EH, 0:CTRL], d["L1_ffn_shared_w2"])
                load(sp, g.w2s[ONE:ONE + 1, 0:CTRL], row(d["L1_ffn_shared_b2"]))
                for q in range(PAIRS):
                    load(sp, g.b1[:, q:q + 1], d["L1_ffn_expert_b1"][2 * q:2 * q + 2, :].rearrange("t (h a) -> (t h) a", a=1))
                load(sp, g.b1s[0:EH, :], d["L1_ffn_shared_b1"].rearrange("(p a) -> p a", a=1))
                load(sp, g.w1s[:, 0, EH:ONE], d["L1_ffn_halt_w1"])
                load(sp, g.b1s[EH:ONE, :], d["L1_ffn_halt_b1"].rearrange("(p a) -> p a", a=1))
                load(sp, g.w2s[EH:ONE, CTRL:CTRL + 1], d["L1_ffn_halt_w2"])
                load(sp, g.w2s[ONE:ONE + 1, CTRL:CTRL + 1], row(d["L1_ffn_halt_b2"]))
                load(sp, g.rw1[:, :], d["L1_ffn_refine_w1"])
                load(sp, g.rw2[:, :, :], d["L1_ffn_refine_w2"].rearrange("(j p) c -> p j c", p=P))
                for j in range(2):
                    load(sp, g.rb1[:, j:j + 1], d["L1_ffn_refine_b1"][j * P:(j + 1) * P].rearrange("(p a) -> p a", a=1))
                load(sp, g.rb2[:, :], spread(d["L1_ffn_refine_b2"]))
                load(sp, g.iw[:, :], spread(d["L1_ffn_integration_weight"]))
                load(sp, g.mu[:, :], spread(d["L1_ffn_mu"]))
                sp.wait_ge(cut, 3)
                for n in range(3):
                    for s in range(2):
                        at = n * 2 * E + s * E
                        sp.dma_start(g.b2[at:at + E, s, :], part[:, n, :]).then_inc(placed, 16)
                sp.wait_ge(placed, 96)
                sp.wait_ge(dyn_loaded, 16 * len(loads))

            @block.gpsimd
            def _(pool):
                @pairs(pool)
                def _(i, a):
                    t = i * 2 + a
                    c = Chain(pool, order_p, t)
                    wait(pool, xf_ready, t)
                    c.link(nc.gpsimd.tensor_tensor(xc[:, :, :], tiles_of(k.x, t), per_token(k.mean, t), ALU.subtract))
                    wait(pool, xT_done, t - 1)
                    wait(pool, xf_kept, t - 1)
                    nc.gpsimd.tensor_tensor(xf[a][:, :, :], xc[:, :, :], per_token(k.rstd, t), ALU.mult).then_inc(xf_ready, 1)
                pool.wait_ge(dyn_loaded, 16 * len(loads))
                nc.gpsimd.tensor_copy(part[:, 0, :], b2e[:, :]).then_inc(cut, 1)
                pool.wait_ge(cut, 1)
                c = Chain(pool, cut_order)
                c.link(nc.gpsimd.tensor_copy(back[:, :], part[:, 0, :]))
                c.link(nc.gpsimd.tensor_tensor(rest[:, :], b2e[:, :], back[:, :], ALU.subtract))
                nc.gpsimd.tensor_copy(part[:, 1, :], rest[:, :]).then_inc(cut, 1)
                pool.wait_ge(cut, 2)
                c.link(nc.gpsimd.tensor_copy(back[:, :], part[:, 1, :]))
                c.link(nc.gpsimd.tensor_tensor(rest[:, :], rest[:, :], back[:, :], ALU.subtract))
                nc.gpsimd.tensor_copy(part[:, 2, :], rest[:, :]).then_inc(cut, 1)
                nc.gpsimd.tensor_copy(g.sel[:, :], sel[:, :])
                pool.wait_ge(cut, 3)

            @block.tensor
            def _(pe):
                pe.wait_ge(loaded, 80)

                def logits(t):
                    pe.wait_ge(hid_ready, t + 1)
                    wait(pe, log_copied, t)
                    for j in range(CT):
                        last = nc.tensor.matmul(k.bank[2][:, j * E:(j + 1) * E], hid[:, j * P:(j + 1) * P], w2[:, :],
                                                start=True, stop=True)
                    last.then_inc(log_done, 1)

                @pairs(pe)
                def _(i, a):
                    t = i * 2 + a
                    pe.wait_ge(xf_ready, t + 1)
                    wait(pe, xT_copied, t)
                    for j in range(CT):
                        last = nc.tensor.transpose(k.bank[0][:, j * P:(j + 1) * P], xf[a][:, j, :], k.ident)
                    last.then_inc(xT_done, 1)
                    if not (isinstance(t, int) and t == 0):
                        logits(t - 1)
                    pe.wait_ge(xT_copied, t + 1)
                    nc.tensor.matmul(k.bank[1][0:RH, :], w1[:, :], g.xfT[:, bass.ds(t * SEQ, SEQ)], start=True, stop=True
                                     ).then_inc(hid_done, 1)
                logits(CHUNKS - 1)

            @block.scalar
            def _(act):
                act.wait_ge(loaded, 80)
                nc.scalar.activation(sw[:, 0:1], sw[:, 0:1], ACT.Sigmoid).then_inc(sw_ready, 1)

                @pairs(act)
                def _(i, a):
                    t = i * 2 + a
                    act.wait_ge(xT_done, t + 1)
                    nc.scalar.copy(g.xfT[:, bass.ds(t * SEQ, SEQ)], k.bank[0][:, :]).then_inc(xT_copied, 1)
                    nc.scalar.copy(tiles_of(g.xf, t), xf[a][:, :, :]).then_inc(xf_kept, 1)
                    act.wait_ge(hid_done, t + 1)
                    wait(act, log_done, t)
                    nc.scalar.activation(hid[:, :], k.bank[1][0:RH, :], ACT.Gelu, bias=b1[:, 0:1]).then_inc(hid_ready, 1)
                act.wait_ge(shifted, 1)
                nc.scalar.activation(lg[:, :, :], lg[:, :, :], ACT.Exp).then_inc(exp_ready, 1)
                act.wait_ge(exp_ready, 1)

            @block.vector
            def _(dve):
                nc.vector.memset(g.b2[:, :, :], 0.0).then_inc(zeroed, 1)
                nc.vector.memset(g.w1s[:, :, :], 0.0).then_inc(zeroed, 1)
                nc.vector.memset(g.w2s[:, :], 0.0).then_inc(zeroed, 1)
                for u in range(2):
                    nc.vector.memset(g.hs[u][:, :], 1.0)
                dve.wait_ge(loaded, 80)

                @rounds(dve, CHUNKS)
                def _(i):
                    dve.wait_ge(log_done, i + 1)
                    nc.vector.tensor_tensor(tiles_of(lg, i), k.bank[2][:, 0:CT * E].rearrange("p (t e) -> p t e", e=E),
                                            b2[:, :].unsqueeze(1).to_broadcast([P, CT, E]), ALU.add).then_inc(log_copied, 1)
                dve.wait_ge(log_copied, CHUNKS)
                c = Chain(dve, order)

                def over_e(t):
                    return t.unsqueeze(2).to_broadcast([P, TILES, E])
                rank8 = k.c("rank8").unsqueeze(1).to_broadcast([P, TILES, E])
                c.link(nc.vector.tensor_reduce(one[:, :], lg[:, :, :], AXX, ALU.max))
                nc.vector.tensor_tensor(lg[:, :, :], lg[:, :, :], over_e(one[:, :]), ALU.subtract).then_inc(shifted, 1)
                dve.wait_ge(exp_ready, 1)
                c.link(nc.vector.tensor_reduce(one[:, :], lg[:, :, :], AXX, ALU.add))
                c.link(nc.vector.reciprocal(one[:, :], one[:, :]))
                c.link(mul(nc, lg[:, :, :], lg[:, :, :], over_e(one[:, :])))
                for s in range(2):
                    oh = g.onehot[:, :, s * E:(s + 1) * E]
                    c.link(nc.vector.tensor_reduce(best[:, s, :], lg[:, :, :], AXX, ALU.max))
                    c.link(nc.vector.tensor_tensor(key[:, :, :], lg[:, :, :], over_e(best[:, s, :]), ALU.is_equal))
                    c.link(mul(nc, key[:, :, :], key[:, :, :], rank8))
                    c.link(nc.vector.tensor_reduce(one[:, :], key[:, :, :], AXX, ALU.max))
                    c.link(nc.vector.tensor_tensor(oh, key[:, :, :], over_e(one[:, :]), ALU.is_equal))
                    if s == 0:
                        c.link(nc.vector.scalar_tensor_tensor(out=lg[:, :, :], in0=oh, scalar=-2.0, in1=lg[:, :, :],
                                                              op0=ALU.mult, op1=ALU.add))
                c.link(nc.vector.tensor_tensor(one[:, :], best[:, 0, :], best[:, 1, :], ALU.add))
                c.link(nc.vector.reciprocal(one[:, :], one[:, :]))
                dve.wait_ge(sw_ready, 1)
                c.link(nc.vector.tensor_scalar(sw[:, 1:2], sw[:, 0:1], -1.0, 1.0, ALU.mult, ALU.add))
                c.link(nc.vector.tensor_scalar(one[:, :], one[:, :], sw[:, 1:2], None, ALU.mult))
                c.link(nc.vector.tensor_scalar(g.weight[:, 0, :], k.c("ones")[:, 0:TILES], sw[:, 0:1], None, ALU.mult))
                for s in range(2):
                    c.link(mul(nc, g.weight[:, 1 + s, :], best[:, s, :], one[:, :]))


def dynamics_phase(k, g, out):
    nc = k.nc
    ROUNDS = CHUNKS // 2
    Z = k.bank[0]
    HB = k.bank[1:3]
    MB = k.bank[3:5]
    CB = k.bank[5:8]
    Z_PER, H_PER, STEP_H = 9, 24, 5
    m = {n: k.sem(n) for n in (
        "oh_staged", "z_done", "z_read", "hid_done", "hid_ready", "mask_done", "masked", "ctrl_done",
        "ctrl_read", "absb_ready", "exp_ready", "ln_ready", "xm_ready", "state_ready", "order",
        "out_order", "out_ready", "ref_order")}
    stored = [k.sem(f"out_stored{u}") for u in range(2)]

    def z_index(i, what, u=0, n=0):
        first = isinstance(i, int) and i == 0
        final = isinstance(i, int) and i == ROUNDS - 1
        return {"onehot": i * Z_PER - (0 if first else 2), "it1": i * Z_PER + 1 + 2 * u + n,
                "refine": i * Z_PER + (5 if u == 0 else 7 if final else 8) + n}[what]

    def step_hidden(i, n, q):
        shift = 2 if n == 0 and not (isinstance(i, int) and i == 0) else 0
        return i * H_PER + n * STEP_H + q - shift, HB[(n * STEP_H + q) % 2]

    def refine_hidden(i, u, j):
        final = isinstance(i, int) and i == ROUNDS - 1
        at = 4 * STEP_H if u == 0 else (H_PER - 2 if final else H_PER + STEP_H - 2)
        return i * H_PER + at + j, HB[(at + j) % 2]

    def ahead(i, n):
        return (z_index(i - 1, "refine", 1), z_index(i, "it1", 0), z_index(i, "it1", 1), z_index(i, "refine", 0))[n]

    def steps_and_refinements(eng, start, step, refine, after_last=lambda: None):
        def body(i):
            step(i, 0, lambda: start(i))
            if isinstance(i, int) and i == 0:
                step(i, 1)
            else:
                second_half = refine(i - 1, 1, split=True)
                step(i, 1, second_half)
            for n in range(2, 4):
                step(i, n)
            refine(i, 0)
        rounds(eng, ROUNDS)(body)
        after_last()
        refine(ROUNDS - 1, 1)

    with ExitStack() as ctx:
        def two(n, shape, dt=FP32):
            return [k.sb(ctx, f"{n}{u}", shape, dt) for u in range(2)]
        ohs = k.sb(ctx, "onehot_copies", [P, CT, 2, P // (4 * E), 2 * E])
        ohT = two("ohT", [6 * E, SEQ], BF16)
        state, vel, xT, vT = two("state", [P, SEQ]), two("vel", [P, SEQ]), two("stateT", [P, SEQ]), two("velT", [P, SEQ])
        hp = two("pair_hidden", [P, SEQ])
        hm = two("masked_hidden", [P, 2, PAIRS, SEQ])
        tt = two("tanh_a_g", [P, 2, 3, SEQ])
        bb = two("ctrl_b", [P, 3, SEQ])
        xm = two("x_minus_mu", [P, SEQ])
        th = two("halt", [P, CT])
        xx = two("x_plus_xf", [P, SEQ])
        L = k.sb(ctx, "softplus", [P, 3, SEQ])
        s1 = k.sb(ctx, "sum_v", [P, SEQ])
        s2 = k.sb(ctx, "sum_g", [P, SEQ])

        def tiles(t):
            return t.rearrange("p (t c) -> p t c", c=P)

        def state_in(i, u, it):
            return tiles_of(g.xf, i * 2 + u) if it == 0 else tiles(state[u][:, :])

        STEPS = [(it, u) for it in range(2) for u in range(2)]

        def each_round(eng):
            return rounds(eng, ROUNDS)

        with nc.Block() as block:
            @block.sync
            def _(sp):
                @each_round(sp)
                def _(i):
                    for u in range(2):
                        to = out[bass.ds(i * 2 + u, 1), :, :].rearrange("s (t p) c -> p (s t) c", p=P)
                        sp.wait_ge(m["out_ready"], i * 2 + u + 1)
                        sp.dma_start(to, tiles(xx[u][:, :])).then_inc(stored[u], 16)
                for u in range(2):
                    sp.wait_ge(stored[u], 16 * ROUNDS)

            @block.gpsimd
            def _(pool):
                def spread_row(t):
                    return t[:, :].unsqueeze(1).to_broadcast([P, CT, P])

                def output(i, u):
                    t = i * 2 + u
                    wait(pool, stored[u], i * 16)
                    nc.gpsimd.tensor_tensor(tiles(xx[u][:, :]), tiles_of(k.x, t), tiles_of(g.xf, t), ALU.add
                                            ).then_inc(m["out_order"], 1)
                    pool.wait_ge(m["z_read"], z_index(i, "refine", u) + 2)
                    ro = tiles(xT[u][:, :])
                    nc.gpsimd.tensor_tensor(ro, ro, spread_row(g.rb2), ALU.add).then_inc(m["out_order"], 1)
                    pool.wait_ge(m["out_order"], t * 3 + 2)
                    nc.gpsimd.tensor_tensor(ro, ro, spread_row(g.iw), ALU.mult).then_inc(m["out_order"], 1)
                    pool.wait_ge(m["out_order"], t * 3 + 3)
                    nc.gpsimd.tensor_tensor(tiles(xx[u][:, :]), tiles(xx[u][:, :]), ro, ALU.add).then_inc(m["out_ready"], 1)

                @each_round(pool)
                def _(i):
                    first = isinstance(i, int) and i == 0
                    if not first:
                        pool.wait_ge(m["z_done"], z_index(i - 1, "it1", 0) + 1)
                    for u in range(2):
                        nc.gpsimd.tensor_copy(ohs[:, :, u, :, :], tiles_of(g.onehot, i * 2 + u).unsqueeze(2).to_broadcast(
                            [P, CT, P // (4 * E), 2 * E])).then_inc(m["oh_staged"], 1)
                    for n, (it, u) in enumerate(STEPS):
                        o = i * 4 + n
                        wait(pool, m["state_ready"], o - 1)
                        nc.gpsimd.tensor_tensor(tiles(xm[u][:, :]), state_in(i, u, it), spread_row(g.mu), ALU.subtract
                                                ).then_inc(m["xm_ready"], 1)
                        if n < 2 and not first:
                            output(i - 1, n)
                output(ROUNDS - 1, 0)
                output(ROUNDS - 1, 1)

            def masks_of(pe, o, q, u):
                for s in range(2):
                    wait(pe, m["masked"], o * 8 + q * 2 + s - 1)
                    nc.tensor.matmul(MB[s][:, :], g.sel[:, (s * PAIRS + q) * P:(s * PAIRS + q + 1) * P],
                                     ohT[u][0:2 * E, :], start=True, stop=True).then_inc(m["mask_done"], 1)

            @block.tensor
            def _(pe):
                def use_z(z):
                    wait(pe, m["z_read"], z)

                def transposed(z, src, ident=None):
                    use_z(z)
                    for j in range(CT):
                        last = nc.tensor.transpose(Z[:, j * P:(j + 1) * P], src[:, j * P:(j + 1) * P], k.ident)
                    last.then_inc(m["z_done"], 1)

                def start(i):
                    pe.wait_ge(m["oh_staged"], i * 2 + 2)
                    use_z(z_index(i, "onehot"))
                    for j in range(CT):
                        last = nc.tensor.transpose(Z[:, j * P:(j + 1) * P],
                                                   ohs[:, j, :, :, :].rearrange("p u n c -> p (u n c)"), k.ident)
                    last.then_inc(m["z_done"], 1)

                def step(i, n, after_first_hidden=None):
                    (it, u), o = STEPS[n], i * 4 + n
                    if it == 0:
                        moving = [g.xfT[:, bass.ds((i * 2 + u) * SEQ, SEQ)]]
                    else:
                        z = z_index(i, "it1", u)
                        transposed(z + 1, vel[u])
                        pe.wait_ge(m["z_read"], z + 1)
                        moving = [xT[u][:, :], vT[u][:, :]]

                    def hidden(q, weights):
                        h, hb = step_hidden(i, n, q)
                        wait(pe, m["hid_ready"], h - 1)
                        for kt, x in enumerate(moving):
                            if kt and q == 0:
                                pe.wait_ge(m["z_read"], z + 2)
                            last = nc.tensor.matmul(hb[:, :], weights[:, kt, :], x,
                                                    start=kt == 0, stop=kt == len(moving) - 1)
                        last.then_inc(m["hid_done"], 1)

                    for q in range(PAIRS):
                        hidden(q, g.w1[:, :, q * P:(q + 1) * P])
                        if q == 0 and after_first_hidden:
                            after_first_hidden()
                        if q == 1 and n == 0:
                            pe.wait_ge(m["z_read"], z_index(i, "onehot") + 1)
                        if q >= 1:
                            masks_of(pe, o, q - 1, u)
                    hidden(4, g.w1s)
                    masks_of(pe, o, PAIRS - 1, u)
                    pe.wait_ge(m["hid_ready"], step_hidden(i, n, STEP_H - 1)[0] + 1)
                    for t in range(CT):
                        cols = slice(t * P, (t + 1) * P)
                        for s in range(3):
                            wait(pe, m["ctrl_read"], o * 12 + t * 3 + s - 2)
                            if s == 0:
                                last = nc.tensor.matmul(CB[s][:, 0:CTRL + 1], g.hs[u][:, cols], g.w2s[:, :],
                                                        start=True, stop=True)
                            else:
                                nc.tensor.matmul(CB[s][:, 0:CTRL], ohT[u][:, cols], g.b2[:, s - 1, :],
                                                 start=True, stop=False)
                                if t == 0 and s == 1:
                                    pe.wait_ge(m["masked"], o * 8 + 8)
                                for q in range(PAIRS):
                                    last = nc.tensor.matmul(CB[s][:, 0:CTRL], hm[u][:, s - 1, q, cols],
                                                            g.w2[:, q, :], start=False, stop=q == PAIRS - 1)
                            last.then_inc(m["ctrl_done"], 1)
                            if (t, s) == (CT - 1, 1) and not (isinstance(o, int) and o == 0):
                                pe.wait_ge(m["state_ready"], o)
                                transposed(ahead(i, n), state[1 - u])

                def refine(i, u, split=False):
                    z = z_index(i, "refine", u)
                    if isinstance(i, int) and (i, u) == (ROUNDS - 1, 1):
                        pe.wait_ge(m["state_ready"], ROUNDS * 4)
                        transposed(z, state[u])
                    pe.wait_ge(m["z_read"], z + 1)
                    for j in range(2):
                        h, hb = refine_hidden(i, u, j)
                        wait(pe, m["hid_ready"], h - 1)
                        nc.tensor.matmul(hb[:, :], g.rw1[:, j * P:(j + 1) * P], xT[u][:, :], start=True, stop=True
                                         ).then_inc(m["hid_done"], 1)

                    def outputs():
                        pe.wait_ge(m["hid_ready"], refine_hidden(i, u, 1)[0] + 1)
                        for t in range(CT):
                            for j in range(2):
                                last = nc.tensor.matmul(Z[:, t * P:(t + 1) * P], hm[u][:, 0, j, t * P:(t + 1) * P],
                                                        g.rw2[:, j, :], start=j == 0, stop=j == 1)
                        last.then_inc(m["z_done"], 1)
                    return outputs if split else outputs()

                steps_and_refinements(pe, start, step, refine)

            @block.scalar
            def _(act):
                def read_z(z, to, of=Z[:, :]):
                    act.wait_ge(m["z_done"], z + 1)
                    nc.scalar.copy(to, of).then_inc(m["z_read"], 1)

                def softplus_exp(o):
                    act.wait_ge(m["absb_ready"], o + 1)
                    nc.scalar.activation(L[:, :, :], L[:, :, :], ACT.Exp).then_inc(m["exp_ready"], 1)

                def softplus_ln(o):
                    act.wait_ge(m["exp_ready"], o + 1)
                    nc.scalar.activation(L[:, :, :], L[:, :, :], ACT.Ln, bias=1.0).then_inc(m["ln_ready"], 1)

                def start(i):
                    act.wait_ge(m["z_done"], z_index(i, "onehot") + 1)
                    nc.scalar.copy(ohT[0][:, :], Z[0:6 * E, :])
                    nc.scalar.copy(ohT[1][:, :], Z[P // 2:P // 2 + 6 * E, :]).then_inc(m["z_read"], 1)

                def step(i, n, after_first_hidden=None):
                    (it, u), o = STEPS[n], i * 4 + n
                    if it == 1:
                        read_z(z_index(i, "it1", u) + 1, vT[u][:, :])

                    def gelu(q, to, rows, bias):
                        h, hb = step_hidden(i, n, q)
                        act.wait_ge(m["hid_done"], h + 1)
                        nc.scalar.activation(to, hb[0:rows, :], ACT.Gelu, bias=bias).then_inc(m["hid_ready"], 1)

                    for q in range(PAIRS):
                        wait(act, m["masked"], o * 8 + 2 * (q - 1))
                        gelu(q, hp[q % 2][:, :], P, g.b1[:, q:q + 1])
                        if q == 0 and after_first_hidden:
                            after_first_hidden()
                    gelu(4, g.hs[u][0:ONE, :], ONE, g.b1s[:, 0:1])
                    started = not (isinstance(o, int) and o == 0)
                    if started:
                        softplus_exp(o - 1)
                    for t in range(CT):
                        cols = slice(t * P, (t + 1) * P)
                        for s in range(3):
                            act.wait_ge(m["ctrl_done"], o * 12 + t * 3 + s + 1)
                            if t == 0 and s == 0:
                                wait(act, m["state_ready"], o - 1)
                            if s == 0:
                                nc.scalar.activation(th[u][:, t:t + 1], CB[s][:, CTRL:CTRL + 1], ACT.Tanh, scale=0.5)
                            nc.scalar.activation(tt[u][:, :, s, cols], CB[s][:, 0:CTRL].rearrange("p (n c) -> p n c", c=P)[:, 0:3:2, :],
                                                 ACT.Tanh, scale=0.5)
                            nc.scalar.copy(bb[u][:, s, cols], CB[s][:, P:2 * P]).then_inc(m["ctrl_read"], 1)
                            if (t, s) == (CT - 1, 1) and started:
                                if n in (1, 2) and not (isinstance(i, int) and i == 0):
                                    act.wait_ge(m["out_ready"], i * 2 - 1 + 1 - u)
                                read_z(ahead(i, n), xT[1 - u][:, :])
                        if t == 0 and started:
                            softplus_ln(o - 1)

                def refine(i, u, split=False):
                    z = z_index(i, "refine", u)
                    if isinstance(i, int) and (i, u) == (ROUNDS - 1, 1):
                        read_z(z, xT[u][:, :])
                    for j in range(2):
                        h, hb = refine_hidden(i, u, j)
                        act.wait_ge(m["hid_done"], h + 1)
                        nc.scalar.activation(hm[u][:, 0, j, :], hb[:, :], ACT.Gelu, bias=g.rb1[:, j:j + 1]
                                             ).then_inc(m["hid_ready"], 1)

                    def outputs():
                        act.wait_ge(m["z_done"], z + 2)
                        nc.scalar.copy(xT[u][:, :], Z[:, :]).then_inc(m["z_read"], 1)
                    return outputs if split else outputs()

                def last_softplus():
                    softplus_exp(ROUNDS * 4 - 1)
                    softplus_ln(ROUNDS * 4 - 1)

                steps_and_refinements(act, start, step, refine, last_softplus)

            @block.vector
            def _(dve):
                LINKS = {0: 6, 1: 10}
                PER = 2 * (LINKS[0] + LINKS[1])

                def abs_b(o, u):
                    dve.wait_ge(m["ctrl_read"], o * 12 + 12)
                    wait(dve, m["state_ready"], o)
                    nc.vector.scalar_tensor_tensor(out=L[:, :, :], in0=bb[u][:, :, :], scalar=-1.0, in1=bb[u][:, :, :],
                                                   op0=ALU.mult, op1=ALU.min).then_inc(m["absb_ready"], 1)

                def mask(o, u, hid_base):
                    for q in range(PAIRS):
                        for s in range(2):
                            dve.wait_ge(m["mask_done"], o * 8 + q * 2 + s + 1)
                            if s == 0:
                                dve.wait_ge(m["hid_ready"], hid_base + q + 1)
                            mul(nc, hm[u][:, s, q, :], hp[q % 2][:, :], MB[s][:, :]).then_inc(m["masked"], 1)

                def integrate(i, it, u):
                    o = i * 4 + it * 2 + u
                    c = Chain(dve, m["order"], i * PER + it * 2 * LINKS[0] + u * LINKS[it])
                    a, gg = tt[u][:, 0, :, :], tt[u][:, 1, :, :]
                    weight = g.weight[:, :, bass.ds((i * 2 + u) * CT, CT)].unsqueeze(3).to_broadcast([P, 3, CT, P])

                    def sets(t):
                        return t.rearrange("p s (t c) -> p s t c", c=P)

                    def over_sets(t):
                        return t.unsqueeze(1).to_broadcast([P, 3, SEQ])
                    if it == 1:
                        c.mark(nc.vector.scalar_tensor_tensor(out=a, in0=a, scalar=1.0, in1=over_sets(vel[u][:, :]),
                                                              op0=ALU.add, op1=ALU.mult))
                        for s in range(3):
                            c.mark(nc.vector.scalar_tensor_tensor(out=tiles(gg[:, s, :]), in0=tiles(gg[:, s, :]), scalar=1.0,
                                                                  in1=weight[:, s, :, :], op0=ALU.add, op1=ALU.mult))
                    dve.wait_ge(m["ln_ready"], o + 1)
                    c.link(nc.vector.scalar_tensor_tensor(out=L[:, :, :], in0=bb[u][:, :, :], scalar=0.0, in1=L[:, :, :],
                                                          op0=ALU.max, op1=ALU.add))
                    dve.wait_ge(m["xm_ready"], o + 1)
                    c.link(mul(nc, L[:, :, :], L[:, :, :], over_sets(xm[u][:, :])))
                    if it == 1:
                        c.link(nc.vector.scalar_tensor_tensor(out=L[:, :, :], in0=L[:, :, :], scalar=-2.0, in1=a,
                                                              op0=ALU.mult, op1=ALU.add))
                        c.link(mul(nc, gg, gg, L[:, :, :]))
                    else:
                        c.link(mul(nc, sets(L[:, :, :]), sets(L[:, :, :]), weight))
                        c.link(nc.vector.scalar_tensor_tensor(out=gg, in0=gg, scalar=1.0, in1=L[:, :, :],
                                                              op0=ALU.add, op1=ALU.mult))
                    factor = -1.0 if it == 0 else 0.5
                    c.link(nc.vector.tensor_tensor(s2[:, :], gg[:, 0, :], gg[:, 1, :], ALU.add))
                    if it == 0:
                        nc.vector.tensor_tensor(s1[:, :], L[:, 0, :], L[:, 1, :], ALU.add)
                    c.link(nc.vector.tensor_scalar(th[u][:, :], th[u][:, :], 0.5, 0.5, ALU.mult, ALU.add))
                    nc.vector.tensor_tensor(s2[:, :], s2[:, :], gg[:, 2, :], ALU.add).then_inc(m["ref_order"], 1)
                    halt = th[u][:, :].unsqueeze(2).to_broadcast([P, CT, P])
                    if it == 0:
                        nc.vector.tensor_tensor(s1[:, :], s1[:, :], L[:, 2, :], ALU.add).then_inc(m["ref_order"], 1)
                    n_ref = (i * 12 + u * 4) if it == 0 else (i * 12 + 8 + u * 2)
                    dve.wait_ge(m["ref_order"], n_ref + (2 if it == 0 else 1))
                    mul(nc, tiles(s2[:, :]), tiles(s2[:, :]), halt).then_inc(m["ref_order"], 1)
                    if it == 0:
                        nc.vector.scalar_tensor_tensor(out=tiles(vel[u][:, :]), in0=tiles(s1[:, :]), scalar=factor,
                                                       in1=halt, op0=ALU.mult, op1=ALU.mult).then_inc(m["ref_order"], 1)
                    dve.wait_ge(m["ref_order"], n_ref + (4 if it == 0 else 2))
                    nc.vector.scalar_tensor_tensor(out=tiles(state[u][:, :]), in0=tiles(s2[:, :]), scalar=factor * DT / 2,
                                                   in1=state_in(i, u, it), op0=ALU.mult, op1=ALU.add
                                                   ).then_inc(m["state_ready"], 1)
                    assert c.n == LINKS[it], (it, c.n)

                @each_round(dve)
                def _(i):
                    for n, (it, u) in enumerate(STEPS):
                        o = i * 4 + n
                        started = not (isinstance(o, int) and o == 0)
                        if started:
                            abs_b(o - 1, 1 - u)
                        mask(o, u, step_hidden(i, n, 0)[0])
                        if started:
                            integrate(i if n else i - 1, *STEPS[n - 1])
                abs_b(ROUNDS * 4 - 1, 1)
                integrate(ROUNDS - 1, *STEPS[3])



def emit(nc, dram, cols, out):
    with ExitStack() as ctx:
        k = Core(nc, ctx, dram)
        k.x = k.sb(ctx, "x_res", [P, TILES, P])
        k.const = k.sb(ctx, "const_sb", list(dram["const"].shape))
        k.zeros = k.sb(ctx, "zeros", [P, 512], BF16)
        k.mean = k.sb(ctx, "mean", [P, TILES])
        k.rstd = k.sb(ctx, "rstd", [P, TILES])
        k.st = k.sb(ctx, "bn_stats_of_x", [P, TILES, 6])

        def const(name):
            a, b = cols[name]
            return k.const[:, a:b]

        k.c = const
        k.ident = const("ident")
        k.ident_r = k.sb(ctx, "ident_r", [P, P], F32R)
        f = lambda: None
        f.sorted_in = nc.dram_tensor("sorted_in", (PADDED * P, P), FP32, kind="Internal").ap()
        load_phase(k, f.sorted_in)
        mean, rstd = k.mean[:, :], k.rstd[:, :]
        statistics_phase(k, "ln1", mean, rstd, k.st)
        with ExitStack() as ttt:
            k.kT = k.sb(ttt, "kT", [P, TILES + 1, 2, P], F32R)
            k.ktok = k.sb(ttt, "ktok", [P, TILES, 2, P], F32R)
            k.qT = k.sb(ttt, "qT", [P, TOKENS + SEQ])
            k.vT = k.sb(ttt, "vT", [P, TOKENS])
            k.theta_gate = k.sb(ttt, "theta_gate", [P, HID])
            k.theta_val = k.sb(ttt, "theta_val", [P, HID])
            k.theta_proj = k.sb(ttt, "theta_proj", [P, HT, P])
            k.theta_projT = k.sb(ttt, "theta_projT", [P, HID])
            qkv_phase(k)
            gradient_phase(k, "grad1")
            muon_phase(k, "muon1")
            gradient_phase(k, "grad2")
            muon_phase(k, "muon2")
            k.clear_semaphores()
            query_phase(k)
        f.sorted_out = nc.dram_tensor("sorted_out", (PADDED * P, P), FP32, kind="Internal").ap()
        with ExitStack() as moe:
            f.xl = k.sb(moe, "xl", [P, TILES, P])
            f.sorted = k.sb(moe, "sorted_tokens", [P, PADDED, P])
            f.ys = k.sb(moe, "expert_outputs", [P, PADDED, P])
            f.mean, f.rstd = k.sb(moe, "sorted_mean", [P, PADDED]), k.sb(moe, "sorted_rstd", [P, PADDED])
            f.st = k.sb(moe, "bn_stats_of_sorted", [P, PADDED, 6])
            f.w1 = k.sb(moe, "w1T", [P, E, HID])
            f.w2 = k.sb(moe, "w2T", [P, E, HID])
            f.b1 = k.sb(moe, "b1_spread", [P, E, HID])
            f.b2 = k.sb(moe, "b2_spread", [P, E, P])
            f.vecT = k.sb(moe, "centroids_g_b_T", [P, 3 * E])
            f.alpha = k.sb(moe, "alpha", [P, TILES])
            f.slot_expert = k.sb(moe, "slot_expert", [P, PADDED], I32)
            f.pos = k.sb(moe, "pos", [P, TILES], U32)
            statistics_phase(k, "ln2", mean, rstd, k.st)
            affinity_phase(k, f)
            sort_phase(k, f)
            statistics_phase(k, "ln2b", f.mean[:, :], f.rstd[:, :], f.st, f.sorted)
            experts_phase(k, f)
        statistics_phase(k, "ln3", mean, rstd, k.st)
        diagonal_attention_phase(k)
        statistics_phase(k, "ln4", mean, rstd, k.st)
        k.clear_semaphores()
        g = lambda: None
        with ExitStack() as dyn:
            g.xf = k.sb(dyn, "xf", [P, TILES, P])
            g.xfT = k.sb(dyn, "xfT", [P, TOKENS])
            g.onehot = k.sb(dyn, "slot_onehot", [P, TILES, 2 * E])
            g.weight = k.sb(dyn, "control_weight", [P, 3, TILES])
            g.w1 = k.sb(dyn, "dyn_w1", [P, 2, E * EH])
            g.w1s = k.sb(dyn, "dyn_w1_shared_halt", [P, 2, P])
            g.w2 = k.sb(dyn, "dyn_w2", [P, PAIRS, CTRL])
            g.w2s = k.sb(dyn, "dyn_w2_shared_halt", [ONE + 1, CTRL + 1])
            g.b1 = k.sb(dyn, "dyn_b1", [P, PAIRS])
            g.b1s = k.sb(dyn, "dyn_b1_shared_halt", [ONE, 1])
            g.b2 = k.sb(dyn, "dyn_b2", [6 * E, 2, CTRL], BF16)
            g.sel = k.sb(dyn, "pair_rows", [2 * E, 2 * PAIRS * P], BF16)
            g.hs = [k.sb(dyn, f"shared_halt_hidden{u}", [ONE + 1, SEQ]) for u in range(2)]
            g.rw1 = k.sb(dyn, "refine_w1", [P, 2 * P])
            g.rw2 = k.sb(dyn, "refine_w2", [P, 2, P])
            g.rb1 = k.sb(dyn, "refine_b1", [P, 2])
            g.rb2 = k.sb(dyn, "refine_b2", [P, P])
            g.iw = k.sb(dyn, "integration_weight", [P, P])
            g.mu = k.sb(dyn, "mu", [P, P])
            router_phase(k, g)
            dynamics_phase(k, g, out)


def kernel(**inputs):
    import concourse.bacc as _bacc
    from concourse.bass_utils import run_bass_kernel_spmd as _run

    nc = _bacc.Bacc("TRN2", target_bir_lowering=False, num_devices=1)
    const, sel, cols = constant_columns()
    arrays = {name: np.ascontiguousarray(a) for name, a in inputs.items()}
    arrays["const"], arrays["sel"] = const, sel
    dram = {n: nc.dram_tensor(n, a.shape if a.ndim else (1,), mybir.dt.from_np(a.dtype), kind="ExternalInput").ap()
            for n, a in arrays.items()}
    arrays = {n: a.reshape(a.shape or (1,)) for n, a in arrays.items()}
    out = nc.dram_tensor("out", (SEQS, SEQ, P), FP32, kind="ExternalOutput").ap()
    emit(nc, dram, cols, out)
    r = _run(nc, [arrays], core_ids=[0])
    return r.results[0]["out"]
```
